# Optimizing a Trainium2 kernel written in Bass

```python
import numpy as np
import jax
import jax.numpy as jnp

def _softmax(x, axis=-1):
    return jax.nn.softmax(x, axis=axis)

def _gelu(x):
    return jax.nn.gelu(x, approximate=True)

def _silu(x):
    return jax.nn.silu(x)

def _sigmoid(x):
    return jax.nn.sigmoid(x)

def _layernorm(x, axis=-1, eps=1e-05):
    m = jnp.mean(x, axis=axis, keepdims=True)
    v = jnp.var(x, axis=axis, keepdims=True)
    return (x - m) / jnp.sqrt(v + eps)

def _scatter_add(tgt, idx, src, axis=0):
    return tgt.at[idx].add(src)

def _segment_sum(src, seg, n):
    return jax.ops.segment_sum(src, seg, n)
kernel_name = 'mk_gps_d2_gnn_r32_6c3144'

def setup_inputs(seed: int=0):
    np.random.seed(seed)
    _w = jnp.asarray

    def _rec_inputs():
        import jax
        import jax.numpy as jnp
        _gk = jax.random.key(seed)
        x = -0.0003713 + 1 * jax.random.normal(jax.random.fold_in(_gk, 1), (3125, 256), jnp.float32)
        src = jax.random.randint(jax.random.fold_in(_gk, 2), (50000,), 0, 3125, jnp.int32)
        dst = jnp.minimum((3125 * jax.random.uniform(jax.random.fold_in(_gk, 3), (50000,)) ** 2.0).astype(jnp.int32), 99999)
        _o = jnp.argsort(dst, stable=True)
        src = src[_o]
        dst = dst[_o]
        edge_weight = jax.random.uniform(jax.random.fold_in(_gk, 12), (50000,), jnp.float32, 0.0, 0.999998)
        return (x, src, dst, edge_weight)
    x, src, dst, edge_weight = _rec_inputs()

    def _L0_gnn_setup():
        import jax, jax.numpy as jnp
        import numpy as np
        N_NODES = 50000
        N_EDGES = 25000
        H, D_IN, D_OUT = (4, 256, 64)
        key = jax.random.key(seed)
        ks = jax.random.split(key, 7)
        x = jax.random.normal(ks[0], (N_NODES, D_IN), dtype=jnp.float32)
        idx = jax.random.randint(ks[1], (2, N_EDGES), 0, N_NODES, dtype=jnp.int32)
        elem = jax.random.uniform(ks[2], (N_EDGES,), dtype=jnp.float32)
        Ws = jax.random.normal(ks[3], (H, D_IN, D_OUT), dtype=jnp.float32) * 0.05
        bs = jax.random.normal(ks[4], (H, D_OUT), dtype=jnp.float32) * 0.05
        aw = jax.random.normal(ks[5], (H, 2 * D_OUT + 1), dtype=jnp.float32) * 0.05
        ab = jax.random.normal(ks[6], (H,), dtype=jnp.float32) * 0.05
        return {'x': x, 'idx': idx, 'elem': elem, 'Ws': Ws, 'bs': bs, 'aw': aw, 'ab': ab}
    _L0_gnn_all = _L0_gnn_setup()
    _L0_gnn_in = {k: v for k, v in _L0_gnn_all.items() if k in ('Ws', 'bs', 'aw', 'ab')}
    del _L0_gnn_all

    def _L0_mix_setup():
        import math
        import jax, jax.numpy as jnp
        import numpy as np
        EPS_DIV = 1e-07
        EPS_NORM = 1e-12

        def _l2_normalize(x, axis):
            n = jnp.sqrt(jnp.sum(x * x, axis=axis, keepdims=True))
            return x / jnp.maximum(n, EPS_NORM)
        key = jax.random.key(seed)
        ks = jax.random.split(key, 5)
        b, N, C = (8, 128, 256)
        x = jax.random.normal(ks[0], (b, N, C), dtype=jnp.float32)
        W_qkv = jax.random.normal(ks[1], (C, 3 * C), dtype=jnp.float32) * (1.0 / math.sqrt(C))
        b_qkv = jax.random.normal(ks[2], (3 * C,), dtype=jnp.float32) * 0.02
        W_out = jax.random.normal(ks[3], (C, C), dtype=jnp.float32) * (1.0 / math.sqrt(C))
        b_out = jax.random.normal(ks[4], (C,), dtype=jnp.float32) * 0.02
        return {'x': x, 'W_qkv': W_qkv, 'b_qkv': b_qkv, 'W_out': W_out, 'b_out': b_out}
    _L0_mix_all = _L0_mix_setup()
    _L0_mix_in = {k: v for k, v in _L0_mix_all.items() if k in ('W_qkv', 'b_qkv', 'W_out', 'b_out')}
    del _L0_mix_all

    def _L0_ffn_setup():
        import jax, jax.numpy as jnp
        import numpy as np
        B, S, H, F, E, K = (8, 128, 256, 512, 16, 2)
        EPS = 1e-05
        key = jax.random.key(seed)
        ks = jax.random.split(key, 9)
        sc = 0.02
        return {'x': jax.random.normal(ks[0], (B, S, H), dtype=jnp.float32), 'gate_w': jax.random.normal(ks[1], (H, E), dtype=jnp.float32) * sc, 'gate_b': jnp.zeros((E,), dtype=jnp.float32), 'w1': jax.random.normal(ks[2], (E, H, F), dtype=jnp.float32) * sc, 'b1': jnp.zeros((E, F), dtype=jnp.float32), 'w2': jax.random.normal(ks[3], (E, F, H), dtype=jnp.float32) * sc, 'b2': jnp.zeros((E, H), dtype=jnp.float32), 'gamma': jnp.ones((H,), dtype=jnp.float32), 'beta': jnp.zeros((H,), dtype=jnp.float32)}
    _L0_ffn_all = _L0_ffn_setup()
    _L0_ffn_in = {k: v for k, v in _L0_ffn_all.items() if k in ('gate_w', 'gate_b', 'w1', 'b1', 'w2', 'b2', 'gamma', 'beta')}
    del _L0_ffn_all

    def _L1_gnn_setup():
        import jax, jax.numpy as jnp
        import numpy as np
        NEG_SLOPE = 0.2
        N_NODES = 3125
        N_EDGES = 50000
        IN_CH = 256
        HEADS = 4
        OUT_CH = 64
        key = jax.random.key(seed)
        k1, k2, k3, k4, k5 = jax.random.split(key, 5)
        x = jax.random.normal(k1, (N_NODES, IN_CH), dtype=jnp.float32)
        edge_index = jax.random.randint(k2, (2, N_EDGES), 0, N_NODES, dtype=jnp.int64)
        W = jax.random.normal(k3, (IN_CH, HEADS * OUT_CH), dtype=jnp.float32) / np.sqrt(IN_CH)
        att_src = jax.random.normal(k4, (HEADS, OUT_CH), dtype=jnp.float32) / np.sqrt(OUT_CH)
        att_dst = jax.random.normal(k5, (HEADS, OUT_CH), dtype=jnp.float32) / np.sqrt(OUT_CH)
        bias = jnp.zeros((HEADS * OUT_CH,), dtype=jnp.float32)
        return {'graph_node_features': x, 'edge_index': edge_index, 'W': W, 'att_src': att_src, 'att_dst': att_dst, 'bias': bias}
    _L1_gnn_all = _L1_gnn_setup()
    _L1_gnn_in = {k: v for k, v in _L1_gnn_all.items() if k in ('W', 'att_src', 'att_dst', 'bias')}
    del _L1_gnn_all

    def _L1_mix_setup():
        import jax, jax.numpy as jnp
        import numpy as np
        EPS_NORM = 1e-06
        EPS_ATTN = 1e-06
        HEADS = 8

        def rmsnorm(x, w):
            ms = jnp.mean(x * x, axis=-1, keepdims=True)
            return w * (x * jax.lax.rsqrt(ms + EPS_NORM))

        def linear_attention(x, w_qkv, w_out, b_out):
            B, N, D = x.shape
            hd = D // HEADS
            qkv = (x @ w_qkv).reshape(B, N, 3, HEADS, hd)
            q, k, v = (qkv[:, :, 0], qkv[:, :, 1], qkv[:, :, 2])
            q = jax.nn.elu(q) + 1.0
            k = jax.nn.elu(k) + 1.0
            kv = jnp.einsum('bnhd,bnhm->bhdm', k, v)
            z = 1.0 / (jnp.einsum('bnhd,bhd->bnh', q, k.sum(axis=1)) + EPS_ATTN)
            out = jnp.einsum('bnhd,bhdm,bnh->bnhm', q, kv, z)
            out = out.reshape(B, N, D)
            return out @ w_out + b_out
        key = jax.random.key(seed)
        ks = jax.random.split(key, 4)
        B, N, D = (16, 256, 256)
        x = jax.random.normal(ks[0], (B, N, D), dtype=jnp.float32)
        w_norm1 = jnp.ones((D,), dtype=jnp.float32)
        w_qkv = jax.random.normal(ks[1], (D, 3 * D), dtype=jnp.float32) * 0.02
        w_out = jax.random.normal(ks[2], (D, D), dtype=jnp.float32) * 0.02
        b_out = jnp.zeros((D,), dtype=jnp.float32)
        w_norm2 = jnp.ones((D,), dtype=jnp.float32)
        return {'x': x, 'w_norm1': w_norm1, 'w_qkv': w_qkv, 'w_out': w_out, 'b_out': b_out, 'w_norm2': w_norm2}
    _L1_mix_all = _L1_mix_setup()
    _L1_mix_in = {k: v for k, v in _L1_mix_all.items() if k in ('w_norm1', 'w_qkv', 'w_out', 'b_out', 'w_norm2')}
    del _L1_mix_all

    def _L1_ffn_setup():
        import math
        import jax, jax.numpy as jnp
        import numpy as np
        CAPACITY_FACTOR = 1.25
        TOP_K = 2
        LN_EPS = 1e-05

        def _layer_norm(x, gamma, beta):
            mu = jnp.mean(x, axis=-1, keepdims=True)
            var = jnp.var(x, axis=-1, keepdims=True)
            return (x - mu) * jax.lax.rsqrt(var + LN_EPS) * gamma + beta
        key = jax.random.key(seed)
        ks = jax.random.split(key, 4)
        B, S, D, F, E = (8, 128, 256, 512, 8)
        x = jax.random.normal(ks[0], (B, S, D), dtype=jnp.float32)
        Wr = jax.random.normal(ks[1], (D, E), dtype=jnp.float32) / np.sqrt(D)
        br = jnp.zeros((E,), jnp.float32)
        W1 = jax.random.normal(ks[2], (E, D, F), dtype=jnp.float32) / np.sqrt(D)
        b1 = jnp.zeros((E, F), jnp.float32)
        W2 = jax.random.normal(ks[3], (E, F, D), dtype=jnp.float32) / np.sqrt(F)
        b2 = jnp.zeros((E, D), jnp.float32)
        gamma = jnp.ones((D,), jnp.float32)
        beta = jnp.zeros((D,), jnp.float32)
        return {'x': x, 'Wr': Wr, 'br': br, 'W1': W1, 'b1': b1, 'W2': W2, 'b2': b2, 'gamma': gamma, 'beta': beta}
    _L1_ffn_all = _L1_ffn_setup()
    _L1_ffn_in = {k: v for k, v in _L1_ffn_all.items() if k in ('Wr', 'br', 'W1', 'b1', 'W2', 'b2', 'gamma', 'beta')}
    del _L1_ffn_all
    return {'x': x, 'src': src, 'dst': dst, 'edge_weight': edge_weight, 'L0_gnn_Ws': _L0_gnn_in['Ws'], 'L0_gnn_bs': _L0_gnn_in['bs'], 'L0_gnn_aw': _L0_gnn_in['aw'], 'L0_gnn_ab': _L0_gnn_in['ab'], 'L0_mix_W_qkv': _L0_mix_in['W_qkv'], 'L0_mix_b_qkv': _L0_mix_in['b_qkv'], 'L0_mix_W_out': _L0_mix_in['W_out'], 'L0_mix_b_out': _L0_mix_in['b_out'], 'L0_ffn_gate_w': _L0_ffn_in['gate_w'], 'L0_ffn_gate_b': _L0_ffn_in['gate_b'], 'L0_ffn_w1': _L0_ffn_in['w1'], 'L0_ffn_b1': _L0_ffn_in['b1'], 'L0_ffn_w2': _L0_ffn_in['w2'], 'L0_ffn_b2': _L0_ffn_in['b2'], 'L0_ffn_gamma': _L0_ffn_in['gamma'], 'L0_ffn_beta': _L0_ffn_in['beta'], 'L1_gnn_W': _L1_gnn_in['W'], 'L1_gnn_att_src': _L1_gnn_in['att_src'], 'L1_gnn_att_dst': _L1_gnn_in['att_dst'], 'L1_gnn_bias': _L1_gnn_in['bias'], 'L1_mix_w_norm1': _L1_mix_in['w_norm1'], 'L1_mix_w_qkv': _L1_mix_in['w_qkv'], 'L1_mix_w_out': _L1_mix_in['w_out'], 'L1_mix_b_out': _L1_mix_in['b_out'], 'L1_mix_w_norm2': _L1_mix_in['w_norm2'], 'L1_ffn_Wr': _L1_ffn_in['Wr'], 'L1_ffn_br': _L1_ffn_in['br'], 'L1_ffn_W1': _L1_ffn_in['W1'], 'L1_ffn_b1': _L1_ffn_in['b1'], 'L1_ffn_W2': _L1_ffn_in['W2'], 'L1_ffn_b2': _L1_ffn_in['b2'], 'L1_ffn_gamma': _L1_ffn_in['gamma'], 'L1_ffn_beta': _L1_ffn_in['beta']}

def reference(x, src, dst, edge_weight, L0_gnn_Ws, L0_gnn_bs, L0_gnn_aw, L0_gnn_ab, L0_mix_W_qkv, L0_mix_b_qkv, L0_mix_W_out, L0_mix_b_out, L0_ffn_gate_w, L0_ffn_gate_b, L0_ffn_w1, L0_ffn_b1, L0_ffn_w2, L0_ffn_b2, L0_ffn_gamma, L0_ffn_beta, L1_gnn_W, L1_gnn_att_src, L1_gnn_att_dst, L1_gnn_bias, L1_mix_w_norm1, L1_mix_w_qkv, L1_mix_w_out, L1_mix_b_out, L1_mix_w_norm2, L1_ffn_Wr, L1_ffn_br, L1_ffn_W1, L1_ffn_b1, L1_ffn_W2, L1_ffn_b2, L1_ffn_gamma, L1_ffn_beta):
    import jax
    import jax.numpy as jnp

    def _L0_gnn_ref(x, idx, elem, Ws, bs, aw, ab):
        import jax, jax.numpy as jnp
        import numpy as np
        N_NODES = 50000
        N_EDGES = 25000
        H, D_IN, D_OUT = (4, 256, 64)
        N = x.shape[0]
        O = Ws.shape[-1]
        feats = jnp.einsum('nd,hdo->hno', x, Ws) + bs[:, None, :]
        aw_src, aw_dst, aw_e = (aw[:, :O], aw[:, O:2 * O], aw[:, 2 * O])
        a_s = jnp.einsum('hno,ho->hn', feats, aw_src)
        a_d = jnp.einsum('hno,ho->hn', feats, aw_dst)
        src, dst = (idx[0], idx[1])
        score = a_s[:, src] + a_d[:, dst] + aw_e[:, None] * elem[None, :] + ab[:, None]
        w = jnp.exp(-jax.nn.relu(score / 20.0))
        dst_f = feats[:, dst]
        seg = lambda vals: jax.ops.segment_sum(vals, src, num_segments=N)
        pooled = jax.vmap(lambda wi, fi: seg(wi[:, None] * fi))(w, dst_f)
        row_sum = jax.vmap(lambda wi: seg(wi))(w)
        out = pooled / row_sum[:, :, None]
        return jnp.transpose(out, (1, 0, 2)).reshape(N, H * O)

    def _L0_mix_ref(x, W_qkv, b_qkv, W_out, b_out):
        import math
        import jax, jax.numpy as jnp
        import numpy as np
        EPS_DIV = 1e-07
        EPS_NORM = 1e-12

        def _l2_normalize(x, axis):
            n = jnp.sqrt(jnp.sum(x * x, axis=axis, keepdims=True))
            return x / jnp.maximum(n, EPS_NORM)
        b, N, C = x.shape
        qkv = x @ W_qkv + b_qkv
        q, k, v = jnp.split(qkv, 3, axis=2)
        q = q - jnp.mean(q, axis=2, keepdims=True)
        k = k - jnp.mean(k, axis=2, keepdims=True)
        q2 = q * q
        k2 = k * k
        q2s = jnp.sum(q2, axis=2, keepdims=True)
        k2s = jnp.sum(k2, axis=2, keepdims=True)
        k2 = _l2_normalize(k2 / (k2s + EPS_DIV), axis=-2)
        q2 = _l2_normalize(q2 / (q2s + EPS_DIV), axis=-1)
        kv = jnp.einsum('bnc,bnd->bcd', k2, v)
        t2 = jnp.einsum('bnc,bcd->bnd', q2, kv) / math.sqrt(N)
        attn = v + t2
        return attn @ W_out + b_out

    def _L0_ffn_ref(x, gate_w, gate_b, w1, b1, w2, b2, gamma, beta):
        import jax, jax.numpy as jnp
        import numpy as np
        B, S, H, F, E, K = (8, 128, 256, 512, 16, 2)
        EPS = 1e-05
        gate_logits = x @ gate_w + gate_b
        topk_vals, topk_idx = jax.lax.top_k(gate_logits, K)
        topk_w = jax.nn.softmax(topk_vals, axis=-1)
        h = jax.nn.relu(jnp.einsum('bsh,ehf->bsef', x, w1) + b1)
        expert_out = jnp.einsum('bsef,efh->bseh', h, w2) + b2
        sel = jnp.take_along_axis(expert_out, topk_idx[:, :, :, None], axis=2)
        moe = jnp.sum(topk_w[..., None] * sel, axis=2)
        y = x + moe
        mu = jnp.mean(y, axis=-1, keepdims=True)
        var = jnp.var(y, axis=-1, keepdims=True)
        return (y - mu) / jnp.sqrt(var + EPS) * gamma + beta

    def _L1_gnn_ref(graph_node_features, edge_index, W, att_src, att_dst, bias):
        import jax, jax.numpy as jnp
        import numpy as np
        NEG_SLOPE = 0.2
        N_NODES = 3125
        N_EDGES = 50000
        IN_CH = 256
        HEADS = 4
        OUT_CH = 64
        x = graph_node_features
        N = x.shape[0]
        H, C = att_src.shape
        x_lin = (x @ W).reshape(N, H, C)
        a_src = jnp.einsum('nhc,hc->nh', x_lin, att_src)
        a_dst = jnp.einsum('nhc,hc->nh', x_lin, att_dst)
        loop = jnp.arange(N, dtype=edge_index.dtype)
        src = jnp.concatenate([edge_index[0], loop])
        dst = jnp.concatenate([edge_index[1], loop])
        alpha = jax.nn.leaky_relu(a_src[src] + a_dst[dst], NEG_SLOPE)
        amax = jax.ops.segment_max(alpha, dst, num_segments=N)
        amax = jnp.where(jnp.isfinite(amax), amax, 0.0)
        ex = jnp.exp(alpha - amax[dst])
        denom = jax.ops.segment_sum(ex, dst, num_segments=N)
        alpha_n = ex / (denom[dst] + 1e-16)
        msg = x_lin[src] * alpha_n[:, :, None]
        out = jax.ops.segment_sum(msg, dst, num_segments=N)
        return out.reshape(N, H * C) + bias

    def _L1_mix_ref(x, w_norm1, w_qkv, w_out, b_out, w_norm2):
        import jax, jax.numpy as jnp
        import numpy as np
        EPS_NORM = 1e-06
        EPS_ATTN = 1e-06
        HEADS = 8

        def rmsnorm(x, w):
            ms = jnp.mean(x * x, axis=-1, keepdims=True)
            return w * (x * jax.lax.rsqrt(ms + EPS_NORM))

        def linear_attention(x, w_qkv, w_out, b_out):
            B, N, D = x.shape
            hd = D // HEADS
            qkv = (x @ w_qkv).reshape(B, N, 3, HEADS, hd)
            q, k, v = (qkv[:, :, 0], qkv[:, :, 1], qkv[:, :, 2])
            q = jax.nn.elu(q) + 1.0
            k = jax.nn.elu(k) + 1.0
            kv = jnp.einsum('bnhd,bnhm->bhdm', k, v)
            z = 1.0 / (jnp.einsum('bnhd,bhd->bnh', q, k.sum(axis=1)) + EPS_ATTN)
            out = jnp.einsum('bnhd,bhdm,bnh->bnhm', q, kv, z)
            out = out.reshape(B, N, D)
            return out @ w_out + b_out
        h = x + linear_attention(rmsnorm(x, w_norm1), w_qkv, w_out, b_out)
        return h + rmsnorm(h, w_norm2)

    def _L1_ffn_ref(x, Wr, br, W1, b1, W2, b2, gamma, beta):
        import math
        import jax, jax.numpy as jnp
        import numpy as np
        CAPACITY_FACTOR = 1.25
        TOP_K = 2
        LN_EPS = 1e-05

        def _layer_norm(x, gamma, beta):
            mu = jnp.mean(x, axis=-1, keepdims=True)
            var = jnp.var(x, axis=-1, keepdims=True)
            return (x - mu) * jax.lax.rsqrt(var + LN_EPS) * gamma + beta
        B, S, D = x.shape
        E = Wr.shape[1]
        N = B * S
        K = TOP_K
        logits = jnp.mean(x, axis=1) @ Wr + br
        routing_weights = jax.nn.softmax(logits, axis=-1)
        capacity = float(math.ceil(N * CAPACITY_FACTOR / E))
        expected_loads = routing_weights.sum(axis=0) * (N / B)
        scale = jnp.where(expected_loads > capacity, capacity / expected_loads, 1.0)
        routing_weights = jax.nn.softmax(routing_weights * scale, axis=-1)
        rw_tok = jnp.broadcast_to(routing_weights[:, None, :], (B, S, E)).reshape(N, E)
        top_w, top_i = jax.lax.top_k(rw_tok, K)
        top_w = jax.nn.softmax(top_w, axis=-1)
        xf = x.reshape(N, D)
        h = jax.nn.gelu(jnp.einsum('nd,edf->enf', xf, W1) + b1[:, None, :], approximate=False)
        y = jnp.einsum('enf,efd->end', h, W2) + b2[:, None, :]
        w_dense = jnp.zeros((N, E), x.dtype).at[jnp.arange(N)[:, None], top_i].add(top_w)
        out = jnp.einsum('ne,end->nd', w_dense, y).reshape(B, S, D)
        out = _layer_norm(out + x, gamma, beta)
        return out
    edge_index = jnp.stack([src, dst])
    xn = _layernorm(x, axis=-1)
    x = x + _L0_gnn_ref(xn, edge_index, edge_weight, L0_gnn_Ws, L0_gnn_bs, L0_gnn_aw, L0_gnn_ab) + _L0_mix_ref(xn[None], L0_mix_W_qkv, L0_mix_b_qkv, L0_mix_W_out, L0_mix_b_out)[0]
    x = x + _L0_ffn_ref(_layernorm(x, axis=-1)[None], L0_ffn_gate_w, L0_ffn_gate_b, L0_ffn_w1, L0_ffn_b1, L0_ffn_w2, L0_ffn_b2, L0_ffn_gamma, L0_ffn_beta)[0]
    xn = _layernorm(x, axis=-1)
    x = x + _L1_gnn_ref(xn, edge_index, L1_gnn_W, L1_gnn_att_src, L1_gnn_att_dst, L1_gnn_bias) + _L1_mix_ref(xn[None], L1_mix_w_norm1, L1_mix_w_qkv, L1_mix_w_out, L1_mix_b_out, L1_mix_w_norm2)[0]
    x = x + _L1_ffn_ref(_layernorm(x, axis=-1)[None], L1_ffn_Wr, L1_ffn_br, L1_ffn_W1, L1_ffn_b1, L1_ffn_W2, L1_ffn_b2, L1_ffn_gamma, L1_ffn_beta)[0]
    return x

_drawn_inputs = setup_inputs


def setup_inputs(seed=0):
    import zlib

    import numpy as np

    out = dict(_drawn_inputs(seed))
    spreads = {'L0_ffn_gate_b': (0.0, 0.278),
     'L0_ffn_b1': (0.0, 0.8),
     'L0_ffn_b2': (0.0, 0.1),
     'L0_ffn_gamma': (1.0, 0.2),
     'L0_ffn_beta': (0.0, 0.1),
     'L1_gnn_bias': (0.0, 0.357),
     'L1_mix_w_norm1': (1.0, 0.6),
     'L1_mix_b_out': (0.0, 0.1),
     'L1_mix_w_norm2': (1.0, 0.2),
     'L1_ffn_br': (0.0, 0.8),
     'L1_ffn_b1': (0.0, 0.8),
     'L1_ffn_b2': (0.0, 0.714),
     'L1_ffn_gamma': (1.0, 0.2),
     'L1_ffn_beta': (0.0, 0.453)}
    factors = {'edge_weight': 64.0,
     'L0_gnn_aw': 24.946,
     'L0_gnn_ab': 64.0,
     'L0_mix_b_out': 3.944,
     'L1_gnn_att_dst': 3.414,
     'L1_mix_w_qkv': 8.0,
     'L1_mix_w_out': 8.0}
    for name, (base, spread) in spreads.items():
        noise = np.random.default_rng([zlib.crc32(name.encode()), seed]).standard_normal(out[name].shape)
        drawn = base * np.exp(spread * noise) if base else spread * noise
        out[name] = jnp.asarray(drawn.astype(out[name].dtype))
    for name, factor in factors.items():
        out[name] = (out[name] * factor).astype(out[name].dtype)
    return out
```

```python
from contextlib import ExitStack

import concourse.bass as bass
from concourse import mybir

F32 = mybir.dt.float32
I32 = mybir.dt.int32
U32 = mybir.dt.uint32
BF16 = mybir.dt.bfloat16
ALU = mybir.AluOpType
ACT = mybir.ActivationFunctionType
AX = mybir.AxisListType.X

P = 128
NN = 3125
NP = 125
TN = 25
D = 256
DC = D // P
H = 4
HD = D // H
NE = 50000
EC = NE // NP
ROW = D + H
G0_SIZE = 2 * P
G0_BINS = TN
G0_N = (NE + G0_BINS * (G0_SIZE - 1)) // G0_SIZE
G0_N += -G0_N % 8
G0_TILES = 2 * G0_N
B1 = 32
G1_BINS = -(-NN // B1)
G1_N = (NE + G1_BINS * (P - 1)) // P
G1_N += -G1_N % 8
TB = 5
NB = TN // TB
R1 = 4
assert R1 * TN >= G1_BINS
E0 = 16
F0 = 512
TOPK = 2
X_N = (NN * TOPK + E0 * (P - 1)) // P
X_N += -X_N % 4
E1 = 8
MAGIC = 12582912.0
LN_EPS = 1e-5


class Order:

    def __init__(self, eng, sem):
        self.eng, self.sem, self.n, self.off = eng, sem, 0, None

    def done(self, ins):
        ins.then_inc(self.sem, 1)
        self.n += 1
        return ins

    def value(self):
        return self.n if self.off is None else self.off + self.n

    def settle(self):
        self.eng.wait_ge(self.sem, self.value())

    def settle_alone(self):
        wait_alone(self.eng, self.sem, self.value())

    def enter(self, i, per):
        self.start, self.per, self.off = self.n, per, i * per

    def leave(self, count):
        assert self.n - self.start == self.per, (self.n - self.start, self.per)
        self.n, self.off = self.start + self.per * count, None


def wait_alone(eng, sem, value):
    eng.wait_ge(sem, value)
    eng.nop(nofuse=True)


def spread(ap, *shape):
    return ap.to_broadcast(list(shape))


def rank_count(o, bins, cnt, junk, iota, nbins):
    with o.eng.Fori(0, nbins) as b:
        o.enter(b, 1)
        rank_count_bin(o, bins, cnt, junk, iota, b)
        o.leave(nbins)


def rank_count_bin(o, bins, cnt, junk, iota, b):
    o.settle_alone()
    o.done(o.eng.tensor_scalar(junk, bins, iota[0:NP, bass.ds(b, 1)], 0.0, ALU.is_equal, ALU.add,
                               accum_out=cnt[:, bass.ds(b, 1)]))


def rank_bases(o, first, total, prefix, groups, start, one, size, nbins):
    o.done(o.eng.tensor_scalar(groups, total, (size - 1) / 2.0, 1.0 / size, ALU.add, ALU.mult))
    o.settle()
    o.done(o.eng.tensor_scalar(groups, groups, MAGIC, MAGIC, ALU.add, ALU.subtract))
    o.settle()
    o.done(o.eng.tensor_tensor_scan(start, one[0:NP, 0:nbins], groups, 0.0, ALU.mult, ALU.add))
    o.settle()
    o.done(o.eng.tensor_tensor(start, start, groups, ALU.subtract))
    o.settle()
    o.done(o.eng.tensor_scalar(first, start, float(size), -1.0, ALU.mult, ALU.add))
    o.settle()
    o.done(o.eng.tensor_tensor(first, first, prefix, ALU.add))
    o.settle()


def rank_slots(o, slot, bins, first, mask, running, one, iota, nbins):
    with o.eng.Fori(0, nbins) as b:
        o.enter(b, 3)
        rank_slots_bin(o, slot, bins, first, mask, running, one, iota, b)
        o.leave(nbins)
    o.settle()


def rank_slots_bin(o, slot, bins, first, mask, running, one, iota, b):
    o.settle_alone()
    o.done(o.eng.tensor_scalar(mask, bins, iota[0:NP, bass.ds(b, 1)], None, ALU.is_equal))
    o.settle_alone()
    o.done(o.eng.tensor_tensor_scan(running, one[0:NP, 0:mask.shape[1]], mask, first[:, bass.ds(b, 1)],
                                    ALU.mult, ALU.add))
    o.settle_alone()
    o.done(o.eng.copy_predicated(slot, mask, running))


def group_bins(o, bin_of, tmp, start, iota_groups, nbins, ngroups):
    o.done(o.eng.memset(bin_of, -1.0))
    o.settle()
    with o.eng.Fori(0, nbins) as b:
        o.enter(b, 1)
        o.settle()
        o.done(o.eng.scalar_tensor_tensor(bin_of, iota_groups, start[0:1, bass.ds(b, 1)], bin_of,
                                          ALU.is_ge, ALU.add))
        o.leave(nbins)
    o.settle()


def split_index(o, whole, rest, key, size):
    o.done(o.eng.tensor_scalar(whole, key, -(size - 1) / 2.0, 1.0 / size, ALU.add, ALU.mult))
    o.settle()
    o.done(o.eng.tensor_scalar(whole, whole, MAGIC, MAGIC, ALU.add, ALU.subtract))
    o.settle()
    o.done(o.eng.scalar_tensor_tensor(rest, whole, -float(size), key, ALU.mult, ALU.add))
    o.settle()


def sorted_rows(o, row, tile, lane, slot, tiles):
    split_index(o, tile, lane, slot, P)
    o.done(o.eng.scalar_tensor_tensor(row, lane, float(tiles), tile, ALU.mult, ALU.add))
    o.settle()


def layer_norm_stats(o, x, st, mean, rstd, tmp):
    with o.eng.Fori(0, TN) as t:
        o.enter(t, 1)
        o.done(o.eng.bn_stats(st[:, bass.ds(t, 1), :], x[:, bass.ds(t, 1), :].rearrange("p a d -> p (a d)")))
        o.leave(TN)
    o.settle()
    o.done(o.eng.tensor_tensor(mean, st[:, :, 1], st[:, :, 4], ALU.add))
    o.done(o.eng.tensor_tensor(tmp, st[:, :, 1], st[:, :, 4], ALU.subtract))
    o.done(o.eng.tensor_tensor(rstd, st[:, :, 2], st[:, :, 5], ALU.add))
    o.settle()
    o.done(o.eng.tensor_scalar(mean, mean, 0.5, None, ALU.mult))
    o.done(o.eng.tensor_tensor(tmp, tmp, tmp, ALU.mult))
    o.done(o.eng.tensor_scalar(rstd, rstd, 1.0 / D, None, ALU.mult))
    o.settle()
    o.done(o.eng.scalar_tensor_tensor(rstd, tmp, 0.25, rstd, ALU.mult, ALU.add))
    o.settle()


def load_weight(eng, dst, src, sem):
    eng.dma_start(dst, src.rearrange("(c p) n -> p c n", p=P)).then_inc(sem, 16)


def tile_places(ps):
    return [ps[:, j // 2, j % 2 * DC * NP:(j % 2 + 1) * DC * NP].rearrange("p (c n) -> p c n", c=DC) for j in range(TB)]


def keep_transposed(act, sem, xT, ps):
    flat = xT.rearrange("p t c n -> p (t c n)")
    act.activation(flat[:, 0:4 * DC * NP].rearrange("p (b n) -> p b n", b=2), ps[:, 0:2, 0:2 * DC * NP], ACT.Copy)
    act.activation(flat[:, 4 * DC * NP:], ps[:, 2, 0:DC * NP], ACT.Copy).then_inc(sem, 1)


class Memory:

    def __init__(self, nc, ctx, stage):
        self.nc, self.ctx, self.stage, self.sems = nc, ctx, stage, []
        ctx.callback(self.release_semaphores)

    def release_semaphores(self):
        self.nc.clear_and_free_semaphores(self.sems)
        self.nc.all_engine_barrier(sem_only=True)

    def sb(self, name, shape, dt=F32):
        return self.ctx.enter_context(self.nc.sbuf_tensor(f"{self.stage}_{name}", shape, dt))

    def ps(self, name, shape, dt=F32):
        bank = self.ctx.enter_context(self.nc.psum_tensor(f"{self.stage}_{name}", [P, 512], dt))
        size = 1
        for n in shape[1:]:
            size *= n
        flat = bank[0:shape[0], 0:size]
        return flat if len(shape) == 2 else flat.rearrange("p (a b) -> p a b", a=shape[1])

    def banks(self, name, n, dt=F32):
        return self.ctx.enter_context(self.nc.psum_tensor(f"{self.stage}_{name}", [P, n, 512], dt))

    def sem(self, name):
        self.sems.append(self.nc.alloc_semaphore(f"{self.stage}_{name}"))
        return self.sems[-1]


def stage_project0(nc, a, k):
    with ExitStack() as ctx:
        m = Memory(nc, ctx, "p0")
        src = m.sb("src", [NP, EC], I32)
        dst = m.sb("dst", [NP, EC], I32)
        wgt = m.sb("wgt", [NP, EC])
        key = m.sb("key", [NP, EC])
        whole = m.sb("whole", [NP, EC])
        rest = m.sb("rest", [NP, EC])
        slot = m.sb("slot", [NP, EC])
        mask = m.sb("mask", [NP, EC], I32)
        running = m.sb("running", [NP, EC])
        ones = m.sb("ones", [NP, EC])
        iota_g = m.sb("iota_g", [1, G1_N])
        bin1f = m.sb("bin1f", [1, G1_N])
        bin_of1 = m.sb("bin_of1", [NP, EC])
        record0 = m.sb("record0", [NP, EC, 4])
        row0 = m.sb("row0", [NP, EC], I32)
        cnt = m.sb("cnt", [NP, P])
        prefix = m.sb("prefix", [NP, P])
        total = m.sb("total", [NP, P])
        groups = m.sb("groups", [NP, P])
        start = m.sb("start", [NP, P])
        first = m.sb("first", [NP, P])
        pad = m.sb("pad", [P, 4 * G0_TILES])
        pad1 = m.sb("pad1", [P, 2 * G1_N])
        zrow = m.sb("zrow", [P, D])
        stage_row = m.sb("stage_row", [NP, 2, 8], I32)
        stage_rec = m.sb("stage_rec", [NP, 2, 8, 4])
        st = m.sb("st", [NP, TN, 6])
        mean = m.sb("mean", [NP, TN])
        rstd = m.sb("rstd", [NP, TN])
        tmp = m.sb("tmp", [NP, TN])
        w = m.sb("w", [P, DC, 4 * D])
        wa = m.sb("wa", [P, DC, 2, H])
        wprod = m.sb("wprod", [P, D])
        awb = m.sb("awb", [P, H, 2 * HD + 1])
        bias = m.sb("bias", [NP, 4 * D])
        biasa = m.sb("biasa", [NP, 2, H])
        wout = m.sb("wout", [P, DC, D])
        bout = m.sb("bout", [NP, D])
        xn = m.sb("xn", [NP, D])
        xT = m.sb("xT", [P, DC, NP])
        qk = m.sb("qk", [NP, 2, D])
        qkc = m.sb("qkc", [NP, 2, D])
        sums = m.sb("sums", [NP, 2])
        ksum = m.sb("ksum", [NP, 1])
        k2 = m.sb("k2", [NP, D])
        k4 = m.sb("k4", [NP, D])
        q4 = m.sb("q4", [NP, D])
        qsum = m.sb("qsum", [NP, TN])
        q4sum = m.sb("q4sum", [NP, TN])
        q2 = m.sb("q2", [NP, TN, D])
        v = m.sb("v", [NP, TN, D])
        feat = m.sb("feat", [NP, ROW])
        kv = m.sb("kv", [P, DC, D])
        kvT = m.sb("kvT", [P, DC, D])
        kw = m.sb("kw", [P, DC, D])
        cnorm = m.sb("cnorm", [P, DC])
        qv = m.sb("qv", [NP, 2, D])
        qvT = m.sb("qvT", [P, 4, NP])
        part = m.sb("part", [NP, D])

        ps_rank = m.ps("ps_rank", [P, 2, P])
        ps_T = m.ps("ps_T", [P, 4, P])
        ps_qk = m.ps("ps_qk", [P, 2 * D])
        ps_vf = m.ps("ps_vf", [P, 2 * D])
        ps_a = m.ps("ps_a", [P, 2, H])
        ps_kv = m.ps("ps_kv", [P, DC, D])
        ps_cn = m.ps("ps_cn", [P, DC, 2])
        ps_mix = m.ps("ps_mix", [P, 2, D])

        s_const = m.sem("const")
        s_x = m.sem("x")
        s_edges = m.sem("edges")
        s_w = m.sem("weights")
        s_pad = m.sem("pad_tile")
        s_fill = m.sem("filled")
        s_cnt = m.sem("counted")
        s_base = m.sem("bases")
        s_rows = m.sem("rows_known")
        s_stage = m.sem("staged")
        s_scat = [m.sem(f"scattered{i}") for i in range(2)]
        s_var = m.sem("variance")
        s_std = m.sem("std")
        s_xn = m.sem("normed")
        s_xT = m.sem("xT_made")
        s_xTs = m.sem("xT_kept")
        s_proj = m.sem("projected")
        s_evac = m.sem("projections_kept")
        s_sum = m.sem("qk_summed")
        s_cen = m.sem("negative_means")
        s_sq = m.sem("squared")
        s_k2 = m.sem("k2_ready")
        s_k4 = m.sem("k4_ready")
        s_kv = m.sem("kv_added")
        s_feat = m.sem("feature_row")
        s_tab = m.sem("table_written")
        s_kvd = m.sem("kv_done")
        s_kvs = m.sem("kv_kept")
        s_cn = m.sem("column_norms")
        s_kvT = m.sem("kvT_made")
        s_kvTs = m.sem("kvT_kept")
        s_kw = m.sem("kw_made")
        s_kws = m.sem("kw_kept")
        s_qn = m.sem("q_norm_square")
        s_qr = m.sem("q_norm")
        s_qv = m.sem("qv_staged")
        s_qvT = m.sem("qvT_made")
        s_qvTs = m.sem("qvT_kept")
        s_mix = m.sem("mixed")
        s_mixd = m.sem("mix_kept")
        s_v = m.sem("vector_steps")
        s_a = m.sem("scalar_steps")
        block = ctx.enter_context(nc.Block())

        @block.sync
        def _(sp):
            for t, s in ((src, a["src"]), (dst, a["dst"]), (wgt, a["edge_weight"])):
                sp.dma_start(t[:], s.rearrange("(p c) -> p c", p=NP)).then_inc(s_edges, 16)
            sp.dma_start(k["x"][:], a["x"].rearrange("(p t) d -> p t d", p=NP)).then_inc(s_x, 16)
            load_weight(sp, w[:, :, 0:3 * D], a["L0_mix_W_qkv"], s_w)
            for h in range(H):
                load_weight(sp, w[:, :, 3 * D + h * HD:3 * D + (h + 1) * HD], a["L0_gnn_Ws"][h], s_w)
            load_weight(sp, wout[:], a["L0_mix_W_out"], s_w)
            sp.dma_start(bias[:, 0:3 * D], a["L0_mix_b_qkv"].partition_broadcast(NP)).then_inc(s_w, 16)
            sp.dma_start(bias[:, 3 * D:], a["L0_gnn_bs"].rearrange("h o -> (h o)").partition_broadcast(NP)).then_inc(s_w, 16)
            sp.dma_start(bout[:], a["L0_mix_b_out"].partition_broadcast(NP)).then_inc(s_w, 16)
            sp.dma_start(awb[:].rearrange("p h o -> p (h o)"),
                         a["L0_gnn_aw"].rearrange("h o -> (h o)").partition_broadcast(P)).then_inc(s_w, 16)
            sp.wait_ge(s_pad, 3)
            sp.dma_start(k["sorted0"].rearrange("(p t) f -> p (t f)", p=P), pad[:]).then_inc(s_fill, 16)
            sp.dma_start(k["expert_in"].rearrange("(t p) d -> p t d", p=P),
                         spread(zrow[:].unsqueeze(1), P, X_N, D)).then_inc(s_fill, 16)
            sp.dma_start(k["sorted1"].rearrange("(p t) f -> p (t f)", p=P), pad1[:]).then_inc(s_fill, 16)
            with sp.Fori(0, TN) as t:
                sp.wait_ge(s_feat, t + 1)
                sp.dma_start(k["table"].rearrange("(p t) d -> p t d", p=NP)[:, bass.ds(t, 1), :],
                             feat[:].unsqueeze(1)).then_inc(s_tab, 16)
            sp.wait_ge(s_tab, 16 * TN)
            sp.wait_ge(s_fill, 48)

        @block.gpsimd
        def _(pool):
            nc.gpsimd.iota(k["iota"][:], [[1, P]], base=0, channel_multiplier=0,
                           allow_small_or_imprecise_dtypes=True).then_inc(s_const, 1)
            nc.gpsimd.iota(iota_g[:], [[1, G1_N]], base=0, channel_multiplier=0,
                           allow_small_or_imprecise_dtypes=True).then_inc(s_const, 1)
            nc.gpsimd.memset(k["ident"][:], 0.0).then_inc(s_const, 1)
            nc.gpsimd.memset(k["before"][:], 1.0).then_inc(s_const, 1)
            nc.gpsimd.memset(k["one"][:], 1.0).then_inc(s_const, 1)
            pool.wait_ge(s_const, 5)
            nc.gpsimd.affine_select(out=k["ident"][:], in_=k["ident"][:], compare_op=ALU.not_equal, fill=1.0, base=0,
                                    pattern=[[-1, P]], channel_multiplier=1).then_inc(s_const, 1)
            nc.gpsimd.affine_select(out=k["before"][:], in_=k["before"][:], compare_op=ALU.is_ge, fill=0.0, base=-1,
                                    pattern=[[1, P]], channel_multiplier=-1).then_inc(s_const, 1)
            nc.gpsimd.memset(zrow[:], 0.0).then_inc(s_pad, 1)
            pool.wait_ge(s_rows, 1)
            pool.wait_ge(s_fill, 48)

            def scatter(half, i, staged):
                at = i * 16 + half * 8
                nc.gpsimd.tensor_copy(stage_row[:, half, :], row0[:, bass.ds(at, 8)]).then_inc(s_stage, 1)
                nc.gpsimd.tensor_copy(stage_rec[:, half], record0[:, bass.ds(at, 8), :]).then_inc(s_stage, 1)
                wait_alone(pool, s_stage, staged + 2 * half + 2)
                for j in range(8):
                    pool.indirect_dma_start(
                        out=k["sorted0"], out_offset=bass.IndirectOffsetOnAxis(
                            ap=stage_row[:, half, j:j + 1].bitcast(U32), axis=0),
                        in_=stage_rec[:, half, j, :], in_offset=None).then_inc(s_scat[half], 16)

            for half in range(2):
                scatter(half, 0, 0)
            with pool.Fori(1, EC // 16) as i:
                for half in range(2):
                    wait_alone(pool, s_scat[half], i * 128)
                    scatter(half, i, i * 4)
            for half in range(2):
                pool.wait_ge(s_scat[half], 128 * (EC // 16))

        @block.scalar
        def _(act):
            o = Order(act, s_a)
            act.wait_ge(s_var, 1)
            nc.scalar.activation(rstd[:], rstd[:], ACT.Sqrt, bias=k["eps5"][0:NP, :]).then_inc(s_std, 1)
            with act.Fori(0, TN) as t:
                wait_alone(act, s_xT, t + 1)
                nc.scalar.activation(xT[:], ps_T[:, 0:DC, 0:NP], ACT.Copy).then_inc(s_xTs, 1)
                o.enter(t, 3)
                wait_alone(act, s_evac, t + 1)
                for j in range(2):
                    nc.scalar.activation(qkc[:, j, :], qk[:, j, :], ACT.Copy, accum_out=sums[:, j:j + 1]).then_inc(s_sum, 1)
                wait_alone(act, s_cen, t + 1)
                o.done(nc.scalar.activation(q2[:, bass.ds(t, 1), :].rearrange("p a d -> p (a d)"), qk[:, 0, :], ACT.Square,
                                            bias=sums[:, 0:1], accum_out=qsum[:, bass.ds(t, 1)]))
                o.done(nc.scalar.activation(k2[:], qk[:, 1, :], ACT.Square, bias=sums[:, 1:2], accum_out=ksum[:]))
                o.settle_alone()
                o.done(nc.scalar.activation(q4[:], q2[:, bass.ds(t, 1), :].rearrange("p a d -> p (a d)"), ACT.Square,
                                            accum_out=q4sum[:, bass.ds(t, 1)]))
                o.settle_alone()
                act.sem_inc(s_sq, 1)
                wait_alone(act, s_k2, t + 1)
                nc.scalar.activation(k4[:], k2[:], ACT.Square).then_inc(s_k4, 1)
                o.leave(TN)
            act.wait_ge(s_kvd, 1)
            nc.scalar.activation(cnorm[:], ps_cn[:, :, 0], ACT.Sqrt).then_inc(s_cn, 1)
            act.wait_ge(s_qn, 1)
            nc.scalar.activation(q4sum[:], q4sum[:], ACT.Sqrt).then_inc(s_qr, 1)
            act.wait_ge(s_kvT, 1)
            nc.scalar.activation(kvT[:].rearrange("p a d -> p (a d)"), ps_T[:].rearrange("p a d -> p (a d)"), ACT.Copy).then_inc(s_kvTs, 1)
            act.wait_ge(s_kw, 1)
            nc.scalar.activation(kw[:], ps_mix[:], ACT.Copy).then_inc(s_kws, 1)
            with act.Fori(0, TN) as t:
                wait_alone(act, s_mix, t + 1)
                nc.scalar.activation(qv[:, 0, :], q2[:, bass.ds(t, 1), :].rearrange("p a d -> p (a d)"), ACT.Copy).then_inc(s_qv, 1)
                nc.scalar.activation(qv[:, 1, :], v[:, bass.ds(t, 1), :].rearrange("p a d -> p (a d)"), ACT.Copy).then_inc(s_qv, 1)
                wait_alone(act, s_qvT, t + 1)
                nc.scalar.activation(qvT[:], ps_T[:, :, 0:NP], ACT.Copy).then_inc(s_qvTs, 1)

        @block.vector
        def _(dve):
            o = Order(dve, s_v)
            o.done(nc.vector.memset(pad[:], 0.0))
            o.done(nc.vector.memset(pad1[:], float(NN)))
            o.settle()
            for tile, fields in ((pad, 4), (pad1, 2)):
                nc.vector.memset(tile[:].rearrange("p (t f) -> p t f", f=fields)[:, :, 1:2], -1.0).then_inc(s_pad, 1)
            o.done(nc.vector.memset(k["eps5"][:], LN_EPS))
            o.done(nc.vector.memset(ones[:], 1.0))
            dve.wait_ge(s_edges, 48)
            dve.wait_ge(s_const, 7)
            o.done(nc.vector.tensor_copy(key[:], src[:]))
            o.done(nc.vector.memset(record0[:], 0.0))
            o.settle()
            split_index(o, whole[:], rest[:], key[:], TN)
            o.done(nc.vector.tensor_copy(record0[:, :, 0], dst[:]))
            o.done(nc.vector.tensor_copy(record0[:, :, 1], whole[:]))
            o.done(nc.vector.tensor_copy(record0[:, :, 2], wgt[:]))
            rank_count(o, rest[:], cnt, running[:], k["iota"], G0_BINS)
            o.settle()
            dve.sem_inc(s_cnt, 1)
            dve.wait_ge(s_base, 1)
            o.done(nc.vector.tensor_copy(prefix[:, 0:G0_BINS], ps_rank[0:NP, 0, 0:G0_BINS]))
            o.done(nc.vector.tensor_copy(total[:, 0:G0_BINS], ps_rank[0:NP, 1, 0:G0_BINS]))
            o.settle()
            rank_bases(o, first[:, 0:G0_BINS], total[:, 0:G0_BINS], prefix[:, 0:G0_BINS], groups[:, 0:G0_BINS],
                       start[:, 0:G0_BINS], k["one"], G0_SIZE, G0_BINS)
            rank_slots(o, slot[:], rest[:], first, mask[:], running[:], ones, k["iota"], G0_BINS)
            sorted_rows(o, running[:], whole[:], rest[:], slot[:], G0_TILES)
            o.done(nc.vector.tensor_copy(row0[:], running[:]))
            o.settle()
            group_bins(o, running[0:1, 0:G0_N + 8], None, start, iota_g[0:1, 0:G0_N + 8], G0_BINS, G0_N)
            nc.vector.tensor_copy(k["bin0"][:], running[0:1, 0:G0_N + 8]).then_inc(s_rows, 1)

            o.done(nc.vector.tensor_copy(key[:], dst[:]))
            o.done(nc.vector.memset(k["record1"][:], 0.0))
            o.done(nc.vector.memset(cnt[:], 0.0))
            o.settle()
            split_index(o, rest[:], bin_of1[:], key[:], G1_BINS)
            o.done(nc.vector.tensor_copy(k["record1"][:, :, 0], src[:]))
            o.done(nc.vector.tensor_copy(k["record1"][:, :, 1], rest[:]))
            dve.wait_ge(s_x, 16)
            layer_norm_stats(o, k["x"], st, mean[:], rstd[:], tmp[:])
            dve.sem_inc(s_var, 1)
            dve.wait_ge(s_std, 1)
            o.done(nc.vector.reciprocal(rstd[:], rstd[:]))
            dve.wait_ge(s_w, 16 * 10)
            for c in range(DC):
                for j in range(2):
                    o.settle()
                    o.done(nc.vector.tensor_tensor(wprod[:].rearrange("p (h o) -> p h o", h=H),
                                                   w[:, c, 3 * D:].rearrange("p (h o) -> p h o", h=H),
                                                   awb[:, :, j * HD:(j + 1) * HD], ALU.mult))
                    o.settle()
                    o.done(nc.vector.tensor_reduce(wa[:, c, j, :], wprod[:].rearrange("p (h o) -> p h o", h=H),
                                                   AX, ALU.add))
            for j in range(2):
                o.settle()
                o.done(nc.vector.tensor_tensor(wprod[0:NP].rearrange("p (h o) -> p h o", h=H),
                                               bias[:, 3 * D:].rearrange("p (h o) -> p h o", h=H),
                                               awb[0:NP, :, j * HD:(j + 1) * HD], ALU.mult))
                o.settle()
                o.done(nc.vector.tensor_reduce(biasa[:, j, :], wprod[0:NP].rearrange("p (h o) -> p h o", h=H),
                                               AX, ALU.add))
            o.settle()

            def norm(t):
                nc.vector.tensor_scalar(xn[:], k["x"][:, bass.ds(t, 1), :].rearrange("p a d -> p (a d)"), mean[:, bass.ds(t, 1)],
                                        rstd[:, bass.ds(t, 1)], ALU.subtract, ALU.mult).then_inc(s_xn, 1)

            with dve.Fori(0, TN) as t:
                norm(t)
                o.enter(t, 6 + R1)
                wait_alone(dve, s_proj, t + 1)
                o.done(nc.vector.tensor_tensor(qk[:].rearrange("p a d -> p (a d)"), ps_qk[0:NP, :], bias[:, 0:2 * D], ALU.add))
                o.settle_alone()
                dve.sem_inc(s_evac, 1)
                o.done(nc.vector.tensor_tensor(v[:, bass.ds(t, 1), :].rearrange("p a d -> p (a d)"), ps_vf[0:NP, 0:D], bias[:, 2 * D:3 * D], ALU.add))
                o.done(nc.vector.tensor_tensor(k["a_src"][:, bass.ds(t, 1), :].rearrange("p a h -> p (a h)"), ps_a[0:NP, 0, :],
                                               biasa[:, 0, :], ALU.add))
                o.done(nc.vector.tensor_tensor(feat[:, D:], ps_a[0:NP, 1, :], biasa[:, 1, :], ALU.add))
                o.settle()
                nc.vector.tensor_tensor(feat[:, 0:D], ps_vf[0:NP, D:], bias[:, 3 * D:], ALU.add).then_inc(s_feat, 1)
                wait_alone(dve, s_sum, t * 2 + 2)
                nc.vector.tensor_scalar(sums[:], sums[:], -1.0 / D, None, ALU.mult).then_inc(s_cen, 1)
                wait_alone(dve, s_sq, t + 1)
                o.done(nc.vector.tensor_scalar(ksum[:], ksum[:], 1e-7, None, ALU.add))
                o.settle()
                o.done(nc.vector.reciprocal(ksum[:], ksum[:]))
                o.settle()
                nc.vector.tensor_scalar(k2[:], k2[:], ksum[:], None, ALU.mult).then_inc(s_k2, 1)
                for j in range(R1):
                    rank_count_bin(o, bin_of1[:], cnt, running[:], k["iota"], t * R1 + j)
                wait_alone(dve, s_kv, t + 1)
                wait_alone(dve, s_tab, t * 16 + 16)
                o.leave(TN)
            o.settle()
            dve.sem_inc(s_cnt, 1)
            dve.wait_ge(s_base, 2)
            o.done(nc.vector.tensor_copy(prefix[:], ps_rank[0:NP, 0, :]))
            o.done(nc.vector.tensor_copy(total[:], ps_rank[0:NP, 1, :]))
            o.settle()
            rank_bases(o, first[:], total[:], prefix[:], groups[:], start[:], k["one"], P, P)
            dve.wait_ge(s_cn, 1)
            o.done(nc.vector.tensor_scalar(cnorm[:], cnorm[:], 1e-12, None, ALU.max))
            o.settle()
            o.done(nc.vector.reciprocal(cnorm[:], cnorm[:]))
            o.settle()
            for c in range(DC):
                nc.vector.tensor_scalar(kv[:, c, :], ps_kv[:, c, :], cnorm[:, c:c + 1], float(NN) ** -0.5,
                                        ALU.mult, ALU.mult).then_inc(s_kvs, 1)
            o.done(nc.vector.tensor_scalar(qsum[:], qsum[:], 1e-7, None, ALU.add))
            o.settle()
            o.done(nc.vector.reciprocal(qsum[:], qsum[:]))
            o.settle()
            o.done(nc.vector.tensor_tensor(tmp[:], qsum[:], qsum[:], ALU.mult))
            o.settle()
            nc.vector.tensor_tensor(q4sum[:], q4sum[:], tmp[:], ALU.mult).then_inc(s_qn, 1)
            dve.wait_ge(s_qr, 1)
            o.done(nc.vector.tensor_scalar(q4sum[:], q4sum[:], 1e-12, None, ALU.max))
            o.settle()
            o.done(nc.vector.reciprocal(q4sum[:], q4sum[:]))
            o.settle()
            o.done(nc.vector.tensor_tensor(qsum[:], qsum[:], q4sum[:], ALU.mult))
            o.settle()
            dve.sem_inc(s_mixd, 1)
            with dve.Fori(0, TN) as t:
                o.enter(t, 2 + 3 * R1)
                xt = k["x"][:, bass.ds(t, 1), :].rearrange("p a d -> p (a d)")
                wait_alone(dve, s_mix, t + 2)
                o.done(nc.vector.tensor_tensor(part[:], ps_mix[0:NP, 1, :], bout[:], ALU.add))
                o.settle()
                o.done(nc.vector.scalar_tensor_tensor(part[:], ps_mix[0:NP, 0, :], qsum[:, bass.ds(t, 1)], part[:], ALU.mult, ALU.add))
                o.settle()
                nc.vector.tensor_tensor(xt, xt, part[:], ALU.add).then_inc(s_mixd, 1)
                for j in range(R1):
                    rank_slots_bin(o, slot[:], bin_of1[:], first, mask[:], running[:], ones, k["iota"], t * R1 + j)
                o.leave(TN)
            o.settle()
            sorted_rows(o, running[:], whole[:], rest[:], slot[:], G1_N)
            o.done(nc.vector.tensor_copy(k["row1"][:], running[:]))
            o.settle()
            group_bins(o, bin1f[:], None, start, iota_g[0:1, :], G1_BINS, G1_N)
            o.done(nc.vector.tensor_copy(k["bin1"][:], bin1f[:]))

        @block.tensor
        def _(pe):
            mm = nc.tensor.matmul
            pe.wait_ge(s_const, 7)
            pe.wait_ge(s_cnt, 1)
            mm(ps_rank[0:NP, 0, 0:G0_BINS], k["before"][0:NP, 0:NP], cnt[:, 0:G0_BINS], start=True, stop=True)
            mm(ps_rank[0:NP, 1, 0:G0_BINS], k["one"][0:NP, 0:NP], cnt[:, 0:G0_BINS], start=True, stop=True).then_inc(s_base, 1)
            pe.wait_ge(s_pad, 3)
            pe.wait_ge(s_w, 16 * 10)
            mm(ps_kv[:].rearrange("p a d -> p (a d)"), zrow[:, 0:P], w[:, 0, 0:2 * D], start=True, stop=False, skip_group_check=True)
            mm(ps_cn[:].rearrange("p a d -> p (a d)"), zrow[:, 0:P], w[:, 0, 0:2 * DC], start=True, stop=False, skip_group_check=True)
            with pe.Fori(0, TN) as t:
                wait_alone(pe, s_xn, t + 1)
                for c in range(DC):
                    last = nc.tensor.transpose(ps_T[:, c, 0:NP], xn[:, c * P:(c + 1) * P], k["ident"][0:NP, 0:NP])
                last.then_inc(s_xT, 1)
                wait_alone(pe, s_xTs, t + 1)
                for c in range(DC):
                    first_c, last_c = c == 0, c == DC - 1
                    mm(ps_qk[0:NP, :], xT[:, c, :], w[:, c, 0:2 * D], start=first_c, stop=last_c)
                for c in range(DC):
                    first_c, last_c = c == 0, c == DC - 1
                    mm(ps_vf[0:NP, :], xT[:, c, :], w[:, c, 2 * D:], start=first_c, stop=last_c)
                for c in range(DC):
                    first_c, last_c = c == 0, c == DC - 1
                    last = mm(ps_a[0:NP].rearrange("p j h -> p (j h)"), xT[:, c, :], wa[:, c].rearrange("p j h -> p (j h)"),
                              start=first_c, stop=last_c)
                last.then_inc(s_proj, 1)
                wait_alone(pe, s_k4, t + 1)
                for c in range(DC):
                    mm(ps_kv[:, c, :], k2[:, c * P:(c + 1) * P], v[:, bass.ds(t, 1), :].rearrange("p a d -> p (a d)"), start=False, stop=False,
                       skip_group_check=True)
                for c in range(DC):
                    last = mm(ps_cn[:, c, :], k4[:, c * P:(c + 1) * P], k["one"][0:NP, 0:2], start=False, stop=False,
                              skip_group_check=True)
                last.then_inc(s_kv, 1)
            mm(ps_kv[:].rearrange("p a d -> p (a d)"), zrow[:, 0:P], w[:, 0, 0:2 * D], start=False, stop=True, skip_group_check=True)
            mm(ps_cn[:].rearrange("p a d -> p (a d)"), zrow[:, 0:P], w[:, 0, 0:2 * DC], start=False, stop=True,
               skip_group_check=True).then_inc(s_kvd, 1)
            pe.wait_ge(s_cnt, 2)
            mm(ps_rank[0:NP, 0, :], k["before"][0:NP, 0:NP], cnt[:], start=True, stop=True)
            mm(ps_rank[0:NP, 1, :], k["one"][0:NP, 0:NP], cnt[:], start=True, stop=True).then_inc(s_base, 1)
            pe.wait_ge(s_kvs, 2)
            pT = ps_T[:].rearrange("p a d -> p (a d)").rearrange("p (b e) -> p b e", b=DC)
            for c in range(DC):
                for b in range(DC):
                    last = nc.tensor.transpose(pT[:, b, c * P:(c + 1) * P], kv[:, c, b * P:(b + 1) * P], k["ident"][:])
            last.then_inc(s_kvT, 1)
            pe.wait_ge(s_kvTs, 1)
            for c in range(DC):
                for b in range(DC):
                    last = mm(ps_mix[:, c, :], kvT[:, b, c * P:(c + 1) * P], wout[:, b, :], start=b == 0, stop=b == DC - 1)
            last.then_inc(s_kw, 1)
            pe.wait_ge(s_kws, 1)
            pe.sem_inc(s_mix, 1)
            with pe.Fori(0, TN) as t:
                wait_alone(pe, s_qv, t * 2 + 2)
                for j in range(2):
                    for c in range(DC):
                        last = nc.tensor.transpose(ps_T[:, j * DC + c, 0:NP], qv[:, j, c * P:(c + 1) * P], k["ident"][0:NP, 0:NP])
                last.then_inc(s_qvT, 1)
                wait_alone(pe, s_qvTs, t + 1)
                wait_alone(pe, s_mixd, t + 1)
                for j in range(2):
                    for c in range(DC):
                        last = mm(ps_mix[0:NP, j, :], qvT[:, j * DC + c, :], (kw if j == 0 else wout)[:, c, :], start=c == 0,
                                  stop=c == DC - 1)
                last.then_inc(s_mix, 1)


def stage_edges0(nc, a, k):
    with ExitStack() as ctx:
        m = Memory(nc, ctx, "e0")
        RING = 8
        AHEAD = 3
        rec = m.sb("rec", [P, G0_TILES + 2 * AHEAD, 4])
        awb = m.sb("awb", [P, H, 2 * HD + 1])
        abb = m.sb("abb", [P, H])
        const = m.sb("const", [P, G0_TILES, H])
        index = m.sb("index", [P, 2, RING], I32)
        rows = m.sb("rows", [P, 2 * RING, ROW])
        hot = m.sb("hot", [P, 2 * RING, NP])
        hotT = m.sb("hotT", [NP, 2, 2, P])
        score = m.sb("score", [P, 2, 2, H])
        acc = k["acc0"]

        ps_T = [m.ps(f"ps_T{i}", [P, 2, P]) for i in range(2)]
        ps_E = [m.ps(f"ps_E{i}", [P, 4, H]) for i in range(2)]
        ps_A = [m.ps(f"ps_A{i}", [P, ROW]) for i in range(4)]

        s_in = m.sem("in")
        s_w1 = m.sem("expert_weights")
        s_const = m.sem("const_ready")
        s_idx = m.sem("index_staged")
        s_rows = [m.sem(f"rows{i}") for i in range(RING)]
        s_hot = m.sem("one_hot")
        s_T = m.sem("one_hot_T")
        s_Tk = m.sem("one_hot_T_kept")
        s_E = m.sem("source_scores")
        s_sc = m.sem("scores")
        s_w = m.sem("weights")
        s_wm = m.sem("weighted_rows")
        s_agg = m.sem("added_up")
        s_acc = m.sem("accumulated")
        s_v = m.sem("vector_steps")
        block = ctx.enter_context(nc.Block())

        @block.sync
        def _(sp):
            sp.dma_start(rec[:, 0:G0_TILES, :].rearrange("p t f -> p (t f)"),
                         k["sorted0"].rearrange("(p t) f -> p (t f)", p=P)).then_inc(s_in, 16)
            sp.dma_start(awb[:].rearrange("p h o -> p (h o)"),
                         a["L0_gnn_aw"].rearrange("h o -> (h o)").partition_broadcast(P)).then_inc(s_in, 16)
            sp.dma_start(abb[:], a["L0_gnn_ab"].partition_broadcast(P)).then_inc(s_in, 16)
            for e in range(E0):
                load_weight(sp, k["w1"][:, e], a["L0_ffn_w1"][e], s_w1)
            sp.wait_ge(s_w1, 16 * E0)

        @block.gpsimd
        def _(pool):
            def gather(i, half, staged):
                nc.gpsimd.tensor_copy(index[:, half, :], rec[:, bass.ds(i * 2 * RING + half * RING, RING), 0:1]
                                      .rearrange("p a b -> p (a b)")).then_inc(s_idx, 1)
                wait_alone(pool, s_idx, staged)
                for j in range(RING):
                    tile = half * RING + j
                    pool.indirect_dma_start(
                        out=rows[:, tile, :], out_offset=None, in_=k["table"],
                        in_offset=bass.IndirectOffsetOnAxis(ap=index[:, half, j:j + 1].bitcast(U32), axis=0)
                    ).then_inc(s_rows[tile // 2], 16)

            pool.wait_ge(s_in, 48)
            for half in range(2):
                gather(0, half, half + 1)
            with pool.Fori(1, G0_N // RING) as i:
                for half in range(2):
                    wait_alone(pool, s_agg, (i - 1) * RING + (half + 1) * RING // 2)
                    gather(i, half, i * 2 + half + 1)

        def turns(eng, step, tail=()):
            for q in range(RING):
                step(q, q, 0)
            with eng.Fori(1, G0_N // RING) as i:
                for q in range(RING):
                    step(i * RING + q, q, i)
            for s in tail:
                step(G0_N + s, s, None)

        @block.vector
        def _(dve):
            o = Order(dve, s_v)

            def one_hot(s, q):
                for j in range(2):
                    last = nc.vector.tensor_scalar(hot[:, q * 2 + j, :], k["iota"][:, 0:NP],
                                                   rec[:, bass.ds(s * 2 + j, 1), 1:2].rearrange("p a b -> p (a b)"), None, ALU.is_equal)
                last.then_inc(s_hot, 1)

            def scores(s, q, i):
                sc = score[:, q % 2]
                dve.wait_ge(s_E, s + 1)
                o.done(nc.vector.tensor_tensor(sc, ps_E[q % 2][:, q // 2 % 2 * 2:q // 2 % 2 * 2 + 2, :],
                                               const[:, bass.ds(s * 2, 2), :], ALU.add))
                dve.wait_ge(s_rows[q], i * 32 + 32)
                o.settle()
                o.done(nc.vector.tensor_tensor(sc, sc, rows[:, q * 2:q * 2 + 2, D:], ALU.add))
                o.settle()
                nc.vector.tensor_scalar(sc, sc, 0.0, -1.0 / 20.0, ALU.max, ALU.mult).then_inc(s_sc, 1)

            def weigh(s, q):
                r = rows[:, q * 2:q * 2 + 2, 0:D].rearrange("p a (h c) -> p a h c", h=H)
                w = rows[:, q * 2:q * 2 + 2, D:].unsqueeze(3)
                dve.wait_ge(s_w, s + 1)
                nc.vector.tensor_tensor(r, r, spread(w, P, 2, H, HD), ALU.mult).then_inc(s_wm, 1)

            def accumulate(s, q):
                block_of = dve.value_load(k["bin0"][0:1, bass.ds(s, 1)], min_val=0, max_val=G0_BINS - 1)
                at = acc[:, bass.ds(block_of, 1), :].rearrange("p a d -> p (a d)")
                if isinstance(s, int) and s == 0:
                    pass
                else:
                    dve.wait_ge(s_acc, s)
                dve.wait_ge(s_agg, s + 1)
                nc.vector.tensor_tensor(at, at, ps_A[q % 4][0:NP, :], ALU.add).then_inc(s_acc, 1)

            nc.vector.memset(acc[:], 0.0).then_inc(s_const, 1)
            nc.vector.memset(rec[:, G0_TILES:, :], -1.0).then_inc(s_const, 1)
            dve.wait_ge(s_in, 48)
            for h in range(H):
                nc.vector.tensor_scalar(const[:, :, h], rec[:, 0:G0_TILES, 2], awb[:, h, 2 * HD:], abb[:, h:h + 1],
                                        ALU.mult, ALU.add).then_inc(s_const, 1)
            dve.wait_ge(s_const, 2 + H)
            for s in range(AHEAD):
                one_hot(s, s)

            def step(s, q, i):
                first, over = i is not None and isinstance(i, int), i is None
                if first:
                    o.n = 2 * s
                elif not over and q == 0:
                    o.enter(i - 1, 2 * RING)
                if not (first and s < 1 or over and q > 0):
                    weigh(s - 1, (q - 1) % RING)
                if not over:
                    scores(s, q, i)
                    one_hot(s + AHEAD, (q + AHEAD) % RING)
                if not (first and s < 3):
                    accumulate(s - 3, (q - 3) % RING)
                if not first and not over and q == RING - 1:
                    o.leave(G0_N // RING - 1)

            turns(dve, step, range(3))

        @block.scalar
        def _(act):
            def evacuate(s, q):
                act.wait_ge(s_T, s + 1)
                nc.scalar.activation(hotT[:, q % 2], ps_T[q % 2][0:NP], ACT.Copy).then_inc(s_Tk, 1)

            def step(s, q, i):
                act.wait_ge(s_sc, s + 1)
                nc.scalar.activation(rows[:, q * 2:q * 2 + 2, D:], score[:, q % 2], ACT.Exp).then_inc(s_w, 1)
                evacuate(s + 2, q)

            for s in range(2):
                evacuate(s, s)
            turns(act, step)

        @block.tensor
        def _(pe):
            def transpose(s, q):
                pe.wait_ge(s_hot, s + 1)
                for j in range(2):
                    last = nc.tensor.transpose(ps_T[q % 2][0:NP, j, :], hot[:, q * 2 + j, :], k["ident"][:])
                last.then_inc(s_T, 1)

            def source_scores(s, q):
                block_of = pe.value_load(k["bin0"][0:1, bass.ds(s, 1)], min_val=0, max_val=G0_BINS - 1)
                pe.wait_ge(s_Tk, s + 1)
                for j in range(2):
                    last = nc.tensor.matmul(ps_E[q % 2][:, q // 2 % 2 * 2 + j, :], hotT[:, q % 2, j, :],
                                            k["a_src"][:, bass.ds(block_of, 1), :].rearrange("p a h -> p (a h)"),
                                            start=True, stop=True)
                last.then_inc(s_E, 1)

            def add_up(s, q):
                pe.wait_ge(s_wm, s + 1)
                for j in range(2):
                    last = nc.tensor.matmul(ps_A[q % 4][0:NP, :], hot[:, q * 2 + j, :], rows[:, q * 2 + j, :],
                                            start=j == 0, stop=j == 1)
                last.then_inc(s_agg, 1)

            def step(s, q, i):
                if i is not None:
                    source_scores(s + 1, (q + 1) % RING)
                    transpose(s + AHEAD, (q + AHEAD) % RING)
                if not (isinstance(i, int) and s < 1):
                    add_up(s - 1, (q - 1) % RING)

            for s in range(2):
                transpose(s, s)
            source_scores(0, 0)
            transpose(2, 2)
            turns(pe, step, range(1))


def stage_gate(nc, a, k):
    with ExitStack() as ctx:
        m = Memory(nc, ctx, "g")
        st = m.sb("st", [NP, TN, 6])
        mean = m.sb("mean", [NP, TN])
        rstd = m.sb("rstd", [NP, TN])
        tmp = m.sb("tmp", [NP, TN])
        xn = m.sb("xn", [NP, TB, D])
        xT = m.sb("xT", [P, TB, DC, NP])
        gw = m.sb("gw", [P, DC, E0])
        gb = m.sb("gb", [NP, E0])
        b1r = m.sb("b1r", [E0 * F0 // P, P])
        logit = m.sb("logit", [NP, TN, E0])
        pick = m.sb("pick", [NP, TN, E0])
        best = m.sb("best", [NP, TOPK, TN])
        which = m.sb("which", [NP, TOPK, TN])
        cnt = m.sb("cnt", [NP, E0])
        prefix = m.sb("prefix", [NP, E0])
        total = m.sb("total", [NP, E0])
        groups = m.sb("groups", [NP, E0])
        start = m.sb("start", [NP, E0])
        first = m.sb("first", [NP, E0])
        slot = m.sb("slot", [NP, TOPK * TN])
        mask = m.sb("mask", [NP, TOPK * TN], I32)
        running = m.sb("running", [NP, TOPK * TN])
        expert = m.sb("expert", [1, X_N + 2])
        ps_T = m.banks("ps_T", 3)
        ps_L = m.ps("ps_L", [P, TB, E0])
        ps_rank = m.ps("ps_rank", [P, 2, E0])
        ps_b = m.ps("ps_b", [P, P])

        s_w = m.sem("weights")
        s_var = m.sem("variance")
        s_std = m.sem("std")
        s_xn = m.sem("normed")
        s_xT = m.sem("xT_made")
        s_xTk = m.sem("xT_kept")
        s_L = m.sem("logits")
        s_b = m.sem("b1_turned")
        s_d = m.sem("difference")
        s_e = m.sem("exponential")
        s_cnt = m.sem("counted")
        s_base = m.sem("bases")
        s_v = m.sem("vector_steps")
        block = ctx.enter_context(nc.Block())

        @block.sync
        def _(sp):
            load_weight(sp, gw[:], a["L0_ffn_gate_w"], s_w)
            sp.dma_start(gb[:], a["L0_ffn_gate_b"].partition_broadcast(NP)).then_inc(s_w, 16)
            sp.dma_start(b1r[:], a["L0_ffn_b1"].rearrange("e (c p) -> (e c) p", p=P)).then_inc(s_w, 16)

        @block.scalar
        def _(act):
            act.wait_ge(s_b, 1)
            nc.scalar.activation(k["b1T"][:], ps_b[:, 0:E0 * F0 // P], ACT.Copy)
            act.wait_ge(s_var, 1)
            nc.scalar.activation(rstd[:], rstd[:], ACT.Sqrt, bias=k["eps5"][0:NP, :]).then_inc(s_std, 1)
            with act.Fori(0, NB) as u:
                wait_alone(act, s_xT, u + 1)
                keep_transposed(nc.scalar, s_xTk, xT[:], ps_T)
            act.wait_ge(s_d, 1)
            nc.scalar.activation(tmp[:], tmp[:], ACT.Exp).then_inc(s_e, 1)

        @block.vector
        def _(dve):
            o = Order(dve, s_v)
            v = nc.vector
            w = k["acc0"][:, :, D:]
            rows = k["normed"]
            o.done(v.reciprocal(w, w))
            o.settle()
            heads = rows.rearrange("p t (h c) -> p t h c", h=H)
            o.done(v.tensor_tensor(heads, heads, spread(w.unsqueeze(3), NP, TN, H, HD), ALU.mult))
            o.settle()
            o.done(v.tensor_tensor(k["x"][:], k["x"][:], rows, ALU.add))
            o.settle()
            layer_norm_stats(o, k["x"], st, mean[:], rstd[:], tmp[:])
            dve.sem_inc(s_var, 1)
            dve.wait_ge(s_std, 1)
            o.done(v.reciprocal(rstd[:], rstd[:]))
            o.settle()
            dve.wait_ge(s_w, 16 * 3)
            with dve.Fori(0, NB) as u:
                for j in range(TB):
                    t = u * TB + j
                    for out in (rows[:, bass.ds(t, 1), :].rearrange("p a d -> p (a d)"), xn[:, j, :]):
                        last = v.tensor_scalar(out, k["x"][:, bass.ds(t, 1), :].rearrange("p a d -> p (a d)"),
                                               mean[:, bass.ds(t, 1)], rstd[:, bass.ds(t, 1)], ALU.subtract, ALU.mult)
                last.then_inc(s_xn, 1)
                o.enter(u, 1)
                wait_alone(dve, s_L, u + 1)
                o.done(v.tensor_tensor(logit[:, bass.ds(u * TB, TB), :], ps_L[0:NP], spread(gb[:].unsqueeze(1), NP, TB, E0), ALU.add))
                o.leave(NB)
            o.settle()
            iota = spread(k["iota"][0:NP, 0:E0].unsqueeze(1), NP, TN, E0)
            for r in range(TOPK):
                o.done(v.tensor_reduce(best[:, r, :], logit[:], AX, ALU.max))
                o.settle()
                o.done(v.tensor_tensor(pick[:], logit[:], spread(best[:, r, :].unsqueeze(2), NP, TN, E0), ALU.is_equal))
                o.settle()
                o.done(v.scalar_tensor_tensor(pick[:], pick[:], -float(E0), iota, ALU.mult, ALU.add))
                o.settle()
                o.done(v.tensor_reduce(which[:, r, :], pick[:], AX, ALU.min))
                o.settle()
                o.done(v.tensor_scalar(which[:, r, :], which[:, r, :], float(E0), None, ALU.add))
                o.settle()
                if r + 1 < TOPK:
                    o.done(v.tensor_tensor(pick[:], iota, spread(which[:, r, :].unsqueeze(2), NP, TN, E0), ALU.is_equal))
                    o.settle()
                    o.done(v.scalar_tensor_tensor(logit[:], pick[:], -1e30, logit[:], ALU.mult, ALU.add))
                    o.settle()
            v.tensor_tensor(tmp[:], best[:, 1, :], best[:, 0, :], ALU.subtract).then_inc(s_d, 1)
            flat = which[:].rearrange("p r t -> p (r t)")
            rank_count(o, flat, cnt, running[:], k["iota"], E0)
            o.settle()
            dve.sem_inc(s_cnt, 1)
            dve.wait_ge(s_e, 1)
            o.done(v.tensor_scalar(k["gate"][:, 0, :], tmp[:], 1.0, None, ALU.add))
            o.settle()
            o.done(v.reciprocal(k["gate"][:, 0, :], k["gate"][:, 0, :]))
            o.settle()
            o.done(v.tensor_tensor(k["gate"][:, 1, :], tmp[:], k["gate"][:, 0, :], ALU.mult))
            dve.wait_ge(s_base, 1)
            o.done(v.tensor_copy(prefix[:], ps_rank[0:NP, 0, :]))
            o.done(v.tensor_copy(total[:], ps_rank[0:NP, 1, :]))
            o.settle()
            rank_bases(o, first[:], total[:], prefix[:], groups[:], start[:], k["one"], P, E0)
            rank_slots(o, slot[:], flat, first, mask[:], running[:], k["one"], k["iota"], E0)
            o.done(v.tensor_copy(k["pairs"][:], slot[:]))
            group_bins(o, expert[:], None, start, k["iota"][0:1, 0:X_N + 2], E0, X_N)
            o.done(v.tensor_copy(k["expert_of"][:], expert[:]))

        @block.tensor
        def _(pe):
            pe.wait_ge(s_w, 16 * 3)
            nc.tensor.transpose(ps_b[:, 0:E0 * F0 // P], b1r[:], k["ident"][0:E0 * F0 // P, 0:E0 * F0 // P]).then_inc(s_b, 1)
            with pe.Fori(0, NB) as u:
                wait_alone(pe, s_xn, u + 1)
                for j, place in enumerate(tile_places(ps_T)):
                    for c in range(DC):
                        last = nc.tensor.transpose(place[:, c, :], xn[:, j, c * P:(c + 1) * P], k["ident"][0:NP, 0:NP])
                last.then_inc(s_xT, 1)
                wait_alone(pe, s_xTk, u + 1)
                for j in range(TB):
                    for c in range(DC):
                        last = nc.tensor.matmul(ps_L[0:NP, j, :], xT[:, j, c, :], gw[:, c, :], start=c == 0, stop=c == DC - 1)
                last.then_inc(s_L, 1)
            pe.wait_ge(s_cnt, 1)
            nc.tensor.matmul(ps_rank[0:NP, 0, :], k["before"][0:NP, 0:NP], cnt[:], start=True, stop=True)
            nc.tensor.matmul(ps_rank[0:NP, 1, :], k["one"][0:NP, 0:NP], cnt[:], start=True, stop=True).then_inc(s_base, 1)


def stage_experts(nc, a, k):
    with ExitStack() as ctx:
        m = Memory(nc, ctx, "x")
        FC = F0 // P
        w2 = m.sb("w2", [P, E0, FC, D])
        RING = 4
        xs = m.sb("xs", [P, RING, D])
        xT = m.sb("xT", [P, 2, DC, P])
        hidden = m.sb("hidden", [P, F0])
        hT = m.sb("hT", [P, FC, P])
        b2 = m.sb("b2", [P, RING, D])
        y = m.sb("y", [P, 2, D])
        stage_row = m.sb("stage_row", [NP, 2, 8], I32)
        stage_rec = m.sb("stage_rec", [NP, 2, 8, 2])
        ps_x = [m.ps(f"ps_x{i}", [P, DC, P]) for i in range(2)]
        ps_h = [m.ps(f"ps_h{i}", [P, F0]) for i in range(2)]
        ps_hT = [m.ps(f"ps_hT{i}", [P, FC, P]) for i in range(2)]
        ps_y = [m.ps(f"ps_y{i}", [P, D]) for i in range(2)]

        s_w2 = m.sem("second_weights")
        s_sent = m.sem("rows_sent")
        s_xs = [m.sem(f"tile_in{i}") for i in range(RING)]
        s_xT = m.sem("xT_made")
        s_xTk = m.sem("xT_kept")
        s_h = m.sem("hidden_made")
        s_hk = m.sem("hidden_kept")
        s_hT = m.sem("hidden_T_made")
        s_hTk = m.sem("hidden_T_kept")
        s_y = m.sem("y_made")
        s_yk = m.sem("y_kept")
        s_out = [m.sem(f"tile_out{i}") for i in range(2)]
        s_stage = m.sem("staged")
        s_scat = [m.sem(f"scattered{i}") for i in range(2)]
        block = ctx.enter_context(nc.Block())

        def turns(eng, step):
            for q in range(RING):
                step(q, q, 0)
            with eng.Fori(1, X_N // RING - 1) as i:
                for q in range(RING):
                    step(i * RING + q, q, i)
            for q in range(RING):
                step(X_N - RING + q, q, X_N // RING - 1)

        def before(s, last):
            return not isinstance(s, int) or s < last

        def after(s, first):
            return not isinstance(s, int) or s >= first

        def expert(eng, s):
            return eng.value_load(k["expert_of"][0:1, bass.ds(s, 1)], min_val=0, max_val=E0 - 1)

        @block.gpsimd
        def _(pool):
            for r in range(TOPK):
                for t in range(TN):
                    pool.indirect_dma_start(
                        out=k["expert_in"], out_offset=bass.IndirectOffsetOnAxis(
                            ap=k["pairs"][:, r * TN + t:r * TN + t + 1].bitcast(U32), axis=0),
                        in_=k["normed"][:, t, :], in_offset=None).then_inc(s_sent, 16)

            def scatter(half, i, staged):
                at = i * 16 + half * 8
                nc.gpsimd.tensor_copy(stage_row[:, half, :], k["row1"][:, bass.ds(at, 8)]).then_inc(s_stage, 1)
                nc.gpsimd.tensor_copy(stage_rec[:, half], k["record1"][:, bass.ds(at, 8), :]).then_inc(s_stage, 1)
                wait_alone(pool, s_stage, staged + 2 * half + 2)
                for j in range(8):
                    pool.indirect_dma_start(
                        out=k["sorted1"], out_offset=bass.IndirectOffsetOnAxis(
                            ap=stage_row[:, half, j:j + 1].bitcast(U32), axis=0),
                        in_=stage_rec[:, half, j, :], in_offset=None).then_inc(s_scat[half], 16)

            for half in range(2):
                scatter(half, 0, 0)
            with pool.Fori(1, EC // 16) as i:
                for half in range(2):
                    wait_alone(pool, s_scat[half], i * 128)
                    scatter(half, i, i * 4)
            for half in range(2):
                pool.wait_ge(s_scat[half], 128 * (EC // 16))

        @block.sync
        def _(sp):
            for e in range(E0):
                load_weight(sp, w2[:, e], a["L0_ffn_w2"][e], s_w2)
            sp.wait_ge(s_sent, 16 * TOPK * TN)

            tile_in = k["expert_in"].rearrange("(t p) d -> p t d", p=P)
            tile_out = k["expert_out"].rearrange("(t p) d -> p t d", p=P)

            def store(s, q):
                wait_alone(sp, s_yk, s + 1)
                sp.dma_start(tile_out[:, bass.ds(s, 1), :].rearrange("p a d -> p (a d)"), y[:, q % 2, :]).then_inc(s_out[q % 2], 16)

            def step(s, q, i):
                if after(s, RING):
                    store(s - RING, q)
                e = expert(sp, s)
                sp.dma_start(xs[:, q, :], tile_in[:, bass.ds(s, 1), :].rearrange("p a d -> p (a d)")).then_inc(s_xs[q], 16)
                sp.dma_start(b2[:, q, :], a["L0_ffn_b2"][bass.ds(e, 1), :].rearrange("a d -> (a d)").partition_broadcast(P)
                             ).then_inc(s_xs[q], 16)

            turns(sp, step)
            for q in range(RING):
                store(X_N - RING + q, q)
            for n in range(2):
                sp.wait_ge(s_out[n], 16 * X_N // 2)

        @block.scalar
        def _(act):
            def keep_x(s, q):
                act.wait_ge(s_xT, s + 1)
                nc.scalar.activation(xT[:, q % 2], ps_x[q % 2][:], ACT.Copy).then_inc(s_xTk, 1)

            def step(s, q, i):
                e = expert(act, s)
                wait_alone(act, s_hT, s + 1)
                for c in range(FC):
                    last = nc.scalar.activation(hT[:, c, :], ps_hT[q % 2][:, c, :], ACT.Relu, bias=k["b1T"][:, bass.ds(e * FC + c, 1)])
                last.then_inc(s_hTk, 1)
                if before(s + 2, X_N):
                    keep_x(s + 2, q)

            keep_x(0, 0)
            keep_x(1, 1)
            turns(act, step)

        @block.vector
        def _(dve):
            def keep_h(s, q):
                dve.wait_ge(s_h, s + 1)
                nc.vector.tensor_copy(hidden[:], ps_h[q % 2][:]).then_inc(s_hk, 1)

            def step(s, q, i):
                if before(s + 1, X_N):
                    keep_h(s + 1, q + 1)
                if after(s, 2):
                    dve.wait_ge(s_out[q % 2], (i * 2 + q // 2) * 16)
                dve.wait_ge(s_y, s + 1)
                nc.vector.tensor_tensor(y[:, q % 2, :], ps_y[q % 2][:], b2[:, q, :], ALU.add).then_inc(s_yk, 1)

            keep_h(0, 0)
            turns(dve, step)

        @block.tensor
        def _(pe):
            def turn_x(s, q, i):
                wait_alone(pe, s_xs[q], i * 32 + 32)
                for c in range(DC):
                    last = nc.tensor.transpose(ps_x[q % 2][:, c, :], xs[:, q, c * P:(c + 1) * P], k["ident"][:])
                last.then_inc(s_xT, 1)

            def first_product(s, q):
                e = expert(pe, s)
                wait_alone(pe, s_xTk, s + 1)
                for c in range(DC):
                    last = nc.tensor.matmul(ps_h[q % 2][:], xT[:, q % 2, c, :], k["w1"][:, bass.ds(e, 1), c, :].rearrange("p a f -> p (a f)"),
                                            start=c == 0, stop=c == DC - 1)
                last.then_inc(s_h, 1)

            def turn_h(s, q):
                wait_alone(pe, s_hk, s + 1)
                for c in range(FC):
                    last = nc.tensor.transpose(ps_hT[q % 2][:, c, :], hidden[:, c * P:(c + 1) * P], k["ident"][:])
                last.then_inc(s_hT, 1)

            def second_product(s, q):
                e = expert(pe, s)
                if after(s, 2):
                    wait_alone(pe, s_yk, s - 1)
                wait_alone(pe, s_hTk, s + 1)
                for c in range(FC):
                    last = nc.tensor.matmul(ps_y[q % 2][:], hT[:, c, :], w2[:, bass.ds(e, 1), c, :].rearrange("p a d -> p (a d)"),
                                            start=c == 0, stop=c == FC - 1)
                last.then_inc(s_y, 1)

            def step(s, q, i):
                if before(s + 1, X_N):
                    first_product(s + 1, q + 1)
                second_product(s, q)
                if before(s + 2, X_N):
                    turn_x(s + 2, (q + 2) % RING, i + (q + 2) // RING)
                if before(s + 1, X_N):
                    turn_h(s + 1, q + 1)

            turn_x(0, 0, 0)
            turn_x(1, 1, 0)
            pe.wait_ge(s_w2, 16 * E0)
            first_product(0, 0)
            turn_h(0, 0)
            turns(pe, step)


def normalise(o, out, x, mean, rstd):
    with o.eng.Fori(0, TN) as t:
        o.enter(t, 1)
        o.done(o.eng.tensor_scalar(out[:, bass.ds(t, 1), :].rearrange("p a d -> p (a d)"),
                                   x[:, bass.ds(t, 1), :].rearrange("p a d -> p (a d)"),
                                   mean[:, bass.ds(t, 1)], rstd[:, bass.ds(t, 1)], ALU.subtract, ALU.mult))
        o.leave(TN)
    o.settle()


def stage_combine(nc, a, k):
    with ExitStack() as ctx:
        m = Memory(nc, ctx, "c")
        yk = m.sb("yk", [NP, TOPK, TN, D])
        gamma = m.sb("gamma", [NP, D])
        beta = m.sb("beta", [NP, D])
        st = m.sb("st", [NP, TN, 6])
        mean = m.sb("mean", [NP, TN])
        rstd = m.sb("rstd", [NP, TN])
        tmp = m.sb("tmp", [NP, TN])
        s_w = m.sem("weights")
        s_y = [m.sem(f"expert_rows{r}") for r in range(TOPK)]
        s_var = m.sem("variance")
        s_std = m.sem("std")
        s_v = m.sem("vector_steps")
        block = ctx.enter_context(nc.Block())

        @block.sync
        def _(sp):
            sp.dma_start(gamma[:], a["L0_ffn_gamma"].partition_broadcast(NP)).then_inc(s_w, 16)
            sp.dma_start(beta[:], a["L0_ffn_beta"].partition_broadcast(NP)).then_inc(s_w, 16)

        @block.gpsimd
        def _(pool):
            for r in range(TOPK):
                for t in range(TN):
                    pool.indirect_dma_start(
                        out=yk[:, r, t, :], out_offset=None, in_=k["expert_out"],
                        in_offset=bass.IndirectOffsetOnAxis(ap=k["pairs"][:, r * TN + t:r * TN + t + 1].bitcast(U32), axis=0)
                    ).then_inc(s_y[r], 16)

        @block.scalar
        def _(act):
            for n in range(2):
                act.wait_ge(s_var, n + 1)
                nc.scalar.activation(rstd[:], rstd[:], ACT.Sqrt, bias=k["eps5"][0:NP, :]).then_inc(s_std, 1)

        @block.vector
        def _(dve):
            o = Order(dve, s_v)
            v = nc.vector
            y = k["normed"]

            def all_tiles(row):
                return spread(row.unsqueeze(1), NP, TN, D)

            for r in range(TOPK):
                dve.wait_ge(s_y[r], 16 * TN)
                o.done(v.tensor_tensor(yk[:, r], yk[:, r], spread(k["gate"][:, r, :].unsqueeze(2), NP, TN, D), ALU.mult))
                o.settle()
                o.done(v.tensor_tensor(y, y, yk[:, r], ALU.add))
                o.settle()
            for n, rows in enumerate((y, k["x"][:])):
                layer_norm_stats(o, rows, st, mean[:], rstd[:], tmp[:])
                dve.sem_inc(s_var, 1)
                dve.wait_ge(s_std, n + 1)
                o.done(v.reciprocal(rstd[:], rstd[:]))
                o.settle()
                normalise(o, y, rows, mean, rstd)
                if n == 0:
                    dve.wait_ge(s_w, 32)
                    o.done(v.tensor_tensor(y, y, all_tiles(gamma[:]), ALU.mult))
                    o.settle()
                    o.done(v.tensor_tensor(y, y, all_tiles(beta[:]), ALU.add))
                    o.settle()
                    o.done(v.tensor_tensor(k["x"][:], k["x"][:], y, ALU.add))
                    o.settle()


def stage_project1(nc, a, k):
    with ExitStack() as ctx:
        m = Memory(nc, ctx, "p1")
        MH = 8
        MD = D // MH
        HC = P // MD
        w = m.sb("w", [P, DC, 4 * D])
        wa = m.sb("wa", [P, DC, 2, H])
        wprod = m.sb("wprod", [P, D])
        att = m.sb("att", [P, 2, D])
        n1 = m.sb("n1", [P, DC])
        n2 = m.sb("n2", [NP, D])
        wout = m.sb("wout", [P, DC, D])
        bout = m.sb("bout", [NP, D])
        gbias = m.sb("gbias", [NP, D])
        same = m.sb("same", [P, P])
        st = m.sb("st", [NP, TN, 6])
        mean = m.sb("mean", [NP, TN])
        rs = m.sb("rs", [NP, TN])
        tmp = m.sb("tmp", [NP, TN])
        eps6 = m.sb("eps6", [P, 1])
        zrow = m.sb("zrow", [P, ROW])
        xn = m.sb("xn", [NP, TB, D])
        xT = m.sb("xT", [P, TB, DC, NP])
        low = m.sb("low", [NP, TB, 2 * D])
        high = m.sb("high", [NP, TB, 2 * D])
        key = m.sb("key", [NP, TB, D])
        val = m.sb("val", [NP, TB, D])
        lin = m.sb("lin", [NP, TB, D])
        q = m.sb("q", [NP, TN, D])
        score = m.sb("score", [NP, TN, 2 * H])
        least = m.sb("least", [NP, H])
        least1 = m.sb("least1", [H, 1])
        leastb = m.sb("leastb", [H, P])
        shift = m.sb("shift", [NP, H])
        kv = m.sb("kv", [P, DC, P])
        kz = m.sb("kz", [P, DC, HC])
        zinv = m.sb("zinv", [NP, TB, MH])
        ps_T = m.banks("ps_T", 3)
        ps_p = m.banks("ps_p", 3)
        ps_a = m.ps("ps_a", [P, TB * 2 * H])
        ps_kv = m.ps("ps_kv", [P, DC * (P + 1)])
        kv_of = [ps_kv[:, c * (P + 1):c * (P + 1) + P] for c in range(DC)]
        ks_of = [ps_kv[:, c * (P + 1) + P:(c + 1) * (P + 1)] for c in range(DC)]

        s_w = m.sem("weights")
        s_same = m.sem("same_ready")
        s_wk = m.sem("weights_ready")
        s_z = m.sem("zeros")
        s_ms = m.sem("mean_squares")
        s_rms = m.sem("rms")
        s_xn = m.sem("normed")
        s_xT = m.sem("xT_made")
        s_xTk = m.sem("xT_kept")
        s_qk = m.sem("qk_made")
        s_vx = m.sem("vx_made")
        s_vxk = m.sem("vx_kept")
        s_low = m.sem("low_part")
        s_high = m.sem("high_part")
        s_k = m.sem("key_ready")
        s_kv = m.sem("kv_added")
        s_a = m.sem("scores_made")
        s_ak = m.sem("scores_kept")
        s_tab = m.sem("table_written")
        s_zero = m.sem("empty_rows")
        s_l = m.sem("least_steps")
        s_lT = m.sem("least_turned")
        s_sc = m.sem("score_rows")
        s_kvk = m.sem("kv_kept")
        s_num = m.sem("numerators")
        s_att = m.sem("attention_rows")
        s_o = m.sem("outputs")
        s_v = m.sem("vector_steps")
        block = ctx.enter_context(nc.Block())

        def row_of(t3, t):
            return t3[:, bass.ds(t, 1), :].rearrange("p a d -> p (a d)")

        def turns(eng, step):
            step(0, True)
            with eng.Fori(1, NB) as u:
                step(u, False)

        @block.sync
        def _(sp):
            load_weight(sp, w[:, :, 0:3 * D], a["L1_mix_w_qkv"], s_w)
            load_weight(sp, w[:, :, 3 * D:], a["L1_gnn_W"], s_w)
            load_weight(sp, wout[:], a["L1_mix_w_out"], s_w)
            for j, name in enumerate(("L1_gnn_att_src", "L1_gnn_att_dst")):
                sp.dma_start(att[:, j, :], a[name].rearrange("h o -> (h o)").partition_broadcast(P)).then_inc(s_w, 16)
            for c in range(DC):
                sp.dma_start(n1[:, c:c + 1], a["L1_mix_w_norm1"][c * P:(c + 1) * P].rearrange("(p a) -> p a", a=1)).then_inc(s_w, 16)
            for t, name in ((n2, "L1_mix_w_norm2"), (bout, "L1_mix_b_out"), (gbias, "L1_gnn_bias")):
                sp.dma_start(t[:], a[name].partition_broadcast(NP)).then_inc(s_w, 16)
            sp.wait_ge(s_z, 2)
            extra = B1 * G1_BINS - NN
            sp.dma_start(k["table1"][NN:, :], zrow[0:extra, :]).then_inc(s_zero, 16)
            sp.dma_start(k["score1"][NN:, :], zrow[0:extra, 0:2 * H]).then_inc(s_zero, 16)
            rows = k["table1"][0:NN, :].rearrange("(p t) d -> p t d", p=NP)

            def step(u, first):
                for j in range(TB):
                    t = u * TB + j
                    wait_alone(sp, s_vxk, t + 1)
                    sp.dma_start(rows[:, bass.ds(t, 1), 0:D].rearrange("p a d -> p (a d)"), lin[:, j, :]).then_inc(s_tab, 16)

            turns(sp, step)
            sp.wait_ge(s_sc, 1)
            sp.dma_start(rows[:, :, D:], score[:, :, 0:H]).then_inc(s_zero, 16)
            sp.dma_start(k["score1"][0:NN, :].rearrange("(p t) d -> p t d", p=NP), score[:]).then_inc(s_zero, 16)
            sp.wait_ge(s_zero, 64)
            sp.wait_ge(s_tab, 16 * TN)

        @block.gpsimd
        def _(pool):
            nc.gpsimd.memset(same[:], 1.0).then_inc(s_same, 1)
            view = same[:].rearrange("p (h d) -> p h d", h=HC)
            pool.wait_ge(s_same, 1)
            nc.gpsimd.affine_select(out=view, in_=view, compare_op=ALU.is_ge, fill=0.0, base=0,
                                    pattern=[[-MD, HC], [0, MD]], channel_multiplier=1).then_inc(s_same, 1)
            pool.wait_ge(s_same, 2)
            nc.gpsimd.affine_select(out=view, in_=view, compare_op=ALU.is_ge, fill=0.0, base=MD - 1,
                                    pattern=[[MD, HC], [0, MD]], channel_multiplier=-1).then_inc(s_same, 1)

        @block.scalar
        def _(act):
            act.wait_ge(s_ms, 1)
            nc.scalar.activation(rs[:], rs[:], ACT.Sqrt, bias=eps6[0:NP, :]).then_inc(s_rms, 1)

            def step(u, first):
                wait_alone(act, s_xT, u + 1)
                keep_transposed(nc.scalar, s_xTk, xT[:], ps_T)
                for j in range(TB):
                    t = u * TB + j
                    scale = rs[:, bass.ds(t, 1)]
                    if not first:
                        wait_alone(act, s_kv, t - TB + 1)
                        wait_alone(act, s_tab, u * 16 * TB)
                    wait_alone(act, s_vx, t + 1)
                    nc.scalar.activation(val[:, j, :], ps_p[0:NP, 2, 0:D], ACT.Copy, scale=scale)
                    nc.scalar.activation(lin[:, j, :], ps_p[0:NP, 2, D:], ACT.Copy).then_inc(s_vxk, 1)
                    wait_alone(act, s_low, t + 1)
                    nc.scalar.activation(high[:, j, :], ps_p[0:NP, j % 2, :], ACT.Relu, scale=scale)
                    nc.scalar.activation(low[:, j, :], low[:, j, :], ACT.Exp).then_inc(s_high, 1)

            turns(act, step)
            with act.Fori(0, NB) as u:
                for n in range(2):
                    wait_alone(act, s_xT, u * 2 + n + NB + 1)
                    keep_transposed(nc.scalar, s_xTk, xT[:], ps_T)
            act.wait_ge(s_ms, 2)
            nc.scalar.activation(rs[:], rs[:], ACT.Sqrt, bias=eps6[0:NP, :]).then_inc(s_rms, 1)

        @block.vector
        def _(dve):
            o = Order(dve, s_v)
            v = nc.vector
            v.memset(zrow[:], 0.0).then_inc(s_z, 1)
            v.memset(eps6[:], 1e-6).then_inc(s_z, 1)

            def root_mean_square(rows, n):
                layer_norm_stats(o, rows, st, mean[:], rs[:], tmp[:])
                o.done(v.tensor_tensor(mean[:], mean[:], mean[:], ALU.mult))
                o.settle()
                o.done(v.tensor_tensor(rs[:], rs[:], mean[:], ALU.add))
                o.settle()
                dve.sem_inc(s_ms, 1)
                dve.wait_ge(s_rms, n)
                o.done(v.reciprocal(rs[:], rs[:]))
                o.settle()

            root_mean_square(k["normed"], 1)
            dve.wait_ge(s_w, 16 * 10)
            for c in range(DC):
                for j in range(2):
                    o.settle()
                    o.done(v.tensor_tensor(wprod[:], w[:, c, 3 * D:], att[:, j, :], ALU.mult))
                    o.settle()
                    o.done(v.tensor_reduce(wa[:, c, j, :], wprod[:].rearrange("p (h o) -> p h o", h=H), AX, ALU.add))
                v.tensor_scalar(w[:, c, 0:3 * D], w[:, c, 0:3 * D], n1[:, c:c + 1], None, ALU.mult).then_inc(s_wk, 1)
            o.settle()
            dve.sem_inc(s_wk, 1)

            def step(u, first):
                if not first:
                    dve.wait_ge(s_xTk, u)
                v.tensor_copy(xn[:], k["normed"][:, bass.ds(u * TB, TB), :]).then_inc(s_xn, 1)
                for j in range(TB):
                    t = u * TB + j
                    dve.wait_ge(s_qk, t + 1)
                    if not first:
                        dve.wait_ge(s_kv, t - TB + 1)
                    v.tensor_scalar(low[:, j, :], ps_p[0:NP, j % 2, :], rs[:, bass.ds(t, 1)], 0.0, ALU.mult, ALU.min).then_inc(s_low, 1)
                    wait_alone(dve, s_high, t + 1)
                    o.done(v.tensor_tensor(row_of(q, t), low[:, j, 0:D], high[:, j, 0:D], ALU.add))
                    v.tensor_tensor(key[:, j, :], low[:, j, D:], high[:, j, D:], ALU.add).then_inc(s_k, 1)
                dve.wait_ge(s_a, u + 1)
                v.tensor_copy(score[:, bass.ds(u * TB, TB), :], ps_a[0:NP, :].rearrange("p (t h) -> p t h", t=TB)).then_inc(s_ak, 1)

            step(0, True)
            with dve.Fori(1, NB) as u:
                o.enter(u - 1, TB)
                step(u, False)
                o.leave(NB - 1)
            dve.wait_ge(s_ak, NB)
            v.tensor_reduce(least[:], score[:, :, 0:H].rearrange("p t h -> p h t"), AX, ALU.min).then_inc(s_l, 1)
            dve.wait_ge(s_lT, 1)
            o.done(v.tensor_reduce(least1[:], ps_T[0:H, 0, 0:NP], AX, ALU.min))
            o.settle()
            v.tensor_copy(leastb[:], spread(least1[:], H, P)).then_inc(s_l, 1)
            dve.wait_ge(s_lT, 2)
            o.done(v.tensor_copy(shift[:], ps_a[0:NP, 0:H]))
            o.settle()
            sb = spread(shift[:].unsqueeze(1), NP, TN, H)
            o.done(v.scalar_tensor_tensor(score[:, :, 0:H], score[:, :, 0:H], 1.0, sb, ALU.add, ALU.subtract))
            o.done(v.scalar_tensor_tensor(score[:, :, H:], score[:, :, H:], -1.0, sb, ALU.add, ALU.add))
            o.settle()
            dve.sem_inc(s_sc, 1)
            dve.wait_ge(s_kv, TN + 1)
            dve.wait_ge(s_same, 3)
            for c in range(DC):
                v.tensor_tensor(kv[:, c, :], kv_of[c], same[:], ALU.mult).then_inc(s_kvk, 1)
                v.tensor_scalar(kz[:, c, :], same[:, 0:P:MD], ks_of[c], None, ALU.mult).then_inc(s_kvk, 1)
            o.settle()
            with dve.Fori(0, NB) as u:
                o.enter(u, 6)
                v.tensor_copy(xn[:], q[:, bass.ds(u * TB, TB), :]).then_inc(s_xn, 1)
                wait_alone(dve, s_num, u + 1)
                den = ps_a[0:NP, :].rearrange("p (t h) -> p t h", t=TB)
                o.done(v.tensor_scalar(zinv[:], den, 1e-6, None, ALU.add))
                o.settle()
                o.done(v.reciprocal(zinv[:], zinv[:]))
                o.settle()
                for b, n in ((0, 2), (1, 2), (2, 1)):
                    out = xn[:, 2 * b:2 * b + n, :].rearrange("p t (h d) -> p t h d", h=MH)
                    num = ps_p[0:NP, b, 0:n * D].rearrange("p (t h d) -> p t h d", t=n, h=MH)
                    last = v.tensor_tensor(out, num, spread(zinv[:, 2 * b:2 * b + n, :].unsqueeze(3), NP, n, MH, MD), ALU.mult)
                last.then_inc(s_att, 1)
                wait_alone(dve, s_o, u + 1)
                for b, n in ((0, 2), (1, 2)):
                    o.done(v.tensor_tensor(low[:, 2 * b:2 * b + n, 0:D], ps_p[0:NP, b, 0:n * D].rearrange("p (t d) -> p t d", t=n),
                                           spread(bout[:].unsqueeze(1), NP, n, D), ALU.add))
                o.done(v.tensor_tensor(low[:, 4, 0:D], ps_p[0:NP, 2, 0:D], bout[:], ALU.add))
                o.settle()
                rows = k["normed"][:, bass.ds(u * TB, TB), :]
                o.done(v.tensor_tensor(rows, rows, low[:, :, 0:D], ALU.add))
                o.settle()
                o.leave(NB)
            o.settle()
            h = k["normed"]
            root_mean_square(h, 2)

            def add(t3):
                o.done(v.tensor_tensor(k["x"][:], k["x"][:], t3, ALU.add))
                o.settle()

            add(h)
            o.done(v.tensor_tensor(h, h, spread(rs[:].unsqueeze(2), NP, TN, D), ALU.mult))
            o.settle()
            o.done(v.tensor_tensor(h, h, spread(n2[:].unsqueeze(1), NP, TN, D), ALU.mult))
            o.settle()
            add(h)
            add(spread(gbias[:].unsqueeze(1), NP, TN, D))

        @block.tensor
        def _(pe):
            mm = nc.tensor.matmul
            pe.wait_ge(s_wk, DC + 1)
            pe.wait_ge(s_z, 2)
            mm(ps_kv[:], zrow[:, 0:P], w[:, 0, 0:DC * (P + 1)], start=True, stop=False, skip_group_check=True)

            def turn(n):
                wait_alone(pe, s_xn, n)
                for j, place in enumerate(tile_places(ps_T)):
                    for c in range(DC):
                        last = nc.tensor.transpose(place[:, c, :], xn[:, j, c * P:(c + 1) * P], k["ident"][0:NP, 0:NP])
                last.then_inc(s_xT, 1)
                wait_alone(pe, s_xTk, n)

            def state(t, j):
                wait_alone(pe, s_k, t + 1)
                for c in range(DC):
                    kc = key[:, j, c * P:(c + 1) * P]
                    mm(kv_of[c], kc, val[:, j, c * P:(c + 1) * P], start=False, stop=False, skip_group_check=True)
                    last = mm(ks_of[c], kc, k["one"][0:NP, 0:1], start=False, stop=False, skip_group_check=True)
                last.then_inc(s_kv, 1)

            def step(u, first):
                turn(u + 1)
                for j in range(TB):
                    t = u * TB + j
                    if not (first and j < 2):
                        wait_alone(pe, s_high, t - 1 if j else t)
                    for c in range(DC):
                        last = mm(ps_p[0:NP, j % 2, :], xT[:, j, c, :], w[:, c, 0:2 * D], start=c == 0, stop=c == DC - 1)
                    last.then_inc(s_qk, 1)
                    if not (first and j < 1):
                        wait_alone(pe, s_vxk, t)
                    for c in range(DC):
                        last = mm(ps_p[0:NP, 2, :], xT[:, j, c, :], w[:, c, 2 * D:], start=c == 0, stop=c == DC - 1)
                    last.then_inc(s_vx, 1)
                    if not first and j == 0:
                        wait_alone(pe, s_ak, u)
                    for c in range(DC):
                        last = mm(ps_a[0:NP, j * 2 * H:(j + 1) * 2 * H], xT[:, j, c, :], wa[:, c].rearrange("p j h -> p (j h)"),
                                  start=c == 0, stop=c == DC - 1)
                    if j == TB - 1:
                        last.then_inc(s_a, 1)
                    if j > 0:
                        state(t - 1, j - 1)
                state(u * TB + TB - 1, TB - 1)

            turns(pe, step)
            mm(ps_kv[:], zrow[:, 0:P], w[:, 0, 0:DC * (P + 1)], start=False, stop=True, skip_group_check=True).then_inc(s_kv, 1)
            pe.wait_ge(s_l, 1)
            nc.tensor.transpose(ps_T[0:H, 0, 0:NP], least[:], k["ident"][0:NP, 0:NP]).then_inc(s_lT, 1)
            pe.wait_ge(s_l, 2)
            mm(ps_a[:, 0:H], leastb[:], k["ident"][0:H, 0:H], start=True, stop=True).then_inc(s_lT, 1)
            pe.wait_ge(s_kvk, 2 * DC)
            pe.wait_ge(s_sc, 1)
            with pe.Fori(0, NB) as u:
                wait_alone(pe, s_xn, u + NB + 1)
                for j, place in enumerate(tile_places(ps_T)):
                    for c in range(DC):
                        last = nc.tensor.transpose(place[:, c, :], xn[:, j, c * P:(c + 1) * P], k["ident"][0:NP, 0:NP])
                last.then_inc(s_xT, 1)
                wait_alone(pe, s_xTk, u * 2 + NB + 1)
                for j in range(TB):
                    for c in range(DC):
                        at = j % 2 * D + c * P
                        mm(ps_p[0:NP, j // 2, at:at + P], xT[:, j, c, :], kv[:, c, :], start=True, stop=True)
                        at = j * MH + c * HC
                        last = mm(ps_a[0:NP, at:at + HC], xT[:, j, c, :], kz[:, c, :], start=True, stop=True)
                last.then_inc(s_num, 1)
                wait_alone(pe, s_att, u + 1)
                for j, place in enumerate(tile_places(ps_T)):
                    for c in range(DC):
                        last = nc.tensor.transpose(place[:, c, :], xn[:, j, c * P:(c + 1) * P], k["ident"][0:NP, 0:NP])
                last.then_inc(s_xT, 1)
                wait_alone(pe, s_xTk, u * 2 + NB + 2)
                for j in range(TB):
                    for c in range(DC):
                        last = mm(ps_p[0:NP, j // 2, j % 2 * D:(j % 2 + 1) * D], xT[:, j, c, :], wout[:, c, :], start=c == 0, stop=c == DC - 1)
                last.then_inc(s_o, 1)


def stage_edges1(nc, a, k):
    with ExitStack() as ctx:
        m = Memory(nc, ctx, "e1")
        TG = 8
        RING = 3
        TURNS = G1_N // TG
        assert (TURNS - 1) % RING == 0
        STEPS = (TURNS - 1) // RING
        W = HD + 1
        rec = m.sb("rec", [P, G1_N + TG, 2])
        index = m.sb("index", [P, RING, TG], I32)
        rows = m.sb("rows", [P, RING, TG, ROW])
        nodes = m.sb("nodes", [P, G1_BINS, 2 * H])
        to = m.sb("to", [P, G1_BINS])
        top = m.sb("top", [P, G1_BINS])
        acc = m.sb("acc", [P, G1_BINS, W])
        headsel = m.sb("headsel", [P, H])
        identb = m.sb("identb", [P, P], BF16)
        hot = m.sb("hot", [P, RING, TG, P], BF16)
        hotT = m.sb("hotT", [P, RING, TG, P])
        marked = m.sb("marked", [P, TG, P])
        weight = m.sb("weight", [P, TG, P])
        most = m.sb("most", [P, TG])
        tops = m.sb("tops", [P, 2, TG])
        tos = m.sb("tos", [P, TG])
        z = m.sb("z", [P, 2, TG])
        drop = m.sb("drop", [P, TG])
        scale = m.sb("scale", [P, RING, TG])
        spreads = m.sb("spreads", [P, TG, 2 * H])
        score = m.sb("score", [P, TG, H])
        ex = m.sb("ex", [P, TG, H])

        ps_hT = ctx.enter_context(nc.psum_tensor("e1_ps_hT", [P, TG, P], BF16))
        ps_mT = m.banks("ps_mT", 2)
        ps_S = m.ps("ps_S", [P, TG, 2 * H])
        ps_A = m.banks("ps_A", 2)

        s_rec = m.sem("records")
        s_in = m.sem("nodes_in")
        s_const = m.sem("const_ready")
        s_idx = m.sem("index_staged")
        s_rows = [m.sem(f"rows{j}") for j in range(RING)]
        s_hot = m.sem("one_hot")
        s_hT = m.sem("one_hot_T")
        s_hTk = m.sem("one_hot_T_kept")
        s_mk = m.sem("marked_scores")
        s_mT = m.sem("marked_T")
        s_to = m.sem("to_scores_kept")
        s_spr = m.sem("spreads_ready")
        s_S = m.sem("edge_spreads")
        s_sc = m.sem("scores")
        s_ex = m.sem("exponentials")
        s_wt = m.sem("weights")
        s_scale = m.sem("scales")
        s_agg = m.sem("added_up")
        s_acc = m.sem("accumulated")
        s_done = m.sem("averaged")
        s_out = m.sem("written")
        s_v = m.sem("vector_steps")
        block = ctx.enter_context(nc.Block())

        def turns(eng, step, tail=(), enter=None, leave=None):
            step(0, RING - 1, -1)
            for j in range(RING):
                step(1 + j, j, 0)
            with eng.Fori(1, STEPS) as u:
                if enter:
                    enter(u)
                for j in range(RING):
                    step(u * RING + 1 + j, j, u)
                if leave:
                    leave()
            for n in tail:
                step(TURNS + n, n, None)

        def known(i):
            return isinstance(i, int)

        def bucket(eng, tile):
            return eng.value_load(k["bin1"][0:1, bass.ds(tile, 1)], min_val=0, max_val=G1_BINS - 1)

        def column(t2, at):
            return t2[:, bass.ds(at, 1)]

        @block.sync
        def _(sp):
            sp.dma_start(rec[:, 0:G1_N, :].rearrange("p t f -> p (t f)"),
                         k["sorted1"].rearrange("(p t) f -> p (t f)", p=P)).then_inc(s_rec, 16)
            by_lane = k["score1"].rearrange("(n k) c -> n (k c)", n=B1)
            rows_of = k["table1"].rearrange("(n k) d -> n k d", n=B1)
            out_of = k["attended1"].rearrange("(n k) d -> n k d", n=B1)
            for h in range(H):
                sp.dma_start(nodes[h * B1:(h + 1) * B1].rearrange("p k c -> p (k c)"), by_lane).then_inc(s_in, 16)
            for h in range(H):
                sp.dma_start(acc[h * B1:(h + 1) * B1, :, 0:HD], rows_of[:, :, h * HD:(h + 1) * HD]).then_inc(s_in, 16)
            sp.wait_ge(s_done, 1)
            for h in range(H):
                sp.dma_start(out_of[:, :, h * HD:(h + 1) * HD], acc[h * B1:(h + 1) * B1, :, 0:HD]).then_inc(s_out, 16)
            sp.wait_ge(s_out, 16 * H)

        @block.gpsimd
        def _(pool):
            def step(i, j, u):
                if not known(i) or i >= RING + 1:
                    wait_alone(pool, s_agg, i - RING + 1)
                elif i == RING:
                    wait_alone(pool, s_agg, 1)
                nc.gpsimd.tensor_copy(index[:, j, :], rec[:, bass.ds(i * TG, TG), 0:1].rearrange("p a b -> p (a b)")
                                      ).then_inc(s_idx, 1)
                wait_alone(pool, s_idx, i + 1)
                for q in range(TG):
                    pool.indirect_dma_start(
                        out=rows[:, j, q, :], out_offset=None, in_=k["table1"],
                        in_offset=bass.IndirectOffsetOnAxis(ap=index[:, j, q:q + 1].bitcast(U32), axis=0)
                    ).then_inc(s_rows[j], 16)

            pool.wait_ge(s_rec, 16)
            turns(pool, step)

        @block.vector
        def _(dve):
            o = Order(dve, s_v)
            v = nc.vector

            def one_hot(i, j):
                lanes = rec[:, bass.ds(i * TG, TG), 1:2].unsqueeze(3)
                v.tensor_tensor(hot[:, j].rearrange("p t (h n) -> p t h n", h=H),
                                spread(k["iota"][:, 0:B1].unsqueeze(1).unsqueeze(1), P, TG, H, B1),
                                spread(lanes, P, TG, H, B1), ALU.is_equal).then_inc(s_hot, 1)

            def by_head(t3):
                return t3.rearrange("p t (h n) -> p t h n", h=H)

            def mark(i, j, u):
                dve.wait_ge(s_rows[j], 128 * (u + 1 + (j == RING - 1)))
                dve.wait_ge(s_hot, i + 1)
                v.tensor_tensor(by_head(marked[:]), by_head(hot[:, j]), spread(rows[:, j, :, D:].unsqueeze(3), P, TG, H, B1),
                                ALU.mult).then_inc(s_mk, 1)

            def scores(i, j):
                sc = score[:]
                dve.wait_ge(s_S, i + 1)
                o.done(v.tensor_tensor(sc, rows[:, j, :, D:], ps_S[:, :, 0:H], ALU.add))
                o.settle()
                o.done(v.scalar_tensor_tensor(sc, sc, 0.2, sc, ALU.mult, ALU.max))
                o.settle()
                v.tensor_tensor(sc, sc, ps_S[:, :, H:], ALU.subtract).then_inc(s_sc, 1)

            def accumulate(i, j):
                wait_alone(dve, s_agg, i + 1)
                wait_alone(dve, s_scale, i + 1)
                for q in range(TG):
                    tile = i * TG + q
                    block_of = bucket(dve, tile)
                    at = acc[:, bass.ds(block_of, 1), :].rearrange("p a w -> p (a w)")
                    if not (known(i) and i == 0 and q == 0):
                        dve.wait_ge(s_acc, tile)
                    v.scalar_tensor_tensor(at, at, scale[:, j, q:q + 1], ps_A[:, q // 4, q % 4 * W:(q % 4 + 1) * W],
                                           ALU.mult, ALU.add).then_inc(s_acc, 1)

            def weigh(i, j):
                dve.wait_ge(s_ex, i + 1)
                v.tensor_tensor(by_head(weight[:]), by_head(hot[:, j]), spread(ex[:].unsqueeze(3), P, TG, H, B1),
                                ALU.mult).then_inc(s_wt, 1)

            def raise_tops(i):
                wait_alone(dve, s_mT, i + 1)
                o.done(v.tensor_reduce(most[:].rearrange("p (b t) -> p b t", b=2),
                                       ps_mT[:].rearrange("p b (t e) -> p b t e", t=TG // 2), AX, ALU.max))
                for q in range(TG):
                    block_of = bucket(dve, i * TG + q)
                    at = column(top, block_of)
                    o.settle()
                    o.done(v.tensor_tensor(tops[:, 0, q:q + 1], at, at, ALU.max))
                    o.done(v.tensor_tensor(at, at, most[:, q:q + 1], ALU.max))
                o.settle()
                o.done(v.tensor_tensor(tops[:, 1, :], tops[:, 0, :], most[:], ALU.max))
                dve.wait_ge(s_to, i + 1)
                o.done(v.tensor_tensor(spreads[:, :, 0:H], spread(tos[:].unsqueeze(2), P, TG, H),
                                       spread(headsel[:].unsqueeze(1), P, TG, H), ALU.mult))
                o.settle()
                o.done(v.tensor_tensor(z[:], tops[:], spread(tos[:].unsqueeze(1), P, 2, TG), ALU.add))
                o.settle()
                o.done(v.scalar_tensor_tensor(z[:], z[:], 0.2, z[:], ALU.mult, ALU.max))
                o.settle()
                o.done(v.tensor_tensor(drop[:], z[:, 0, :], z[:, 1, :], ALU.subtract))
                o.done(v.tensor_tensor(spreads[:, :, H:], spread(z[:, 1, :].unsqueeze(2), P, TG, H),
                                       spread(headsel[:].unsqueeze(1), P, TG, H), ALU.mult))
                o.settle()
                dve.sem_inc(s_spr, 1)

            o.done(v.memset(headsel[:], 0.0))
            o.done(v.memset(rec[:, G1_N:, :], -1.0))
            o.settle()
            for h in range(H):
                o.done(v.memset(headsel[h * B1:(h + 1) * B1, h:h + 1], 1.0))
            v.tensor_copy(identb[:], k["ident"][:]).then_inc(s_const, 1)
            dve.wait_ge(s_rec, 16)
            dve.wait_ge(s_in, 16 * 2 * H)
            for h in range(H):
                at = slice(h * B1, (h + 1) * B1)
                o.done(v.tensor_copy(top[at, :], nodes[at, :, h]))
                v.tensor_copy(to[at, :], nodes[at, :, H + h]).then_inc(s_const, 1)
            o.done(v.memset(acc[:, :, HD:], 1.0))
            o.settle()
            one_hot(0, RING - 1)

            def step(i, j, u):
                over = u is None
                before, two_before = (j - 1) % RING, (j - 2) % RING
                if not over:
                    mark(i, j, u)
                if not (known(i) and (i < 1 or i > TURNS)):
                    scores(i - 1, before)
                if not (known(i) and i < 2):
                    accumulate(i - 2, two_before)
                if not (known(i) and (i < 1 or i > TURNS)):
                    weigh(i - 1, before)
                if not over:
                    raise_tops(i)
                    one_hot(i + 1, (j + 1) % RING)

            per = RING * (2 + 1 + 2 * TG + 6)

            def enter(u):
                o.enter(u - 1, per)

            turns(dve, step, range(2), enter, lambda: o.leave(STEPS - 1))
            w = acc[:, :, HD:]
            dve.wait_ge(s_acc, G1_N)
            o.done(v.tensor_scalar(w, w, 1e-16, None, ALU.add))
            o.settle()
            o.done(v.reciprocal(w, w))
            o.settle()
            v.tensor_tensor(acc[:, :, 0:HD], acc[:, :, 0:HD], spread(w, P, G1_BINS, HD), ALU.mult).then_inc(s_done, 1)

        @block.scalar
        def _(act):
            def keep_hot(i, j):
                act.wait_ge(s_hT, i + 1)
                nc.scalar.activation(hotT[:, j], ps_hT[:], ACT.Copy).then_inc(s_hTk, 1)

            def step(i, j, u):
                if not (known(i) and i < 1):
                    act.wait_ge(s_sc, i)
                    nc.scalar.activation(ex[:], score[:], ACT.Exp).then_inc(s_ex, 1)
                if u is None:
                    return
                for q in range(TG):
                    block_of = bucket(act, i * TG + q)
                    last = nc.scalar.activation(tos[:, q:q + 1], column(to, block_of), ACT.Copy)
                last.then_inc(s_to, 1)
                keep_hot(i + 1, (j + 1) % RING)
                act.wait_ge(s_spr, i + 1)
                nc.scalar.activation(scale[:, j, :], drop[:], ACT.Exp).then_inc(s_scale, 1)

            act.wait_ge(s_const, 1 + H)
            keep_hot(0, RING - 1)
            turns(act, step, range(1))

        @block.tensor
        def _(pe):
            mm = nc.tensor.matmul

            def turn_hot(i, j):
                wait_alone(pe, s_hot, i + 1)
                if not (known(i) and i == 0):
                    wait_alone(pe, s_hTk, i)
                for q in range(TG):
                    last = nc.tensor.transpose(ps_hT[:, q, :], hot[:, j, q, :], identb[:])
                last.then_inc(s_hT, 1)

            def turn_marked(i):
                wait_alone(pe, s_mk, i + 1)
                for q in range(TG):
                    last = nc.tensor.transpose(ps_mT[:, q // 4, q % 4 * P:(q % 4 + 1) * P], marked[:, q, :], k["ident"][:])
                last.then_inc(s_mT, 1)

            def add_up(i, j):
                wait_alone(pe, s_wt, i + 1)
                for q in range(TG):
                    at = q % 4 * W
                    for h in range(H):
                        mm(ps_A[h * B1:(h + 1) * B1, q // 4, at:at + HD], weight[:, q, h * B1:(h + 1) * B1],
                           rows[:, j, q, h * HD:(h + 1) * HD], start=True, stop=True)
                    last = mm(ps_A[:, q // 4, at + HD:at + W], weight[:, q, :], k["one"][:, 0:1], start=True, stop=True)
                last.then_inc(s_agg, 1)

            def spread_to_edges(i, j):
                wait_alone(pe, s_spr, i + 1)
                wait_alone(pe, s_hTk, i + 1)
                for q in range(TG):
                    last = mm(ps_S[:, q, :], hotT[:, j, q, :], spreads[:, q, :], start=True, stop=True)
                last.then_inc(s_S, 1)

            def step(i, j, u):
                if u is not None:
                    turn_marked(i)
                if not (known(i) and i < 1):
                    add_up(i - 1, (j - 1) % RING)
                if u is not None:
                    turn_hot(i + 1, (j + 1) % RING)
                    spread_to_edges(i, j)

            pe.wait_ge(s_const, 1 + H)
            turn_hot(0, RING - 1)
            turns(pe, step, range(1))


def stage_ffn1(nc, a, k, out):
    with ExitStack() as ctx:
        m = Memory(nc, ctx, "f")
        F = a["L1_ffn_W1"].shape[2]
        FC = F // P
        FF = TOPK * FC
        CAP = float(-(-NN * 5 // (4 * E1)))
        rows = m.sb("rows", [NP, TN, D])
        st = m.sb("st", [NP, TN, 6])
        mean = m.sb("mean", [NP, TN])
        rstd = m.sb("rstd", [NP, TN])
        tmp = m.sb("tmp", [NP, TN])
        xn = m.sb("xn", [NP, TB, D])
        xT = m.sb("xT", [P, TN, DC, NP])
        sums = m.sb("sums", [P, DC, TN])
        total = m.sb("total", [P, DC])
        wr = m.sb("wr", [P, DC, E1])
        br = m.sb("br", [1, E1])
        logit = m.sb("logit", [1, E1])
        route = m.sb("route", [1, E1])
        pick = m.sb("pick", [1, E1])
        norm = m.sb("norm", [1, 1])
        best = m.sb("best", [1, TOPK])
        which = m.sb("which", [1, TOPK])
        expert = m.sb("expert", [1, TOPK], I32)
        share = m.sb("share", [1, TOPK])
        shares = m.sb("shares", [P, TOPK])
        w1 = m.sb("w1", [P, TOPK, DC, F])
        b1 = m.sb("b1", [P, TOPK, FC])
        w2 = m.sb("w2", [P, TOPK, FC, D])
        b2 = m.sb("b2", [NP, TOPK, D])
        gamma = m.sb("gamma", [NP, D])
        beta = m.sb("beta", [NP, D])
        hT = m.sb("hT", [P, FF, TB, NP])
        ps_T = m.banks("ps_T", 3)
        ps_h = [m.ps(f"ps_h{i}", [P, 3, NP]) for i in range(2)]
        ps_y = [m.ps(f"ps_y{i}", [P, D]) for i in range(2)]
        ps_r = m.ps("ps_r", [P, E1 + TOPK])

        s_att = m.sem("attended")
        s_w = m.sem("weights")
        s_var = m.sem("variance")
        s_std = m.sem("std")
        s_xn = m.sem("normed")
        s_xT = m.sem("xT_made")
        s_xTk = m.sem("xT_kept")
        s_tot = m.sem("total")
        s_log = m.sem("logits")
        s_d = m.sem("differences")
        s_e = m.sem("exponentials")
        s_pick = m.sem("picked")
        s_sh = m.sem("shares_spread")
        s_ew = m.sem("expert_weights")
        s_w2 = m.sem("second_weights_scaled")
        s_h = m.sem("hidden_made")
        s_hk = m.sem("hidden_kept")
        s_y = m.sem("y_made")
        s_yk = m.sem("y_kept")
        s_res = m.sem("result_rows")
        s_out = m.sem("written")
        s_v = m.sem("vector_steps")
        block = ctx.enter_context(nc.Block())

        def row_of(t3, t):
            return t3[:, bass.ds(t, 1), :].rearrange("p a d -> p (a d)")

        @block.sync
        def _(sp):
            sp.dma_start(rows[:], k["attended1"][0:NN, :].rearrange("(p t) d -> p t d", p=NP)).then_inc(s_att, 16)
            load_weight(sp, wr[:], a["L1_ffn_Wr"], s_w)
            sp.dma_start(br[:], a["L1_ffn_br"].rearrange("(a e) -> a e", a=1)).then_inc(s_w, 16)
            sp.dma_start(gamma[:], a["L1_ffn_gamma"].partition_broadcast(NP)).then_inc(s_w, 16)
            sp.dma_start(beta[:], a["L1_ffn_beta"].partition_broadcast(NP)).then_inc(s_w, 16)
            sp.wait_ge(s_pick, 1)
            for r in range(TOPK):
                e = sp.value_load(expert[0:1, r:r + 1], min_val=0, max_val=E1 - 1)
                load_weight(sp, w1[:, r], a["L1_ffn_W1"][bass.ds(e, 1)].rearrange("a d f -> (a d) f"), s_ew)
                load_weight(sp, w2[:, r], a["L1_ffn_W2"][bass.ds(e, 1)].rearrange("a f d -> (a f) d"), s_ew)
                for c in range(FC):
                    sp.dma_start(b1[:, r, c:c + 1], a["L1_ffn_b1"][bass.ds(e, 1), c * P:(c + 1) * P].rearrange("a p -> p a")
                                 ).then_inc(s_ew, 16)
                sp.dma_start(b2[:, r, :], a["L1_ffn_b2"][bass.ds(e, 1), :].rearrange("a d -> (a d)").partition_broadcast(NP)
                             ).then_inc(s_ew, 16)
            to = out.rearrange("(p t) d -> p t d", p=NP)
            with sp.Fori(0, NB) as u:
                wait_alone(sp, s_res, u + 1)
                sp.dma_start(to[:, bass.ds(u * TB, TB), :], k["x"][:, bass.ds(u * TB, TB), :]).then_inc(s_out, 16)
            sp.wait_ge(s_out, 16 * NB)

        ALL_EW = 16 * TOPK * (3 + FC)

        @block.scalar
        def _(act):
            def root(n):
                act.wait_ge(s_var, n)
                nc.scalar.activation(rstd[:], rstd[:], ACT.Sqrt, bias=k["eps5"][0:NP, :]).then_inc(s_std, 1)

            root(1)
            with act.Fori(0, NB) as u:
                wait_alone(act, s_xT, u + 1)
                keep_transposed(nc.scalar, s_xTk, xT[:, bass.ds(u * TB, TB)], ps_T)
            for n, row in enumerate((route[:], route[:], share[:, 1:2])):
                act.wait_ge(s_d, n + 1)
                nc.scalar.activation(row, row, ACT.Exp).then_inc(s_e, 1)
            act.wait_ge(s_ew, ALL_EW)
            with act.Fori(0, NB) as u:
                for f in range(FF):
                    for b, n in ((0, 3), (1, 2)):
                        wait_alone(act, s_h, u * 2 * FF + f * 2 + b + 1)
                        nc.scalar.activation(hT[:, f, 3 * b:3 * b + n, :], ps_h[b][:, 0:n, :], ACT.Gelu,
                                             bias=b1[:, f // FC, f % FC:f % FC + 1]).then_inc(s_hk, 1)
            root(2)

        @block.vector
        def _(dve):
            o = Order(dve, s_v)
            v = nc.vector

            def inverse_std(n):
                dve.sem_inc(s_var, 1)
                dve.wait_ge(s_std, n)
                o.done(v.reciprocal(rstd[:], rstd[:]))
                o.settle()

            dve.wait_ge(s_att, 16)
            o.done(v.tensor_tensor(k["x"][:], k["x"][:], rows[:], ALU.add))
            o.settle()
            layer_norm_stats(o, k["x"], st, mean[:], rstd[:], tmp[:])
            inverse_std(1)
            with dve.Fori(0, NB) as u:
                for j in range(TB):
                    t = u * TB + j
                    for to in (row_of(rows, t), xn[:, j, :]):
                        last = v.tensor_scalar(to, row_of(k["x"], t), mean[:, bass.ds(t, 1)], rstd[:, bass.ds(t, 1)],
                                               ALU.subtract, ALU.mult)
                last.then_inc(s_xn, 1)
                wait_alone(dve, s_xTk, u + 1)
            o.done(v.tensor_reduce(sums[:], xT[:].rearrange("p t c n -> p c t n"), AX, ALU.add))
            o.settle()
            v.tensor_reduce(total[:], sums[:], AX, ALU.add).then_inc(s_tot, 1)
            dve.wait_ge(s_w, 16 * 4)
            dve.wait_ge(s_log, 1)
            o.done(v.scalar_tensor_tensor(logit[:], ps_r[0:1, 0:E1], 1.0 / NN, br[:], ALU.mult, ALU.add))
            o.settle()

            def softmax(n):
                o.done(v.tensor_reduce(norm[:], logit[:], AX, ALU.max))
                o.settle()
                v.tensor_scalar(route[:], logit[:], norm[:], None, ALU.subtract).then_inc(s_d, 1)
                dve.wait_ge(s_e, n)
                o.done(v.tensor_reduce(norm[:], route[:], AX, ALU.add))
                o.settle()
                o.done(v.reciprocal(norm[:], norm[:]))
                o.settle()
                o.done(v.tensor_scalar(route[:], route[:], norm[:], None, ALU.mult))
                o.settle()

            softmax(1)
            o.done(v.tensor_scalar(pick[:], route[:], float(NN), CAP, ALU.mult, ALU.max))
            o.settle()
            o.done(v.reciprocal(pick[:], pick[:]))
            o.settle()
            o.done(v.scalar_tensor_tensor(logit[:], route[:], CAP, pick[:], ALU.mult, ALU.mult))
            o.settle()
            softmax(2)
            iota = k["iota"][0:1, 0:E1]
            for r in range(TOPK):
                o.done(v.tensor_reduce(best[:, r:r + 1], route[:], AX, ALU.max))
                o.settle()
                o.done(v.tensor_scalar(pick[:], route[:], best[:, r:r + 1], None, ALU.is_equal))
                o.settle()
                o.done(v.scalar_tensor_tensor(pick[:], pick[:], -float(E1), iota, ALU.mult, ALU.add))
                o.settle()
                o.done(v.tensor_reduce(which[:, r:r + 1], pick[:], AX, ALU.min))
                o.settle()
                o.done(v.tensor_scalar(which[:, r:r + 1], which[:, r:r + 1], float(E1), None, ALU.add))
                o.settle()
                if r + 1 < TOPK:
                    o.done(v.tensor_scalar(pick[:], iota, which[:, r:r + 1], None, ALU.is_equal))
                    o.settle()
                    o.done(v.scalar_tensor_tensor(route[:], pick[:], -2.0, route[:], ALU.mult, ALU.add))
                    o.settle()
            v.tensor_copy(expert[:], which[:]).then_inc(s_pick, 1)
            v.tensor_tensor(share[:, 1:2], best[:, 1:2], best[:, 0:1], ALU.subtract).then_inc(s_d, 1)
            dve.wait_ge(s_e, 3)
            o.done(v.tensor_scalar(share[:, 0:1], share[:, 1:2], 1.0, None, ALU.add))
            o.settle()
            o.done(v.reciprocal(share[:, 0:1], share[:, 0:1]))
            o.settle()
            o.done(v.tensor_tensor(share[:, 1:2], share[:, 1:2], share[:, 0:1], ALU.mult))
            o.settle()
            dve.sem_inc(s_tot, 1)
            dve.wait_ge(s_sh, 1)
            o.done(v.tensor_copy(shares[:], ps_r[:, E1:]))
            o.settle()
            dve.wait_ge(s_ew, ALL_EW)
            for r in range(TOPK):
                v.tensor_scalar(w2[:, r], w2[:, r], shares[:, r:r + 1], None, ALU.mult).then_inc(s_w2, 1)
            o.done(v.tensor_scalar(b2[:, 0, :], b2[:, 0, :], shares[0:NP, 0:1], None, ALU.mult))
            o.settle()
            o.done(v.scalar_tensor_tensor(b2[:, 0, :], b2[:, 1, :], shares[0:NP, 1:2], b2[:, 0, :], ALU.mult, ALU.add))
            o.settle()
            o.done(v.tensor_tensor(rows[:], rows[:], spread(b2[:, 0:1, :], NP, TN, D), ALU.add))
            o.settle()
            with dve.Fori(0, NB) as u:
                for j in range(TB):
                    t = u * TB + j
                    wait_alone(dve, s_y, t + 1)
                    v.tensor_tensor(row_of(rows, t), row_of(rows, t), ps_y[j % 2][0:NP, :], ALU.add).then_inc(s_yk, 1)
            dve.wait_ge(s_yk, TN)
            layer_norm_stats(o, rows, st, mean[:], rstd[:], tmp[:])
            inverse_std(2)
            with dve.Fori(0, NB) as u:
                o.enter(u, 3)
                for j in range(TB):
                    t = u * TB + j
                    last = v.tensor_scalar(xn[:, j, :], row_of(rows, t), mean[:, bass.ds(t, 1)], rstd[:, bass.ds(t, 1)],
                                           ALU.subtract, ALU.mult)
                o.done(last)
                o.settle()
                o.done(v.tensor_tensor(xn[:], xn[:], spread(gamma[:].unsqueeze(1), NP, TB, D), ALU.mult))
                o.settle()
                o.done(v.tensor_tensor(xn[:], xn[:], spread(beta[:].unsqueeze(1), NP, TB, D), ALU.add))
                o.settle()
                xs = k["x"][:, bass.ds(u * TB, TB), :]
                v.tensor_tensor(xs, xs, xn[:], ALU.add).then_inc(s_res, 1)
                wait_alone(dve, s_res, u + 1)
                o.leave(NB)

        @block.tensor
        def _(pe):
            mm = nc.tensor.matmul
            with pe.Fori(0, NB) as u:
                wait_alone(pe, s_xn, u + 1)
                for j, place in enumerate(tile_places(ps_T)):
                    for c in range(DC):
                        last = nc.tensor.transpose(place[:, c, :], xn[:, j, c * P:(c + 1) * P], k["ident"][0:NP, 0:NP])
                last.then_inc(s_xT, 1)
            pe.wait_ge(s_w, 16 * 4)
            pe.wait_ge(s_tot, 1)
            for c in range(DC):
                last = mm(ps_r[0:1, 0:E1], total[:, c:c + 1], wr[:, c, :], start=c == 0, stop=c == DC - 1)
            last.then_inc(s_log, 1)
            pe.wait_ge(s_tot, 2)
            mm(ps_r[:, E1:], k["one"][0:1, :], share[:], start=True, stop=True).then_inc(s_sh, 1)
            pe.wait_ge(s_ew, ALL_EW)
            pe.wait_ge(s_w2, TOPK)

            def first_product(u, f, first):
                for b, n in ((0, 3), (1, 2)):
                    if not (first and f == 0):
                        wait_alone(pe, s_hk, u * 2 * FF + f * 2 + b - 1)
                    for c in range(DC):
                        last = mm(ps_h[b][:, 0:n, :], w1[:, f // FC, c, f % FC * P:(f % FC + 1) * P],
                                  xT[:, bass.ds(u * TB + 3 * b, n), c, :], start=c == 0, stop=c == DC - 1)
                    last.then_inc(s_h, 1)

            def second_product(u, j, first):
                t = u * TB + j
                if not (first and j < 2):
                    wait_alone(pe, s_yk, t - 1 if j else t)
                for f in range(FF):
                    last = mm(ps_y[j % 2][0:NP, :], hT[:, f, j, :], w2[:, f // FC, f % FC, :], start=f == 0, stop=f == FF - 1)
                last.then_inc(s_y, 1)

            def step(u, first):
                for f in range(FF):
                    first_product(u, f, first)
                wait_alone(pe, s_hk, u * 2 * FF + 2 * FF)
                for j in range(TB):
                    second_product(u, j, first)

            step(0, True)
            with pe.Fori(1, NB) as u:
                step(u, False)


def build(nc, a, out):
    with ExitStack() as ctx:
        def keep(name, shape, dt=F32):
            return ctx.enter_context(nc.sbuf_tensor(f"keep_{name}", shape, dt))

        def dram(name, shape):
            return nc.dram_tensor(f"mid_{name}", shape, F32, kind="Internal").ap()

        k = {
            "x": keep("x", [NP, TN, D]),
            "iota": keep("iota", [P, P]),
            "ident": keep("ident", [P, P]),
            "before": keep("before", [P, P]),
            "one": keep("one", [P, P]),
            "eps5": keep("eps5", [P, 1]),
            "a_src": keep("a_src", [NP, TN, H]),
            "bin0": keep("bin0", [1, G0_N + 8], I32),
            "record1": keep("record1", [NP, EC, 2]),
            "row1": keep("row1", [NP, EC], I32),
            "bin1": keep("bin1", [1, G1_N], I32),
            "pairs": keep("pairs", [NP, TOPK * TN], I32),
            "gate": keep("gate", [NP, TOPK, TN]),
            "expert_of": keep("expert_of", [1, X_N + 2], I32),
            "b1T": keep("b1T", [P, E0 * F0 // P]),
            "sorted0": dram("sorted0", [P * G0_TILES, 4]),
            "sorted1": dram("sorted1", [P * G1_N, 2]),
            "expert_in": dram("expert_in", [X_N * P, D]),
            "expert_out": dram("expert_out", [X_N * P, D]),
            "table1": dram("table1", [B1 * G1_BINS, ROW]),
            "score1": dram("score1", [B1 * G1_BINS, 2 * H]),
            "attended1": dram("attended1", [B1 * G1_BINS, D]),
            "table": dram("table", [NN, ROW]),
        }
        stage_project0(nc, a, k)
        with nc.sbuf_tensor("acc0", [NP, TN, ROW], F32) as k["acc0"]:
            k["normed"] = k["acc0"][:, :, 0:D]
            with nc.sbuf_tensor("w1", [P, E0, DC, F0], F32) as k["w1"]:
                stage_edges0(nc, a, k)
                stage_gate(nc, a, k)
                stage_experts(nc, a, k)
            stage_combine(nc, a, k)
            stage_project1(nc, a, k)
        stage_edges1(nc, a, k)
        stage_ffn1(nc, a, k, out)




INPUTS = ['x', 'src', 'dst', 'edge_weight', 'L0_gnn_Ws', 'L0_gnn_bs', 'L0_gnn_aw', 'L0_gnn_ab', 'L0_mix_W_qkv',
          'L0_mix_b_qkv', 'L0_mix_W_out', 'L0_mix_b_out', 'L0_ffn_gate_w', 'L0_ffn_gate_b', 'L0_ffn_w1', 'L0_ffn_b1',
          'L0_ffn_w2', 'L0_ffn_b2', 'L0_ffn_gamma', 'L0_ffn_beta', 'L1_gnn_W', 'L1_gnn_att_src', 'L1_gnn_att_dst',
          'L1_gnn_bias', 'L1_mix_w_norm1', 'L1_mix_w_qkv', 'L1_mix_w_out', 'L1_mix_b_out', 'L1_mix_w_norm2', 'L1_ffn_Wr',
          'L1_ffn_br', 'L1_ffn_W1', 'L1_ffn_b1', 'L1_ffn_W2', 'L1_ffn_b2', 'L1_ffn_gamma', 'L1_ffn_beta']


def kernel(**inputs):
    import concourse.bacc as bacc
    import numpy as np
    from concourse import mybir as _mybir
    from concourse.bass_utils import run_bass_kernel_spmd

    nc = bacc.Bacc("TRN2", target_bir_lowering=False, num_devices=1)
    arrays, a = {}, {}
    for name in INPUTS:
        value = np.ascontiguousarray(inputs[name])
        arrays[f"in_{name}"] = value
        a[name] = nc.dram_tensor(f"in_{name}", value.shape, _mybir.dt.from_np(value.dtype), kind="ExternalInput").ap()
    out = nc.dram_tensor("out", (NN, D), _mybir.dt.from_np(np.dtype("float32")), kind="ExternalOutput").ap()
    build(nc, a, out)
    return run_bass_kernel_spmd(nc, [arrays], core_ids=[0]).results[0]["out"]
```

```python
from contextlib import ExitStack

import concourse.bass as bass
from concourse import mybir

F32 = mybir.dt.float32
I32 = mybir.dt.int32
U32 = mybir.dt.uint32
BF16 = mybir.dt.bfloat16
ALU = mybir.AluOpType
ACT = mybir.ActivationFunctionType
AX = mybir.AxisListType.X

P = 128
NN = 3125
NP = 125
TN = 25
D = 256
DC = D // P
H = 4
HD = D // H
NE = 50000
EC = NE // NP
ROW = D + H
G0_SIZE = 2 * P
G0_BINS = TN
G0_N = (NE + G0_BINS * (G0_SIZE - 1)) // G0_SIZE
G0_N += -G0_N % 8
G0_TILES = 2 * G0_N
B1 = 32
G1_BINS = -(-NN // B1)
G1_N = (NE + G1_BINS * (P - 1)) // P
G1_N += -G1_N % 8
W1 = HD + 1
ROW1 = H * W1 + H
TB = 5
NB = TN // TB
R1 = 4
assert R1 * TN >= G1_BINS
SCATTERS = EC // 16
SCATTERS_EARLY = 17
E0 = 16
F0 = 512
TOPK = 2
X_N = (NN * TOPK + E0 * (P - 1)) // P
X_N += -X_N % 4
E1 = 8
MAGIC = 12582912.0
LN_EPS = 1e-5


class Order:

    def __init__(self, eng, sem):
        self.eng, self.sem, self.n, self.off = eng, sem, 0, None

    def done(self, ins):
        ins.then_inc(self.sem, 1)
        self.n += 1
        return ins

    def value(self):
        return self.n if self.off is None else self.off + self.n

    def settle(self):
        self.eng.wait_ge(self.sem, self.value())

    def settle_alone(self):
        wait_alone(self.eng, self.sem, self.value())

    def enter(self, i, per):
        self.start, self.per, self.off = self.n, per, i * per

    def leave(self, count):
        assert self.n - self.start == self.per, (self.n - self.start, self.per)
        self.n, self.off = self.start + self.per * count, None


def wait_alone(eng, sem, value):
    eng.wait_ge(sem, value)
    eng.nop(nofuse=True)


def spread(ap, *shape):
    return ap.to_broadcast(list(shape))


def rank_count_bins(o, bins, cnt, junk, iota, b, n):
    o.settle_alone()
    for j in range(n):
        o.done(o.eng.tensor_scalar(junk[:, j], bins, iota[0:NP, bass.ds(b + j, 1)], 0.0, ALU.is_equal, ALU.add,
                                   accum_out=cnt[:, bass.ds(b + j, 1)]))


def rank_bases(o, first, total, prefix, groups, start, one, size, nbins):
    o.done(o.eng.tensor_scalar(groups, total, (size - 1) / 2.0, 1.0 / size, ALU.add, ALU.mult))
    o.settle()
    o.done(o.eng.tensor_scalar(groups, groups, MAGIC, MAGIC, ALU.add, ALU.subtract))
    o.settle()
    o.done(o.eng.tensor_tensor_scan(start, one[0:NP, 0:nbins], groups, 0.0, ALU.mult, ALU.add))
    o.settle()
    o.done(o.eng.tensor_tensor(start, start, groups, ALU.subtract))
    o.settle()
    o.done(o.eng.tensor_scalar(first, start, float(size), -1.0, ALU.mult, ALU.add))
    o.settle()
    o.done(o.eng.tensor_tensor(first, first, prefix, ALU.add))
    o.settle()


def rank_slots_bins(o, slot, bins, first, masks, runnings, one, iota, b, n):
    o.settle_alone()
    for j in range(n):
        o.done(o.eng.tensor_scalar(masks[:, j], bins, iota[0:NP, bass.ds(b + j, 1)], None, ALU.is_equal))
    o.settle_alone()
    for j in range(n):
        o.done(o.eng.tensor_tensor_scan(runnings[:, j], one, masks[:, j], first[:, bass.ds(b + j, 1)], ALU.mult, ALU.add))
    for j in range(n):
        o.settle_alone()
        o.done(o.eng.copy_predicated(slot, masks[:, j].bitcast(mybir.dt.uint16), runnings[:, j]))


def group_bins(o, bin_of, column, reached, ps_column, ps_row, iota_groups, nbins, ngroups, s_col, s_row, done):
    o.eng.sem_inc(s_col, 1)
    o.eng.wait_ge(s_row, 2 * done + 1)
    o.done(o.eng.tensor_copy(column[0:nbins, :], ps_column[0:nbins, 0:1]))
    o.settle()
    o.eng.tensor_scalar(reached[0:nbins, 0:ngroups], iota_groups[0:nbins, 0:ngroups], column[0:nbins, :], None,
                        ALU.is_ge).then_inc(s_col, 1)
    o.eng.wait_ge(s_row, 2 * done + 2)
    o.done(o.eng.tensor_scalar(bin_of, ps_row[0:1, 0:ngroups], 1.0, None, ALU.subtract))


def turn_starts(nc, pe, start, ps_column, ps_row, reached, ident, one, nbins, ngroups, s_col, s_row, done):
    pe.wait_ge(s_col, 2 * done + 1)
    nc.tensor.transpose(ps_column[0:nbins, 0:NP], start[0:NP, 0:nbins], ident[0:NP, 0:NP]).then_inc(s_row, 1)
    pe.wait_ge(s_col, 2 * done + 2)
    nc.tensor.matmul(ps_row[0:1, 0:ngroups], one[0:nbins, 0:1], reached[0:nbins, 0:ngroups], start=True, stop=True).then_inc(s_row, 1)


def split_index(o, whole, rest, key, size):
    o.done(o.eng.tensor_scalar(whole, key, -(size - 1) / 2.0, 1.0 / size, ALU.add, ALU.mult))
    o.settle()
    o.done(o.eng.tensor_scalar(whole, whole, MAGIC, MAGIC, ALU.add, ALU.subtract))
    o.settle()
    o.done(o.eng.scalar_tensor_tensor(rest, whole, -float(size), key, ALU.mult, ALU.add))
    o.settle()


def sorted_rows(o, row, tile, lane, slot, tiles):
    split_index(o, tile, lane, slot, P)
    o.done(o.eng.scalar_tensor_tensor(row, lane, float(tiles), tile, ALU.mult, ALU.add))
    o.settle()


def over_tiles(o, step):
    with o.eng.Fori(0, NB) as u:
        o.enter(u, TB)
        for j in range(TB):
            o.done(step(u * TB + j))
        o.leave(NB)


def layer_norm_stats(o, x, st, mean, rstd, tmp):
    over_tiles(o, lambda t: o.eng.bn_stats(st[:, bass.ds(t, 1), :], x[:, bass.ds(t, 1), :].rearrange("p a d -> p (a d)")))
    turn_stats(o, st, mean, rstd, tmp)


def turn_stats(o, st, mean, rstd, tmp):
    o.settle()
    o.done(o.eng.tensor_tensor(mean, st[:, :, 1], st[:, :, 4], ALU.add))
    o.done(o.eng.tensor_tensor(tmp, st[:, :, 1], st[:, :, 4], ALU.subtract))
    o.done(o.eng.tensor_tensor(rstd, st[:, :, 2], st[:, :, 5], ALU.add))
    o.settle()
    o.done(o.eng.tensor_scalar(mean, mean, 0.5, None, ALU.mult))
    o.done(o.eng.tensor_tensor(tmp, tmp, tmp, ALU.mult))
    o.done(o.eng.tensor_scalar(rstd, rstd, 1.0 / D, None, ALU.mult))
    o.settle()
    o.done(o.eng.scalar_tensor_tensor(rstd, tmp, 0.25, rstd, ALU.mult, ALU.add))
    o.settle()


def load_weight(eng, dst, src, sem):
    eng.dma_start(dst, src.rearrange("(c p) n -> p c n", p=P)).then_inc(sem, 16)


def tile_places(ps):
    return [ps[:, j // 2, j % 2 * DC * NP:(j % 2 + 1) * DC * NP].rearrange("p (c n) -> p c n", c=DC) for j in range(TB)]


def keep_transposed(act, sem, xT, ps):
    flat = xT.rearrange("p t c n -> p (t c n)")
    act.activation(flat[:, 0:4 * DC * NP].rearrange("p (b n) -> p b n", b=2), ps[:, 0:2, 0:2 * DC * NP], ACT.Copy)
    act.activation(flat[:, 4 * DC * NP:], ps[:, 2, 0:DC * NP], ACT.Copy).then_inc(sem, 1)


def scatter_records(nc, pool, to, row, record, stage_row, stage_rec, s_stage, s_scat, begin, end):
    def scatter(half, i, staged):
        at = i * 16 + half * 8
        nc.gpsimd.tensor_copy(stage_row[:, half, :], row[:, bass.ds(at, 8)]).then_inc(s_stage, 1)
        nc.gpsimd.tensor_copy(stage_rec[:, half], record[:, bass.ds(at, 8), :]).then_inc(s_stage, 1)
        wait_alone(pool, s_stage, staged + 2 * half + 2)
        for j in range(8):
            pool.indirect_dma_start(
                out=to, out_offset=bass.IndirectOffsetOnAxis(ap=stage_row[:, half, j:j + 1].bitcast(U32), axis=0),
                in_=stage_rec[:, half, j, :], in_offset=None).then_inc(s_scat[half], 16)

    for half in range(2):
        scatter(half, begin, 0)
    with pool.Fori(1, end - begin) as i:
        for half in range(2):
            wait_alone(pool, s_scat[half], i * 128)
            scatter(half, i + begin, i * 4)
    for half in range(2):
        pool.wait_ge(s_scat[half], 128 * (end - begin))


class Memory:

    def __init__(self, nc, ctx, stage):
        self.nc, self.ctx, self.stage, self.sems = nc, ctx, stage, []
        ctx.callback(self.release_semaphores)

    def release_semaphores(self):
        self.nc.clear_and_free_semaphores(self.sems)
        self.nc.all_engine_barrier(sem_only=True)

    def sb(self, name, shape, dt=F32):
        return self.ctx.enter_context(self.nc.sbuf_tensor(f"{self.stage}_{name}", shape, dt))

    def ps(self, name, shape, dt=F32):
        bank = self.ctx.enter_context(self.nc.psum_tensor(f"{self.stage}_{name}", [P, 512], dt))
        size = 1
        for n in shape[1:]:
            size *= n
        flat = bank[0:shape[0], 0:size]
        return flat if len(shape) == 2 else flat.rearrange("p (a b) -> p a b", a=shape[1])

    def banks(self, name, n, dt=F32):
        return self.ctx.enter_context(self.nc.psum_tensor(f"{self.stage}_{name}", [P, n, 512], dt))

    def sem(self, name):
        self.sems.append(self.nc.alloc_semaphore(f"{self.stage}_{name}"))
        return self.sems[-1]


def stage_project0(nc, a, k):
    with ExitStack() as ctx:
        m = Memory(nc, ctx, "p0")
        RB = 5
        assert G0_BINS % RB == 0
        src = m.sb("src", [NP, EC], I32)
        dst = m.sb("dst", [NP, EC], I32)
        wgt = m.sb("wgt", [NP, EC])
        key = m.sb("key", [NP, EC])
        whole = m.sb("whole", [NP, EC])
        rest = m.sb("rest", [NP, EC])
        slot = m.sb("slot", [NP, EC])
        mask = m.sb("mask", [NP, RB, EC], BF16)
        running = m.sb("running", [NP, RB, EC])
        ones = m.sb("ones", [NP, EC])
        iota_g = m.sb("iota_g", [P, G1_N])
        reached = m.sb("reached", [P, G1_N])
        column = m.sb("column", [P, 1])
        bin_of0 = m.sb("bin_of0", [NP, EC], BF16)
        bin_of1 = m.sb("bin_of1", [NP, EC], BF16)
        record0 = m.sb("record0", [NP, EC, 4])
        row0 = m.sb("row0", [NP, EC], I32)
        cnt = m.sb("cnt", [NP, P])
        prefix = m.sb("prefix", [NP, P])
        total = m.sb("total", [NP, P])
        groups = m.sb("groups", [NP, P])
        start = m.sb("start", [NP, P])
        first = m.sb("first", [NP, P])
        pad = m.sb("pad", [P, 4 * G0_TILES])
        pad1 = m.sb("pad1", [P, 2 * G1_N])
        zrow = m.sb("zrow", [P, D])
        stage_row = m.sb("stage_row", [NP, 2, 8], I32)
        stage_rec = m.sb("stage_rec", [NP, 2, 8, 4])
        st = m.sb("st", [NP, TN, 6])
        mean = m.sb("mean", [NP, TN])
        rstd = m.sb("rstd", [NP, TN])
        tmp = m.sb("tmp", [NP, TN])
        w = m.sb("w", [P, DC, 4 * D])
        wa = m.sb("wa", [P, DC, 2, H])
        wprod = m.sb("wprod", [P, D])
        awb = m.sb("awb", [P, H, 2 * HD + 1])
        bias = m.sb("bias", [NP, 4 * D])
        biasa = m.sb("biasa", [NP, 2, H])
        wout = m.sb("wout", [P, DC, D])
        bout = m.sb("bout", [NP, D])
        xn = m.sb("xn", [NP, D])
        xT = m.sb("xT", [P, DC, NP])
        qk = m.sb("qk", [NP, 2, D])
        qkc = m.sb("qkc", [NP, 2, D])
        sums = m.sb("sums", [NP, 2])
        ksum = m.sb("ksum", [NP, 1])
        k2 = m.sb("k2", [NP, D])
        k4 = m.sb("k4", [NP, D])
        q4 = m.sb("q4", [NP, D])
        qsum = m.sb("qsum", [NP, TN])
        q4sum = m.sb("q4sum", [NP, TN])
        q2 = m.sb("q2", [NP, TN, D])
        v = m.sb("v", [NP, TN, D])
        feat = m.sb("feat", [NP, ROW])
        kv = m.sb("kv", [P, DC, D])
        kvT = m.sb("kvT", [P, DC, D])
        kw = m.sb("kw", [P, DC, D])
        cnorm = m.sb("cnorm", [P, DC])
        qv = m.sb("qv", [NP, 2, D])
        qvT = m.sb("qvT", [P, 4, NP])
        part = m.sb("part", [NP, D])

        ps_rank = m.ps("ps_rank", [P, 2, P])
        ps_T = m.ps("ps_T", [P, 4, P])
        ps_qk = m.ps("ps_qk", [P, 2 * D])
        ps_vf = m.ps("ps_vf", [P, 2 * D])
        ps_a = m.ps("ps_a", [P, 2, H])
        ps_kv = m.ps("ps_kv", [P, DC, D])
        ps_cn = m.ps("ps_cn", [P, DC, 2])
        ps_mix = m.ps("ps_mix", [P, 2, D])

        s_const = m.sem("const")
        s_x = m.sem("x")
        s_edges = m.sem("edges")
        s_w = m.sem("weights")
        s_pad = m.sem("pad_tile")
        s_fill = m.sem("filled")
        s_cnt = m.sem("counted")
        s_base = m.sem("bases")
        s_col = m.sem("bin_starts")
        s_row = m.sem("bin_starts_turned")
        s_rows = m.sem("rows_known")
        s_stage = m.sem("staged")
        s_scat = [m.sem(f"scattered{i}") for i in range(2)]
        s_var = m.sem("variance")
        s_std = m.sem("std")
        s_xn = m.sem("normed")
        s_xT = m.sem("xT_made")
        s_xTs = m.sem("xT_kept")
        s_proj = m.sem("projected")
        s_evac = m.sem("projections_kept")
        s_sum = m.sem("qk_summed")
        s_cen = m.sem("negative_means")
        s_sq = m.sem("squared")
        s_k2 = m.sem("k2_ready")
        s_k4 = m.sem("k4_ready")
        s_kv = m.sem("kv_added")
        s_feat = m.sem("feature_row")
        s_tab = m.sem("table_written")
        s_kvd = m.sem("kv_done")
        s_kvs = m.sem("kv_kept")
        s_cn = m.sem("column_norms")
        s_kvT = m.sem("kvT_made")
        s_kvTs = m.sem("kvT_kept")
        s_kw = m.sem("kw_made")
        s_kws = m.sem("kw_kept")
        s_qn = m.sem("q_norm_square")
        s_qr = m.sem("q_norm")
        s_qv = m.sem("qv_staged")
        s_qvT = m.sem("qvT_made")
        s_qvTs = m.sem("qvT_kept")
        s_mix = m.sem("mixed")
        s_mixd = m.sem("mix_kept")
        s_v = m.sem("vector_steps")
        s_a = m.sem("scalar_steps")
        block = ctx.enter_context(nc.Block())

        @block.sync
        def _(sp):
            for t, s in ((src, a["src"]), (dst, a["dst"]), (wgt, a["edge_weight"])):
                sp.dma_start(t[:], s.rearrange("(p c) -> p c", p=NP)).then_inc(s_edges, 16)
            sp.dma_start(k["x"][:], a["x"].rearrange("(p t) d -> p t d", p=NP)).then_inc(s_x, 16)
            load_weight(sp, w[:, :, 0:3 * D], a["L0_mix_W_qkv"], s_w)
            for h in range(H):
                load_weight(sp, w[:, :, 3 * D + h * HD:3 * D + (h + 1) * HD], a["L0_gnn_Ws"][h], s_w)
            load_weight(sp, wout[:], a["L0_mix_W_out"], s_w)
            sp.dma_start(bias[:, 0:3 * D], a["L0_mix_b_qkv"].partition_broadcast(NP)).then_inc(s_w, 16)
            sp.dma_start(bias[:, 3 * D:], a["L0_gnn_bs"].rearrange("h o -> (h o)").partition_broadcast(NP)).then_inc(s_w, 16)
            sp.dma_start(bout[:], a["L0_mix_b_out"].partition_broadcast(NP)).then_inc(s_w, 16)
            sp.dma_start(awb[:].rearrange("p h o -> p (h o)"),
                         a["L0_gnn_aw"].rearrange("h o -> (h o)").partition_broadcast(P)).then_inc(s_w, 16)
            sp.wait_ge(s_pad, 3)
            sp.dma_start(k["sorted0"].rearrange("(p t) f -> p (t f)", p=P), pad[:]).then_inc(s_fill, 16)
            sp.dma_start(k["expert_in"].rearrange("(t p) d -> p t d", p=P),
                         spread(zrow[:].unsqueeze(1), P, X_N, D)).then_inc(s_fill, 16)
            sp.dma_start(k["sorted1"].rearrange("(p t) f -> p (t f)", p=P), pad1[:]).then_inc(s_fill, 16)
            sp.sem_inc(s_tab, 16)
            with sp.Fori(0, TN) as t:
                sp.wait_ge(s_feat, t + 1)
                sp.dma_start(k["table"].rearrange("(p t) d -> p t d", p=NP)[:, bass.ds(t, 1), :],
                             feat[:].unsqueeze(1)).then_inc(s_tab, 16)
            sp.wait_ge(s_tab, 16 * TN + 16)
            sp.wait_ge(s_fill, 48)

        @block.gpsimd
        def _(pool):
            nc.gpsimd.iota(k["iota"][:], [[1, P]], base=0, channel_multiplier=0,
                           allow_small_or_imprecise_dtypes=True).then_inc(s_const, 1)
            nc.gpsimd.iota(iota_g[:], [[1, G1_N]], base=0, channel_multiplier=0,
                           allow_small_or_imprecise_dtypes=True).then_inc(s_const, 1)
            nc.gpsimd.iota(k["number"][:], [[0, 1]], base=0, channel_multiplier=1,
                           allow_small_or_imprecise_dtypes=True).then_inc(s_const, 1)
            nc.gpsimd.memset(k["ident"][:], 0.0).then_inc(s_const, 1)
            nc.gpsimd.memset(k["before"][:], 1.0).then_inc(s_const, 1)
            nc.gpsimd.memset(k["one"][:], 1.0).then_inc(s_const, 1)
            pool.wait_ge(s_const, 6)
            nc.gpsimd.affine_select(out=k["ident"][:], in_=k["ident"][:], compare_op=ALU.not_equal, fill=1.0, base=0,
                                    pattern=[[-1, P]], channel_multiplier=1).then_inc(s_const, 1)
            nc.gpsimd.affine_select(out=k["before"][:], in_=k["before"][:], compare_op=ALU.is_ge, fill=0.0, base=-1,
                                    pattern=[[1, P]], channel_multiplier=-1).then_inc(s_const, 1)
            nc.gpsimd.memset(zrow[:], 0.0).then_inc(s_pad, 1)
            pool.wait_ge(s_rows, 1)
            pool.wait_ge(s_fill, 48)
            scatter_records(nc, pool, k["sorted0"], row0, record0, stage_row, stage_rec, s_stage, s_scat, 0, SCATTERS)

        @block.scalar
        def _(act):
            o = Order(act, s_a)
            act.wait_ge(s_var, 1)
            nc.scalar.activation(rstd[:], rstd[:], ACT.Sqrt, bias=k["eps5"][0:NP, :]).then_inc(s_std, 1)
            def keep_xT(t):
                wait_alone(act, s_xT, t + 1)
                nc.scalar.activation(xT[:], ps_T[:, 0:DC, 0:NP], ACT.Copy).then_inc(s_xTs, 1)

            def step(t, last):
                if not last:
                    keep_xT(t + 1)
                o.enter(t, 3) if not last else None
                q2t = q2[:, bass.ds(t, 1), :].rearrange("p a d -> p (a d)")
                wait_alone(act, s_evac, t + 1)
                for j in range(2):
                    nc.scalar.activation(qkc[:, j, :], qk[:, j, :], ACT.Copy, accum_out=sums[:, j:j + 1]).then_inc(s_sum, 1)
                wait_alone(act, s_cen, t + 1)
                wait_alone(act, s_kv, t + 1)
                o.done(nc.scalar.activation(q2t, qk[:, 0, :], ACT.Square, bias=sums[:, 0:1], accum_out=qsum[:, bass.ds(t, 1)]))
                o.done(nc.scalar.activation(k2[:], qk[:, 1, :], ACT.Square, bias=sums[:, 1:2], accum_out=ksum[:]))
                o.settle_alone()
                act.sem_inc(s_sq, 1)
                o.done(nc.scalar.activation(q4[:], q2t, ACT.Square, accum_out=q4sum[:, bass.ds(t, 1)]))
                wait_alone(act, s_k2, t + 1)
                nc.scalar.activation(k4[:], k2[:], ACT.Square).then_inc(s_k4, 1)
                o.leave(TN - 1) if not last else None

            keep_xT(0)
            with act.Fori(0, TN - 1) as t:
                step(t, False)
            step(TN - 1, True)
            o.settle()
            act.sem_inc(s_sq, 1)
            act.wait_ge(s_kvd, 1)
            nc.scalar.activation(cnorm[:], ps_cn[:, :, 0], ACT.Sqrt).then_inc(s_cn, 1)
            act.wait_ge(s_qn, 1)
            nc.scalar.activation(q4sum[:], q4sum[:], ACT.Sqrt).then_inc(s_qr, 1)
            act.wait_ge(s_kvT, 1)
            nc.scalar.activation(kvT[:].rearrange("p a d -> p (a d)"), ps_T[:].rearrange("p a d -> p (a d)"), ACT.Copy).then_inc(s_kvTs, 1)
            act.wait_ge(s_kw, 1)
            nc.scalar.activation(kw[:], ps_mix[:], ACT.Copy).then_inc(s_kws, 1)
            def stage(t):
                for j, rows in enumerate((q2, v)):
                    last = nc.scalar.activation(qv[:, j, :], rows[:, bass.ds(t, 1), :].rearrange("p a d -> p (a d)"), ACT.Copy)
                last.then_inc(s_qv, 1)

            def keep_qvT(t):
                wait_alone(act, s_qvT, t + 1)
                wait_alone(act, s_mix, t + 1)
                nc.scalar.activation(qvT[:], ps_T[:, :, 0:NP], ACT.Copy).then_inc(s_qvTs, 1)

            act.wait_ge(s_k4, TN)
            stage(0)
            with act.Fori(0, TN - 1) as t:
                keep_qvT(t)
                stage(t + 1)
            keep_qvT(TN - 1)

        @block.vector
        def _(dve):
            o = Order(dve, s_v)
            o.done(nc.vector.memset(pad[:], 0.0))
            o.done(nc.vector.memset(pad1[:], float(NN)))
            o.settle()
            for tile, fields in ((pad, 4), (pad1, 2)):
                nc.vector.memset(tile[:].rearrange("p (t f) -> p t f", f=fields)[:, :, 1:2], -1.0).then_inc(s_pad, 1)
            o.done(nc.vector.memset(k["eps5"][:], LN_EPS))
            o.done(nc.vector.memset(ones[:], 1.0))
            dve.wait_ge(s_edges, 48)
            dve.wait_ge(s_const, 8)
            o.done(nc.vector.tensor_copy(key[:], src[:]))
            o.done(nc.vector.memset(record0[:], 0.0))
            o.settle()
            split_index(o, whole[:], rest[:], key[:], TN)
            o.done(nc.vector.tensor_copy(bin_of0[:], rest[:]))
            o.done(nc.vector.tensor_copy(record0[:, :, 0], dst[:]))
            o.done(nc.vector.tensor_copy(record0[:, :, 1], whole[:]))
            o.done(nc.vector.tensor_copy(record0[:, :, 2], wgt[:]))
            with dve.Fori(0, G0_BINS // RB) as b:
                o.enter(b, RB)
                rank_count_bins(o, bin_of0[:], cnt, mask, k["iota"], b * RB, RB)
                o.leave(G0_BINS // RB)
            o.settle()
            dve.sem_inc(s_cnt, 1)
            dve.wait_ge(s_base, 1)
            o.done(nc.vector.tensor_copy(prefix[:, 0:G0_BINS], ps_rank[0:NP, 0, 0:G0_BINS]))
            o.done(nc.vector.tensor_copy(total[:, 0:G0_BINS], ps_rank[0:NP, 1, 0:G0_BINS]))
            o.settle()
            rank_bases(o, first[:, 0:G0_BINS], total[:, 0:G0_BINS], prefix[:, 0:G0_BINS], groups[:, 0:G0_BINS],
                       start[:, 0:G0_BINS], k["one"], G0_SIZE, G0_BINS)
            with dve.Fori(0, G0_BINS // RB) as b:
                o.enter(b, 3 * RB)
                rank_slots_bins(o, slot[:], bin_of0[:], first, mask, running, ones[:], k["iota"], b * RB, RB)
                o.leave(G0_BINS // RB)
            o.settle()
            sorted_rows(o, running[:, 0], whole[:], rest[:], slot[:], G0_TILES)
            nc.vector.tensor_copy(row0[:], running[:, 0]).then_inc(s_rows, 1)
            group_bins(o, k["bin0"][:], column, reached, ps_vf, ps_qk, iota_g, G0_BINS, G0_N + 8, s_col, s_row, 0)

            o.done(nc.vector.tensor_copy(key[:], dst[:]))
            o.done(nc.vector.memset(k["record1"][:], 0.0))
            o.done(nc.vector.memset(cnt[:], 0.0))
            o.settle()
            split_index(o, rest[:], whole[:], key[:], G1_BINS)
            o.done(nc.vector.tensor_copy(bin_of1[:], whole[:]))
            o.done(nc.vector.tensor_copy(k["record1"][:, :, 0], src[:]))
            o.done(nc.vector.tensor_copy(k["record1"][:, :, 1], rest[:]))
            dve.wait_ge(s_x, 16)
            layer_norm_stats(o, k["x"], st, mean[:], rstd[:], tmp[:])
            dve.sem_inc(s_var, 1)
            dve.wait_ge(s_std, 1)
            o.done(nc.vector.reciprocal(rstd[:], rstd[:]))
            dve.wait_ge(s_w, 16 * 10)
            for c in range(DC):
                for j in range(2):
                    o.settle()
                    o.done(nc.vector.tensor_tensor(wprod[:].rearrange("p (h o) -> p h o", h=H),
                                                   w[:, c, 3 * D:].rearrange("p (h o) -> p h o", h=H),
                                                   awb[:, :, j * HD:(j + 1) * HD], ALU.mult))
                    o.settle()
                    o.done(nc.vector.tensor_reduce(wa[:, c, j, :], wprod[:].rearrange("p (h o) -> p h o", h=H),
                                                   AX, ALU.add))
            for j in range(2):
                o.settle()
                o.done(nc.vector.tensor_tensor(wprod[0:NP].rearrange("p (h o) -> p h o", h=H),
                                               bias[:, 3 * D:].rearrange("p (h o) -> p h o", h=H),
                                               awb[0:NP, :, j * HD:(j + 1) * HD], ALU.mult))
                o.settle()
                o.done(nc.vector.tensor_reduce(biasa[:, j, :], wprod[0:NP].rearrange("p (h o) -> p h o", h=H),
                                               AX, ALU.add))
            o.settle()

            def row_of(t3, t):
                return t3[:, bass.ds(t, 1), :].rearrange("p a d -> p (a d)")

            def norm(t):
                nc.vector.tensor_scalar(xn[:], k["x"][:, bass.ds(t, 1), :].rearrange("p a d -> p (a d)"), mean[:, bass.ds(t, 1)],
                                        rstd[:, bass.ds(t, 1)], ALU.subtract, ALU.mult).then_inc(s_xn, 1)

            def step(t, norm_ahead):
                o.enter(t, 3 + R1) if not isinstance(t, int) else None
                wait_alone(dve, s_proj, t + 1)
                nc.vector.tensor_tensor(qk[:].rearrange("p a d -> p (a d)"), ps_qk[0:NP, :], bias[:, 0:2 * D], ALU.add).then_inc(s_evac, 1)
                nc.vector.tensor_tensor(row_of(v, t), ps_vf[0:NP, 0:D], bias[:, 2 * D:3 * D], ALU.add)
                nc.vector.tensor_tensor(k["a_src"][:, bass.ds(t, 1), :].rearrange("p a h -> p (a h)"), ps_a[0:NP, 0, :],
                                        biasa[:, 0, :], ALU.add)
                wait_alone(dve, s_tab, t * 16 + 16)
                o.done(nc.vector.tensor_tensor(feat[:, D:], ps_a[0:NP, 1, :], biasa[:, 1, :], ALU.add))
                nc.vector.tensor_tensor(feat[:, 0:D], ps_vf[0:NP, D:], bias[:, 3 * D:], ALU.add).then_inc(s_feat, 1)
                if norm_ahead:
                    wait_alone(dve, s_xT, t + 2)
                    norm(t + 2)
                rank_count_bins(o, bin_of1[:], cnt, mask, k["iota"], t * R1, R1)
                wait_alone(dve, s_sum, t * 2 + 2)
                nc.vector.tensor_scalar(sums[:], sums[:], -1.0 / D, None, ALU.mult).then_inc(s_cen, 1)
                wait_alone(dve, s_sq, t + 1)
                o.done(nc.vector.tensor_scalar(ksum[:], ksum[:], 1e-7, None, ALU.add))
                o.settle()
                o.done(nc.vector.reciprocal(ksum[:], ksum[:]))
                o.settle()
                nc.vector.tensor_scalar(k2[:], k2[:], ksum[:], None, ALU.mult).then_inc(s_k2, 1)
                o.leave(TN - 2) if not isinstance(t, int) else None

            norm(0)
            dve.wait_ge(s_xT, 1)
            norm(1)
            with dve.Fori(0, TN - 2) as t:
                step(t, True)
            for t in range(TN - 2, TN):
                step(t, False)
            o.settle()
            dve.sem_inc(s_cnt, 1)
            dve.wait_ge(s_base, 2)
            o.done(nc.vector.tensor_copy(prefix[:], ps_rank[0:NP, 0, :]))
            o.done(nc.vector.tensor_copy(total[:], ps_rank[0:NP, 1, :]))
            o.settle()
            rank_bases(o, first[:], total[:], prefix[:], groups[:], start[:], k["one"], P, P)
            group_bins(o, k["bin1"][:], column, reached, ps_vf, ps_qk, iota_g, G1_BINS, G1_N, s_col, s_row, 1)
            dve.wait_ge(s_cn, 1)
            o.done(nc.vector.tensor_scalar(cnorm[:], cnorm[:], 1e-12, None, ALU.max))
            o.settle()
            o.done(nc.vector.reciprocal(cnorm[:], cnorm[:]))
            o.settle()
            for c in range(DC):
                nc.vector.tensor_scalar(kv[:, c, :], ps_kv[:, c, :], cnorm[:, c:c + 1], float(NN) ** -0.5,
                                        ALU.mult, ALU.mult).then_inc(s_kvs, 1)
            dve.wait_ge(s_sq, TN + 1)
            o.done(nc.vector.tensor_scalar(qsum[:], qsum[:], 1e-7, None, ALU.add))
            o.settle()
            o.done(nc.vector.reciprocal(qsum[:], qsum[:]))
            o.settle()
            o.done(nc.vector.tensor_tensor(tmp[:], qsum[:], qsum[:], ALU.mult))
            o.settle()
            nc.vector.tensor_tensor(q4sum[:], q4sum[:], tmp[:], ALU.mult).then_inc(s_qn, 1)
            dve.wait_ge(s_qr, 1)
            o.done(nc.vector.tensor_scalar(q4sum[:], q4sum[:], 1e-12, None, ALU.max))
            o.settle()
            o.done(nc.vector.reciprocal(q4sum[:], q4sum[:]))
            o.settle()
            o.done(nc.vector.tensor_tensor(qsum[:], qsum[:], q4sum[:], ALU.mult))
            o.settle()
            dve.sem_inc(s_mixd, 1)
            with dve.Fori(0, TN) as t:
                o.enter(t, 2 + 3 * R1)
                xt = k["x"][:, bass.ds(t, 1), :].rearrange("p a d -> p (a d)")
                wait_alone(dve, s_mix, t + 2)
                o.done(nc.vector.tensor_tensor(part[:], ps_mix[0:NP, 1, :], bout[:], ALU.add))
                o.settle()
                o.done(nc.vector.scalar_tensor_tensor(part[:], ps_mix[0:NP, 0, :], qsum[:, bass.ds(t, 1)], part[:], ALU.mult, ALU.add))
                o.settle()
                nc.vector.tensor_tensor(xt, xt, part[:], ALU.add).then_inc(s_mixd, 1)
                rank_slots_bins(o, slot[:], bin_of1[:], first, mask, running, ones[:], k["iota"], t * R1, R1)
                o.leave(TN)
            o.settle()
            sorted_rows(o, running[:, 0], whole[:], rest[:], slot[:], G1_N)
            o.done(nc.vector.tensor_copy(k["row1"][:], running[:, 0]))

        @block.tensor
        def _(pe):
            mm = nc.tensor.matmul
            pe.wait_ge(s_const, 8)
            pe.wait_ge(s_cnt, 1)
            mm(ps_rank[0:NP, 0, 0:G0_BINS], k["before"][0:NP, 0:NP], cnt[:, 0:G0_BINS], start=True, stop=True)
            mm(ps_rank[0:NP, 1, 0:G0_BINS], k["one"][0:NP, 0:NP], cnt[:, 0:G0_BINS], start=True, stop=True).then_inc(s_base, 1)
            turn_starts(nc, pe, start, ps_vf, ps_qk, reached, k["ident"], k["one"], G0_BINS, G0_N + 8, s_col, s_row, 0)
            pe.wait_ge(s_pad, 3)
            pe.wait_ge(s_w, 16 * 10)
            mm(ps_kv[:].rearrange("p a d -> p (a d)"), zrow[:, 0:P], w[:, 0, 0:2 * D], start=True, stop=False, skip_group_check=True)
            mm(ps_cn[:].rearrange("p a d -> p (a d)"), zrow[:, 0:P], w[:, 0, 0:2 * DC], start=True, stop=False, skip_group_check=True)
            def turn_xn(t):
                wait_alone(pe, s_xn, t + 1)
                for c in range(DC):
                    last = nc.tensor.transpose(ps_T[:, c, 0:NP], xn[:, c * P:(c + 1) * P], k["ident"][0:NP, 0:NP])
                last.then_inc(s_xT, 1)

            def project(t):
                wait_alone(pe, s_xTs, t + 1)
                if not (isinstance(t, int) and t == 0):
                    wait_alone(pe, s_feat, t)
                for ps, at in ((ps_qk[0:NP, :], w[:, :, 0:2 * D]), (ps_vf[0:NP, :], w[:, :, 2 * D:]),
                                   (ps_a[0:NP].rearrange("p j h -> p (j h)"), wa[:].rearrange("p c j h -> p c (j h)"))):
                    for c in range(DC):
                        last = mm(ps, xT[:, c, :], at[:, c], start=c == 0, stop=c == DC - 1)
                last.then_inc(s_proj, 1)

            def add_kv(t):
                wait_alone(pe, s_k4, t + 1)
                for c in range(DC):
                    mm(ps_kv[:, c, :], k2[:, c * P:(c + 1) * P], v[:, bass.ds(t, 1), :].rearrange("p a d -> p (a d)"), start=False, stop=False,
                       skip_group_check=True)
                for c in range(DC):
                    last = mm(ps_cn[:, c, :], k4[:, c * P:(c + 1) * P], k["one"][0:NP, 0:2], start=False, stop=False,
                              skip_group_check=True)
                last.then_inc(s_kv, 1)

            pe.sem_inc(s_kv, 1)
            for t in range(2):
                turn_xn(t)
                project(t)
            with pe.Fori(1, TN - 1) as t:
                turn_xn(t + 1)
                add_kv(t - 1)
                project(t + 1)
            add_kv(TN - 2)
            add_kv(TN - 1)
            mm(ps_kv[:].rearrange("p a d -> p (a d)"), zrow[:, 0:P], w[:, 0, 0:2 * D], start=False, stop=True, skip_group_check=True)
            mm(ps_cn[:].rearrange("p a d -> p (a d)"), zrow[:, 0:P], w[:, 0, 0:2 * DC], start=False, stop=True,
               skip_group_check=True).then_inc(s_kvd, 1)
            pe.wait_ge(s_cnt, 2)
            mm(ps_rank[0:NP, 0, :], k["before"][0:NP, 0:NP], cnt[:], start=True, stop=True)
            mm(ps_rank[0:NP, 1, :], k["one"][0:NP, 0:NP], cnt[:], start=True, stop=True).then_inc(s_base, 1)
            turn_starts(nc, pe, start, ps_vf, ps_qk, reached, k["ident"], k["one"], G1_BINS, G1_N, s_col, s_row, 1)
            pe.wait_ge(s_kvs, 2)
            pT = ps_T[:].rearrange("p a d -> p (a d)").rearrange("p (b e) -> p b e", b=DC)
            for c in range(DC):
                for b in range(DC):
                    last = nc.tensor.transpose(pT[:, b, c * P:(c + 1) * P], kv[:, c, b * P:(b + 1) * P], k["ident"][:])
            last.then_inc(s_kvT, 1)
            pe.wait_ge(s_kvTs, 1)
            for c in range(DC):
                for b in range(DC):
                    last = mm(ps_mix[:, c, :], kvT[:, b, c * P:(c + 1) * P], wout[:, b, :], start=b == 0, stop=b == DC - 1)
            last.then_inc(s_kw, 1)
            pe.wait_ge(s_kws, 1)
            pe.sem_inc(s_mix, 1)
            with pe.Fori(0, TN) as t:
                wait_alone(pe, s_qv, t + 1)
                for j in range(2):
                    for c in range(DC):
                        last = nc.tensor.transpose(ps_T[:, j * DC + c, 0:NP], qv[:, j, c * P:(c + 1) * P], k["ident"][0:NP, 0:NP])
                last.then_inc(s_qvT, 1)
                wait_alone(pe, s_qvTs, t + 1)
                wait_alone(pe, s_mixd, t + 1)
                for j in range(2):
                    for c in range(DC):
                        last = mm(ps_mix[0:NP, j, :], qvT[:, j * DC + c, :], (kw if j == 0 else wout)[:, c, :], start=c == 0,
                                  stop=c == DC - 1)
                last.then_inc(s_mix, 1)


def stage_edges0(nc, a, k):
    with ExitStack() as ctx:
        m = Memory(nc, ctx, "e0")
        RING = 8
        PARTS = 3
        AHEAD = 3
        rec = m.sb("rec", [P, G0_TILES + 2 * AHEAD, 4])
        awb = m.sb("awb", [P, H, 2 * HD + 1])
        abb = m.sb("abb", [P, H])
        const = m.sb("const", [P, G0_TILES, H])
        index = m.sb("index", [P, 2, RING], I32)
        rows = m.sb("rows", [P, 2 * RING, ROW])
        hot = m.sb("hot", [P, 2 * RING, NP])
        hotT = m.sb("hotT", [NP, 2, 2, P], BF16)
        score = m.sb("score", [P, 2, 2, H])
        state = m.sb("state", [NP, RING, ROW])
        acc = k["acc0"]
        GROUPS = G0_N + 8
        bins = m.sb("bins", [1, GROUPS])
        same = m.sb("same", [NP, GROUPS])
        pick = m.sb("pick", [G0_BINS, GROUPS])
        turned = m.sb("turned", [G0_BINS, H, NP])
        source = m.sb("source", [NP, GROUPS, H])
        source3 = m.sb("source3", [NP, GROUPS, PARTS, H], BF16)
        identb = m.sb("identb", [P, P], BF16)

        ps_T = [ctx.enter_context(nc.psum_tensor(f"e0_ps_T{i}", [P, 2, 512], BF16)) for i in range(2)]
        ps_E = [m.ps(f"ps_E{i}", [P, 4, PARTS * H]) for i in range(2)]
        ps_A = m.banks("ps_A", 4)

        s_in = m.sem("in")
        s_w1 = m.sem("expert_weights")
        s_const = m.sem("const_ready")
        s_bin = m.sem("blocks_spread")
        s_turn = m.sem("source_scores_turned")
        s_turnk = m.sem("source_scores_turned_kept")
        s_pick = m.sem("picks_ready")
        s_src = m.sem("source_scores_picked")
        s_srck = m.sem("source_parts_ready")
        s_keep = m.sem("sums_kept")
        s_a = m.sem("scalar_steps")
        s_idx = m.sem("index_staged")
        s_rows = [m.sem(f"rows{i}") for i in range(RING)]
        s_hot = m.sem("one_hot")
        s_T = m.sem("one_hot_T")
        s_Tk = m.sem("one_hot_T_kept")
        s_E = m.sem("source_scores")
        s_sc = m.sem("scores")
        s_w = m.sem("weights")
        s_wm = m.sem("weighted_rows")
        s_agg = m.sem("added_up")
        s_acc = m.sem("accumulated")
        s_v = m.sem("vector_steps")
        block = ctx.enter_context(nc.Block())

        @block.sync
        def _(sp):
            sp.dma_start(rec[:, 0:G0_TILES, :].rearrange("p t f -> p (t f)"),
                         k["sorted0"].rearrange("(p t) f -> p (t f)", p=P)).then_inc(s_in, 16)
            sp.dma_start(awb[:].rearrange("p h o -> p (h o)"),
                         a["L0_gnn_aw"].rearrange("h o -> (h o)").partition_broadcast(P)).then_inc(s_in, 16)
            sp.dma_start(abb[:], a["L0_gnn_ab"].partition_broadcast(P)).then_inc(s_in, 16)
            for e in range(E0):
                load_weight(sp, k["w1"][:, e], a["L0_ffn_w1"][e], s_w1)
            sp.wait_ge(s_w1, 16 * E0)

        @block.gpsimd
        def _(pool):
            def gather(i, half, staged):
                nc.gpsimd.tensor_copy(index[:, half, :], rec[:, bass.ds(i * 2 * RING + half * RING, RING), 0:1]
                                      .rearrange("p a b -> p (a b)")).then_inc(s_idx, 1)
                wait_alone(pool, s_idx, staged)
                for j in range(RING):
                    tile = half * RING + j
                    pool.indirect_dma_start(
                        out=rows[:, tile, :], out_offset=None, in_=k["table"],
                        in_offset=bass.IndirectOffsetOnAxis(ap=index[:, half, j:j + 1].bitcast(U32), axis=0)
                    ).then_inc(s_rows[tile // 2], 16)

            pool.wait_ge(s_in, 48)
            for half in range(2):
                gather(0, half, half + 1)
            with pool.Fori(1, G0_N // RING) as i:
                for half in range(2):
                    wait_alone(pool, s_agg, (i - 1) * RING + (half + 1) * RING // 2)
                    gather(i, half, i * 2 + half + 1)

        def turns(eng, step, tail=()):
            for q in range(RING):
                step(q, q, 0)
            with eng.Fori(1, G0_N // RING) as i:
                for q in range(RING):
                    step(i * RING + q, q, i)
            for s in tail:
                step(G0_N + s, s, None)

        @block.vector
        def _(dve):
            o = Order(dve, s_v)

            def one_hot(s, q):
                for j in range(2):
                    last = nc.vector.tensor_scalar(hot[:, q * 2 + j, :], k["iota"][:, 0:NP],
                                                   rec[:, bass.ds(s * 2 + j, 1), 1:2].rearrange("p a b -> p (a b)"), None, ALU.is_equal)
                last.then_inc(s_hot, 1)

            def scores(s, q, i):
                sc = score[:, q % 2]
                at = q // 2 % 2 * 2
                wait_alone(dve, s_E, s + 1)
                o.done(nc.vector.tensor_reduce(sc, ps_E[q % 2][:, at:at + 2, :].rearrange("p a (c h) -> p a h c", c=PARTS), AX, ALU.add))
                o.settle()
                o.done(nc.vector.tensor_tensor(sc, sc, const[:, bass.ds(s * 2, 2), :], ALU.add))
                dve.wait_ge(s_rows[q], i * 32 + 32)
                o.settle()
                nc.vector.tensor_tensor(sc, sc, rows[:, q * 2:q * 2 + 2, D:], ALU.add).then_inc(s_sc, 1)

            def weigh(s, q):
                r = rows[:, q * 2:q * 2 + 2, 0:D].rearrange("p a (h c) -> p a h c", h=H)
                w = rows[:, q * 2:q * 2 + 2, D:].unsqueeze(3)
                dve.wait_ge(s_w, s + 1)
                nc.vector.tensor_tensor(r, r, spread(w, P, 2, H, HD), ALU.mult).then_inc(s_wm, 1)

            def accumulate(s, q):
                before = state[:, (q - 1) % RING, :]
                if not (isinstance(s, int) and s == 0):
                    dve.wait_ge(s_acc, s)
                wait_alone(dve, s_keep, s + 1)
                dve.wait_ge(s_agg, s + 1)
                nc.vector.scalar_tensor_tensor(state[:, q, :], before, same[:, bass.ds(s, 1)], ps_A[0:NP, q % 4, 0:ROW],
                                               ALU.mult, ALU.add).then_inc(s_acc, 1)

            v = nc.vector
            o.done(v.memset(state[:, RING - 1, :], 0.0))
            o.done(v.memset(same[:, 0:1], 0.0))
            v.tensor_copy(identb[:], k["ident"][:]).then_inc(s_pick, 1)
            v.tensor_copy(bins[:], k["bin0"][:]).then_inc(s_pick, 1)
            nc.vector.memset(acc[:], 0.0).then_inc(s_const, 1)
            nc.vector.memset(rec[:, G0_TILES:, :], -1.0).then_inc(s_const, 1)
            dve.wait_ge(s_in, 48)
            for h in range(H):
                nc.vector.tensor_scalar(const[:, :, h], rec[:, 0:G0_TILES, 2], awb[:, h, 2 * HD:], abb[:, h:h + 1],
                                        ALU.mult, ALU.add).then_inc(s_const, 1)
            dve.wait_ge(s_const, 2 + H)
            for s in range(AHEAD):
                one_hot(s, s)
            dve.wait_ge(s_bin, 1)
            spread_bins = ps_A[:, 0, 0:GROUPS]
            v.tensor_scalar(pick[:], spread_bins[0:G0_BINS], k["number"][0:G0_BINS, :], None, ALU.is_equal).then_inc(s_pick, 1)
            o.done(v.tensor_copy(source[:, :, 0], spread_bins[0:NP]))
            o.settle()
            o.done(v.tensor_tensor(same[:, 1:], source[:, 1:, 0], source[:, 0:GROUPS - 1, 0], ALU.is_equal))
            o.settle()
            dve.wait_ge(s_src, 1)
            for h in range(H):
                o.done(v.tensor_copy(source[:, :, h], ps_A[0:NP, 2 + h // 2, h % 2 * GROUPS:(h % 2 + 1) * GROUPS]))
            o.settle()
            for n in range(PARTS):
                o.done(v.tensor_copy(source3[:, :, n, :], source[:]))
                o.settle()
                if n + 1 < PARTS:
                    o.done(v.tensor_tensor(source[:], source[:], source3[:, :, n, :], ALU.subtract))
                    o.settle()
            dve.sem_inc(s_srck, 1)
            peeled = o.n

            def step(s, q, i):
                first, over = i is not None and isinstance(i, int), i is None
                if first:
                    o.n = peeled + 2 * s
                elif not over and q == 0:
                    o.enter(i - 1, 2 * RING)
                if not (first and s < 1 or over and q > 0):
                    weigh(s - 1, (q - 1) % RING)
                if not over:
                    scores(s, q, i)
                    one_hot(s + AHEAD, (q + AHEAD) % RING)
                if not (first and s < 3):
                    accumulate(s - 3, (q - 3) % RING)
                if not first and not over and q == RING - 1:
                    o.leave(G0_N // RING - 1)

            turns(dve, step, range(3))

        @block.scalar
        def _(act):
            def evacuate(s, q):
                act.wait_ge(s_T, s + 1)
                nc.scalar.activation(hotT[:, q % 2], ps_T[q % 2][0:NP, :, 0:P], ACT.Copy).then_inc(s_Tk, 1)

            def keep(s, q):
                block_of = act.value_load(k["bin0"][0:1, bass.ds(s, 1)], min_val=0, max_val=G0_BINS - 1)
                wait_alone(act, s_acc, s + 1)
                wait_alone(act, s_keep, s + RING)
                nc.scalar.activation(acc[:, bass.ds(block_of, 1), :].rearrange("p a d -> p (a d)"), state[:, q, :], ACT.Copy
                                     ).then_inc(s_keep, 1)

            def step(s, q, i):
                if i is not None:
                    act.wait_ge(s_sc, s + 1)
                    nc.scalar.activation(score[:, q % 2], score[:, q % 2], ACT.Relu, scale=1.0 / 20.0).then_inc(s_a, 1)
                    act.wait_ge(s_a, s + 1)
                    nc.scalar.activation(rows[:, q * 2:q * 2 + 2, D:], score[:, q % 2], ACT.Exp, scale=-1.0).then_inc(s_w, 1)
                    evacuate(s + 2, q)
                if not (isinstance(i, int) and s < 4):
                    keep(s - 4, (q - 4) % RING)

            act.wait_ge(s_turn, 1)
            nc.scalar.activation(turned[:], ps_A[0:G0_BINS, 1, 0:H * NP].rearrange("p (h n) -> p h n", h=H), ACT.Copy).then_inc(s_turnk, 1)
            act.wait_ge(s_const, 2 + H)
            act.sem_inc(s_keep, RING)
            for s in range(2):
                evacuate(s, s)
            turns(act, step, range(4))

        @block.tensor
        def _(pe):
            def transpose(s, q):
                pe.wait_ge(s_hot, s + 1)
                for j in range(2):
                    halves = hot[:, q * 2 + j, :].bitcast(BF16).rearrange("p (n b) -> p n b", b=2)
                    last = nc.tensor.transpose(ps_T[q % 2][0:NP, j, 0:P], halves[:, :, 1], identb[:])
                last.then_inc(s_T, 1)

            def source_scores(s, q):
                pe.wait_ge(s_Tk, s + 1)
                for j in range(2):
                    last = nc.tensor.matmul(ps_E[q % 2][:, q // 2 % 2 * 2 + j, :], hotT[:, q % 2, j, :],
                                            source3[:, bass.ds(s, 1), :, :].rearrange("p a c h -> p (a c h)"),
                                            start=True, stop=True)
                last.then_inc(s_E, 1)

            def add_up(s, q):
                pe.wait_ge(s_wm, s + 1)
                for j in range(2):
                    last = nc.tensor.matmul(ps_A[0:NP, q % 4, 0:ROW], hot[:, q * 2 + j, :], rows[:, q * 2 + j, :],
                                            start=j == 0, stop=j == 1)
                last.then_inc(s_agg, 1)

            def step(s, q, i):
                if i is not None:
                    source_scores(s + 1, (q + 1) % RING)
                    transpose(s + AHEAD, (q + AHEAD) % RING)
                if not (isinstance(i, int) and s < 1):
                    add_up(s - 1, (q - 1) % RING)

            pe.wait_ge(s_pick, 2)
            nc.tensor.matmul(ps_A[:, 0, 0:GROUPS], k["one"][0:1, :], bins[:], start=True, stop=True).then_inc(s_bin, 1)
            for h in range(H):
                last = nc.tensor.transpose(ps_A[0:G0_BINS, 1, h * NP:(h + 1) * NP], k["a_src"][:, :, h], k["ident"][0:NP, 0:NP])
            last.then_inc(s_turn, 1)
            pe.wait_ge(s_turnk, 1)
            pe.wait_ge(s_pick, 3)
            for h in range(H):
                last = nc.tensor.matmul(ps_A[0:NP, 2 + h // 2, h % 2 * GROUPS:(h % 2 + 1) * GROUPS], turned[:, h, :], pick[:],
                                        start=True, stop=True)
            last.then_inc(s_src, 1)
            for s in range(2):
                transpose(s, s)
            pe.wait_ge(s_srck, 1)
            source_scores(0, 0)
            transpose(2, 2)
            turns(pe, step, range(1))


def stage_gate(nc, a, k):
    with ExitStack() as ctx:
        m = Memory(nc, ctx, "g")
        st = m.sb("st", [NP, TN, 6])
        mean = m.sb("mean", [NP, TN])
        rstd = m.sb("rstd", [NP, TN])
        tmp = m.sb("tmp", [NP, TN])
        xn = m.sb("xn", [NP, TB, D])
        xT = m.sb("xT", [P, TB, DC, NP])
        gw = m.sb("gw", [P, DC, E0])
        gb = m.sb("gb", [NP, E0])
        b1r = m.sb("b1r", [E0 * F0 // P, P])
        logit = m.sb("logit", [NP, TN, E0])
        pick = m.sb("pick", [NP, TN, E0])
        best = m.sb("best", [NP, TOPK, TN])
        which = m.sb("which", [NP, TOPK, TN])
        cnt = m.sb("cnt", [NP, E0])
        prefix = m.sb("prefix", [NP, E0])
        total = m.sb("total", [NP, E0])
        groups = m.sb("groups", [NP, E0])
        start = m.sb("start", [NP, E0])
        first = m.sb("first", [NP, E0])
        slot = m.sb("slot", [NP, TOPK * TN])
        mask = m.sb("mask", [NP, E0, TOPK * TN])
        running = m.sb("running", [NP, E0, TOPK * TN])
        ones = m.sb("ones", [NP, E0 * TOPK * TN])
        earlier = m.sb("earlier", [NP, E0])
        column = m.sb("column", [P, 1])
        reached = m.sb("reached", [P, X_N + 2])
        ps_T = m.banks("ps_T", 3)
        ps_L = m.ps("ps_L", [P, TB, E0])
        ps_rank = m.ps("ps_rank", [P, 2, E0])
        ps_b = m.ps("ps_b", [P, P])

        s_w = m.sem("weights")
        s_var = m.sem("variance")
        s_std = m.sem("std")
        s_xn = m.sem("normed")
        s_xT = m.sem("xT_made")
        s_xTk = m.sem("xT_kept")
        s_L = m.sem("logits")
        s_Lk = m.sem("logits_kept")
        s_b = m.sem("b1_turned")
        s_d = m.sem("difference")
        s_e = m.sem("exponential")
        s_cnt = m.sem("counted")
        s_base = m.sem("bases")
        s_col = m.sem("bin_starts")
        s_row = m.sem("bin_starts_turned")
        s_v = m.sem("vector_steps")
        block = ctx.enter_context(nc.Block())

        @block.sync
        def _(sp):
            load_weight(sp, gw[:], a["L0_ffn_gate_w"], s_w)
            sp.dma_start(gb[:], a["L0_ffn_gate_b"].partition_broadcast(NP)).then_inc(s_w, 16)
            sp.dma_start(b1r[:], a["L0_ffn_b1"].rearrange("e (c p) -> (e c) p", p=P)).then_inc(s_w, 16)

        @block.scalar
        def _(act):
            act.wait_ge(s_b, 1)
            nc.scalar.activation(k["b1T"][:], ps_b[:, 0:E0 * F0 // P], ACT.Copy)
            act.wait_ge(s_var, 1)
            nc.scalar.activation(rstd[:], rstd[:], ACT.Sqrt, bias=k["eps5"][0:NP, :]).then_inc(s_std, 1)
            with act.Fori(0, NB) as u:
                wait_alone(act, s_xT, u + 1)
                keep_transposed(nc.scalar, s_xTk, xT[:], ps_T)
            act.wait_ge(s_d, 1)
            nc.scalar.activation(tmp[:], tmp[:], ACT.Exp).then_inc(s_e, 1)

        @block.vector
        def _(dve):
            o = Order(dve, s_v)
            v = nc.vector
            o.done(v.memset(ones[:], 1.0))
            w = k["acc0"][:, :, D:]
            rows = k["normed"]
            o.done(v.reciprocal(w, w))
            o.settle()
            heads = rows.rearrange("p t (h c) -> p t h c", h=H)
            o.done(v.tensor_tensor(heads, heads, spread(w.unsqueeze(3), NP, TN, H, HD), ALU.mult))
            o.settle()
            o.done(v.tensor_tensor(k["x"][:], k["x"][:], rows, ALU.add))
            o.settle()
            layer_norm_stats(o, k["x"], st, mean[:], rstd[:], tmp[:])
            dve.sem_inc(s_var, 1)
            dve.wait_ge(s_std, 1)
            o.done(v.reciprocal(rstd[:], rstd[:]))
            o.settle()
            dve.wait_ge(s_w, 16 * 3)
            def normed_row(to, t):
                return v.tensor_scalar(to, k["x"][:, bass.ds(t, 1), :].rearrange("p a d -> p (a d)"), mean[:, bass.ds(t, 1)],
                                       rstd[:, bass.ds(t, 1)], ALU.subtract, ALU.mult)

            def keep_logits(u):
                wait_alone(dve, s_L, u + 1)
                v.tensor_tensor(logit[:, bass.ds(u * TB, TB), :], ps_L[0:NP], spread(gb[:].unsqueeze(1), NP, TB, E0), ALU.add
                                ).then_inc(s_Lk, 1)

            def step(u, first):
                if not first:
                    wait_alone(dve, s_xT, u)
                for j in range(TB):
                    last = normed_row(xn[:, j, :], u * TB + j)
                last.then_inc(s_xn, 1)
                for j in range(TB):
                    normed_row(rows[:, bass.ds(u * TB + j, 1), :].rearrange("p a d -> p (a d)"), u * TB + j)
                if not first:
                    keep_logits(u - 1)

            step(0, True)
            with dve.Fori(1, NB) as u:
                step(u, False)
            keep_logits(NB - 1)
            dve.wait_ge(s_Lk, NB)
            iota = spread(k["iota"][0:NP, 0:E0].unsqueeze(1), NP, TN, E0)
            for r in range(TOPK):
                o.done(v.tensor_reduce(best[:, r, :], logit[:], AX, ALU.max))
                o.settle()
                o.done(v.tensor_tensor(pick[:], logit[:], spread(best[:, r, :].unsqueeze(2), NP, TN, E0), ALU.is_equal))
                o.settle()
                o.done(v.scalar_tensor_tensor(pick[:], pick[:], -float(E0), iota, ALU.mult, ALU.add))
                o.settle()
                o.done(v.tensor_reduce(which[:, r, :], pick[:], AX, ALU.min))
                o.settle()
                o.done(v.tensor_scalar(which[:, r, :], which[:, r, :], float(E0), None, ALU.add))
                o.settle()
                if r + 1 < TOPK:
                    o.done(v.tensor_tensor(pick[:], iota, spread(which[:, r, :].unsqueeze(2), NP, TN, E0), ALU.is_equal))
                    o.settle()
                    o.done(v.scalar_tensor_tensor(logit[:], pick[:], -1e30, logit[:], ALU.mult, ALU.add))
                    o.settle()
            v.tensor_tensor(tmp[:], best[:, 1, :], best[:, 0, :], ALU.subtract).then_inc(s_d, 1)
            flat = which[:].rearrange("p r t -> p (r t)")
            pairs = [NP, E0, TOPK * TN]
            o.done(v.tensor_tensor(mask[:], spread(flat.unsqueeze(1), *pairs), spread(k["iota"][0:NP, 0:E0].unsqueeze(2), *pairs),
                                   ALU.is_equal))
            o.settle()
            o.done(v.tensor_reduce(cnt[:], mask[:], AX, ALU.add))
            o.done(v.tensor_tensor_scan(running[:].rearrange("p e n -> p (e n)"), ones[:], mask[:].rearrange("p e n -> p (e n)"), 0.0,
                                        ALU.mult, ALU.add))
            o.settle()
            dve.sem_inc(s_cnt, 1)
            o.done(v.tensor_tensor_scan(earlier[:], k["one"][0:NP, 0:E0], cnt[:], 0.0, ALU.mult, ALU.add))
            o.settle()
            o.done(v.tensor_tensor(earlier[:], earlier[:], cnt[:], ALU.subtract))
            o.settle()
            dve.wait_ge(s_e, 1)
            o.done(v.tensor_scalar(k["gate"][:, 0, :], tmp[:], 1.0, None, ALU.add))
            o.settle()
            o.done(v.reciprocal(k["gate"][:, 0, :], k["gate"][:, 0, :]))
            o.settle()
            o.done(v.tensor_tensor(k["gate"][:, 1, :], tmp[:], k["gate"][:, 0, :], ALU.mult))
            dve.wait_ge(s_base, 1)
            o.done(v.tensor_copy(prefix[:], ps_rank[0:NP, 0, :]))
            o.done(v.tensor_copy(total[:], ps_rank[0:NP, 1, :]))
            o.settle()
            rank_bases(o, first[:], total[:], prefix[:], groups[:], start[:], k["one"], P, E0)
            o.done(v.tensor_tensor(first[:], first[:], earlier[:], ALU.subtract))
            o.settle()
            o.done(v.tensor_tensor(running[:], running[:], spread(first[:].unsqueeze(2), *pairs), ALU.add))
            o.settle()
            o.done(v.tensor_tensor(running[:], running[:], mask[:], ALU.mult))
            o.settle()
            o.done(v.tensor_reduce(slot[:], running[:].rearrange("p e n -> p n e"), AX, ALU.add))
            o.settle()
            o.done(v.tensor_copy(k["pairs"][:], slot[:]))
            group_bins(o, k["expert_of"][:], column, reached, ps_T[:, 0], ps_T[:, 1], k["iota"], E0, X_N + 2, s_col, s_row, 0)

        @block.tensor
        def _(pe):
            pe.wait_ge(s_w, 16 * 3)
            nc.tensor.transpose(ps_b[:, 0:E0 * F0 // P], b1r[:], k["ident"][0:E0 * F0 // P, 0:E0 * F0 // P]).then_inc(s_b, 1)
            def step(u, first):
                wait_alone(pe, s_xn, u + 1)
                for j, place in enumerate(tile_places(ps_T)):
                    for c in range(DC):
                        last = nc.tensor.transpose(place[:, c, :], xn[:, j, c * P:(c + 1) * P], k["ident"][0:NP, 0:NP])
                last.then_inc(s_xT, 1)
                wait_alone(pe, s_xTk, u + 1)
                if not first:
                    wait_alone(pe, s_Lk, u)
                for j in range(TB):
                    for c in range(DC):
                        last = nc.tensor.matmul(ps_L[0:NP, j, :], xT[:, j, c, :], gw[:, c, :], start=c == 0, stop=c == DC - 1)
                last.then_inc(s_L, 1)

            step(0, True)
            with pe.Fori(1, NB) as u:
                step(u, False)
            pe.wait_ge(s_cnt, 1)
            nc.tensor.matmul(ps_rank[0:NP, 0, :], k["before"][0:NP, 0:NP], cnt[:], start=True, stop=True)
            nc.tensor.matmul(ps_rank[0:NP, 1, :], k["one"][0:NP, 0:NP], cnt[:], start=True, stop=True).then_inc(s_base, 1)
            turn_starts(nc, pe, start, ps_T[:, 0], ps_T[:, 1], reached, k["ident"], k["one"], E0, X_N + 2, s_col, s_row, 0)


def stage_experts(nc, a, k):
    with ExitStack() as ctx:
        m = Memory(nc, ctx, "x")
        FC = F0 // P
        w2 = m.sb("w2", [P, E0, FC, D])
        RING = 4
        xs = m.sb("xs", [P, RING, D])
        xT = m.sb("xT", [P, 2, DC, P])
        hidden = m.sb("hidden", [P, F0])
        hT = m.sb("hT", [P, FC, P])
        b2 = m.sb("b2", [P, RING, D])
        y = m.sb("y", [P, 2, D])
        stage_row = m.sb("stage_row", [NP, 2, 8], I32)
        stage_rec = m.sb("stage_rec", [NP, 2, 8, 2])
        ps_x = [m.ps(f"ps_x{i}", [P, DC, P]) for i in range(2)]
        ps_h = [m.ps(f"ps_h{i}", [P, F0]) for i in range(2)]
        ps_hT = [m.ps(f"ps_hT{i}", [P, FC, P]) for i in range(2)]
        ps_y = [m.ps(f"ps_y{i}", [P, D]) for i in range(2)]

        s_w2 = m.sem("second_weights")
        s_sent = m.sem("rows_sent")
        s_xs = [m.sem(f"tile_in{i}") for i in range(RING)]
        s_xT = m.sem("xT_made")
        s_xTk = m.sem("xT_kept")
        s_h = m.sem("hidden_made")
        s_hk = m.sem("hidden_kept")
        s_hT = m.sem("hidden_T_made")
        s_hTk = m.sem("hidden_T_kept")
        s_y = m.sem("y_made")
        s_yk = m.sem("y_kept")
        s_out = [m.sem(f"tile_out{i}") for i in range(2)]
        s_stage = m.sem("staged")
        s_scat = [m.sem(f"scattered{i}") for i in range(2)]
        block = ctx.enter_context(nc.Block())

        def turns(eng, step):
            for q in range(RING):
                step(q, q, 0)
            with eng.Fori(1, X_N // RING - 1) as i:
                for q in range(RING):
                    step(i * RING + q, q, i)
            for q in range(RING):
                step(X_N - RING + q, q, X_N // RING - 1)

        def before(s, last):
            return not isinstance(s, int) or s < last

        def after(s, first):
            return not isinstance(s, int) or s >= first

        def expert(eng, s):
            return eng.value_load(k["expert_of"][0:1, bass.ds(s, 1)], min_val=0, max_val=E0 - 1)

        @block.gpsimd
        def _(pool):
            for r in range(TOPK):
                for t in range(TN):
                    pool.indirect_dma_start(
                        out=k["expert_in"], out_offset=bass.IndirectOffsetOnAxis(
                            ap=k["pairs"][:, r * TN + t:r * TN + t + 1].bitcast(U32), axis=0),
                        in_=k["normed"][:, t, :], in_offset=None).then_inc(s_sent, 16)

            scatter_records(nc, pool, k["sorted1"], k["row1"], k["record1"], stage_row, stage_rec, s_stage, s_scat,
                            0, SCATTERS_EARLY)

        @block.sync
        def _(sp):
            for e in range(E0):
                load_weight(sp, w2[:, e], a["L0_ffn_w2"][e], s_w2)
            sp.wait_ge(s_sent, 16 * TOPK * TN)

            tile_in = k["expert_in"].rearrange("(t p) d -> p t d", p=P)
            tile_out = k["expert_out"].rearrange("(t p) d -> p t d", p=P)

            def store(s, q):
                wait_alone(sp, s_yk, s + 1)
                sp.dma_start(tile_out[:, bass.ds(s, 1), :].rearrange("p a d -> p (a d)"), y[:, q % 2, :]).then_inc(s_out[q % 2], 16)

            def step(s, q, i):
                if after(s, RING):
                    store(s - RING, q)
                e = expert(sp, s)
                sp.dma_start(xs[:, q, :], tile_in[:, bass.ds(s, 1), :].rearrange("p a d -> p (a d)")).then_inc(s_xs[q], 16)
                sp.dma_start(b2[:, q, :], a["L0_ffn_b2"][bass.ds(e, 1), :].rearrange("a d -> (a d)").partition_broadcast(P)
                             ).then_inc(s_xs[q], 16)

            turns(sp, step)
            for q in range(RING):
                store(X_N - RING + q, q)
            for n in range(2):
                sp.wait_ge(s_out[n], 16 * X_N // 2)

        @block.scalar
        def _(act):
            def keep_x(s, q):
                act.wait_ge(s_xT, s + 1)
                nc.scalar.activation(xT[:, q % 2], ps_x[q % 2][:], ACT.Copy).then_inc(s_xTk, 1)

            def step(s, q, i):
                e = expert(act, s)
                wait_alone(act, s_hT, s + 1)
                for c in range(FC):
                    last = nc.scalar.activation(hT[:, c, :], ps_hT[q % 2][:, c, :], ACT.Relu, bias=k["b1T"][:, bass.ds(e * FC + c, 1)])
                last.then_inc(s_hTk, 1)
                if before(s + 2, X_N):
                    keep_x(s + 2, q)

            keep_x(0, 0)
            keep_x(1, 1)
            turns(act, step)

        @block.vector
        def _(dve):
            def keep_h(s, q):
                dve.wait_ge(s_h, s + 1)
                nc.vector.tensor_copy(hidden[:], ps_h[q % 2][:]).then_inc(s_hk, 1)

            def step(s, q, i):
                if before(s + 1, X_N):
                    keep_h(s + 1, q + 1)
                if after(s, 2):
                    dve.wait_ge(s_out[q % 2], (i * 2 + q // 2) * 16)
                dve.wait_ge(s_y, s + 1)
                nc.vector.tensor_tensor(y[:, q % 2, :], ps_y[q % 2][:], b2[:, q, :], ALU.add).then_inc(s_yk, 1)

            keep_h(0, 0)
            turns(dve, step)

        @block.tensor
        def _(pe):
            def turn_x(s, q, i):
                wait_alone(pe, s_xs[q], i * 32 + 32)
                for c in range(DC):
                    last = nc.tensor.transpose(ps_x[q % 2][:, c, :], xs[:, q, c * P:(c + 1) * P], k["ident"][:])
                last.then_inc(s_xT, 1)

            def first_product(s, q):
                e = expert(pe, s)
                wait_alone(pe, s_xTk, s + 1)
                for c in range(DC):
                    last = nc.tensor.matmul(ps_h[q % 2][:], xT[:, q % 2, c, :], k["w1"][:, bass.ds(e, 1), c, :].rearrange("p a f -> p (a f)"),
                                            start=c == 0, stop=c == DC - 1)
                last.then_inc(s_h, 1)

            def turn_h(s, q):
                wait_alone(pe, s_hk, s + 1)
                for c in range(FC):
                    last = nc.tensor.transpose(ps_hT[q % 2][:, c, :], hidden[:, c * P:(c + 1) * P], k["ident"][:])
                last.then_inc(s_hT, 1)

            def second_product(s, q):
                e = expert(pe, s)
                if after(s, 2):
                    wait_alone(pe, s_yk, s - 1)
                wait_alone(pe, s_hTk, s + 1)
                for c in range(FC):
                    last = nc.tensor.matmul(ps_y[q % 2][:], hT[:, c, :], w2[:, bass.ds(e, 1), c, :].rearrange("p a d -> p (a d)"),
                                            start=c == 0, stop=c == FC - 1)
                last.then_inc(s_y, 1)

            def step(s, q, i):
                if before(s + 1, X_N):
                    first_product(s + 1, q + 1)
                second_product(s, q)
                if before(s + 2, X_N):
                    turn_x(s + 2, (q + 2) % RING, i + (q + 2) // RING)
                if before(s + 1, X_N):
                    turn_h(s + 1, q + 1)

            turn_x(0, 0, 0)
            turn_x(1, 1, 0)
            pe.wait_ge(s_w2, 16 * E0)
            first_product(0, 0)
            turn_h(0, 0)
            turns(pe, step)


def normalise(o, out, x, mean, rstd):
    over_tiles(o, lambda t: o.eng.tensor_scalar(out[:, bass.ds(t, 1), :].rearrange("p a d -> p (a d)"),
                                                x[:, bass.ds(t, 1), :].rearrange("p a d -> p (a d)"),
                                                mean[:, bass.ds(t, 1)], rstd[:, bass.ds(t, 1)], ALU.subtract, ALU.mult))
    o.settle()


def stage_combine(nc, a, k):
    with ExitStack() as ctx:
        m = Memory(nc, ctx, "c")
        yk = m.sb("yk", [NP, TOPK, TN, D])
        gamma = m.sb("gamma", [NP, D])
        beta = m.sb("beta", [NP, D])
        st = m.sb("st", [NP, TN, 6])
        mean = m.sb("mean", [NP, TN])
        rstd = m.sb("rstd", [NP, TN])
        tmp = m.sb("tmp", [NP, TN])
        s_w = m.sem("weights")
        s_y = [m.sem(f"expert_rows{r}") for r in range(TOPK)]
        s_var = m.sem("variance")
        s_std = m.sem("std")
        s_v = m.sem("vector_steps")
        block = ctx.enter_context(nc.Block())

        @block.sync
        def _(sp):
            sp.dma_start(gamma[:], a["L0_ffn_gamma"].partition_broadcast(NP)).then_inc(s_w, 16)
            sp.dma_start(beta[:], a["L0_ffn_beta"].partition_broadcast(NP)).then_inc(s_w, 16)

        @block.gpsimd
        def _(pool):
            for r in range(TOPK):
                for t in range(TN):
                    pool.indirect_dma_start(
                        out=yk[:, r, t, :], out_offset=None, in_=k["expert_out"],
                        in_offset=bass.IndirectOffsetOnAxis(ap=k["pairs"][:, r * TN + t:r * TN + t + 1].bitcast(U32), axis=0)
                    ).then_inc(s_y[r], 16)

        @block.scalar
        def _(act):
            for n in range(2):
                act.wait_ge(s_var, n + 1)
                nc.scalar.activation(rstd[:], rstd[:], ACT.Sqrt, bias=k["eps5"][0:NP, :]).then_inc(s_std, 1)

        @block.vector
        def _(dve):
            o = Order(dve, s_v)
            v = nc.vector
            y = k["normed"]

            def row_of(t3, t):
                return t3[:, bass.ds(t, 1), :].rearrange("p a d -> p (a d)")

            dve.wait_ge(s_w, 32)
            o.done(v.tensor_tensor(k["x"][:], k["x"][:], spread(beta[:].unsqueeze(1), NP, TN, D), ALU.add))
            for r in range(TOPK):
                dve.wait_ge(s_y[r], 16 * TN)
                over_tiles(o, lambda t: v.scalar_tensor_tensor(row_of(y, t), row_of(yk[:, r], t), k["gate"][:, r, bass.ds(t, 1)],
                                                               row_of(y, t), ALU.mult, ALU.add))
                o.settle()
            for n, rows in enumerate((y, k["x"][:])):
                layer_norm_stats(o, rows, st, mean[:], rstd[:], tmp[:])
                dve.sem_inc(s_var, 1)
                dve.wait_ge(s_std, n + 1)
                o.done(v.reciprocal(rstd[:], rstd[:]))
                o.settle()
                if n == 0:
                    over_tiles(o, lambda t: v.scalar_tensor_tensor(row_of(y, t), row_of(y, t), mean[:, bass.ds(t, 1)], gamma[:],
                                                                   ALU.subtract, ALU.mult))
                    o.settle()
                    over_tiles(o, lambda t: v.scalar_tensor_tensor(row_of(k["x"], t), row_of(y, t), rstd[:, bass.ds(t, 1)],
                                                                   row_of(k["x"], t), ALU.mult, ALU.add))
                    o.settle()
                else:
                    normalise(o, y, rows, mean, rstd)


def stage_project1(nc, a, k):
    with ExitStack() as ctx:
        m = Memory(nc, ctx, "p1")
        MH = 8
        MD = D // MH
        HC = P // MD
        w = m.sb("w", [P, DC, 4 * D])
        wa = m.sb("wa", [P, DC, 2, H])
        wprod = m.sb("wprod", [P, D])
        att = m.sb("att", [P, 2, D])
        n1 = m.sb("n1", [P, DC])
        n2 = m.sb("n2", [NP, D])
        wout = m.sb("wout", [P, DC, D])
        bout = m.sb("bout", [NP, D])
        gbias = m.sb("gbias", [NP, D])
        same = m.sb("same", [P, P])
        st = m.sb("st", [NP, TN, 6])
        mean = m.sb("mean", [NP, TN])
        rs = m.sb("rs", [NP, TN])
        tmp = m.sb("tmp", [NP, TN])
        eps6 = m.sb("eps6", [P, 1])
        zrow = m.sb("zrow", [P, ROW1])
        xn = m.sb("xn", [NP, TB, D])
        xT = m.sb("xT", [P, TB, DC, NP])
        low = m.sb("low", [NP, TB, D])
        high = m.sb("high", [NP, TB, D])
        key = m.sb("key", [NP, TB, D])
        val = m.sb("val", [NP, TB, D])
        lin = m.sb("lin", [NP, TB, H * W1])
        FLAT = DC * TB * NP
        SPANS = ((0, 0, 3 * NP), (1, 3 * NP, 4 * NP), (2, 7 * NP, 3 * NP))
        PIECES = ((0, 0, 3, 0, 0), (0, 3, 2, 1, 0), (1, 3, 2, 1, 2 * NP), (1, 0, 3, 2, 0))
        qT = m.sb("qT", [P, NB, FLAT])
        lowq = m.sb("lowq", [P, FLAT])
        highq = m.sb("highq", [P, FLAT])
        zT = m.sb("zT", [P, FLAT])
        attT = m.sb("attT", [P, FLAT])
        rms = m.sb("rms", [NP, TN])
        score = m.sb("score", [NP, TN, 2 * H])
        least = m.sb("least", [NP, H])
        least1 = m.sb("least1", [H, 1])
        leastb = m.sb("leastb", [H, P])
        shift = m.sb("shift", [NP, H])
        kv = m.sb("kv", [P, DC, P])
        kz = m.sb("kz", [P, DC, P])
        stage_row = m.sb("stage_row", [NP, 2, 8], I32)
        stage_rec = m.sb("stage_rec", [NP, 2, 8, 2])
        ps_T = m.banks("ps_T", 3)
        ps_p = m.banks("ps_p", 3)
        ps_o = m.banks("ps_o", 2)
        ps_a = ps_o[:, 0, 0:TB * 2 * H]
        ps_kv = ps_o[:, 1, 0:DC * (P + 1)]
        kv_of = [ps_kv[:, c * (P + 1):c * (P + 1) + P] for c in range(DC)]
        ks_of = [ps_kv[:, c * (P + 1) + P:(c + 1) * (P + 1)] for c in range(DC)]

        s_w = m.sem("weights")
        s_same = m.sem("same_ready")
        s_wk = m.sem("weights_ready")
        s_z = m.sem("zeros")
        s_ms = m.sem("mean_squares")
        s_rms = m.sem("rms")
        s_xn = m.sem("normed")
        s_xT = m.sem("xT_made")
        s_xTk = m.sem("xT_kept")
        s_q = m.sem("q_made")
        s_lowq = m.sem("q_low_part")
        s_highq = m.sem("q_high_part")
        s_ok = m.sem("outputs_added")
        s_qk = m.sem("kv_projected")
        s_vx = m.sem("vx_made")
        s_vxk = m.sem("vx_kept")
        s_low = m.sem("low_part")
        s_high = m.sem("high_part")
        s_k = m.sem("key_ready")
        s_kv = m.sem("kv_added")
        s_a = m.sem("scores_made")
        s_ak = m.sem("scores_kept")
        s_tab = m.sem("table_written")
        s_zero = m.sem("empty_rows")
        s_l = m.sem("least_steps")
        s_lT = m.sem("least_turned")
        s_sc = m.sem("score_rows")
        s_kvk = m.sem("kv_kept")
        s_num = m.sem("numerators")
        s_att = m.sem("attention_rows")
        s_o = m.sem("outputs")
        s_stage = m.sem("staged")
        s_scat = [m.sem(f"scattered{i}") for i in range(2)]
        s_v = m.sem("vector_steps")
        block = ctx.enter_context(nc.Block())

        def row_of(t3, t):
            return t3[:, bass.ds(t, 1), :].rearrange("p a d -> p (a d)")

        def turns(eng, step):
            step(0, True)
            with eng.Fori(1, NB) as u:
                step(u, False)

        @block.sync
        def _(sp):
            load_weight(sp, w[:, :, 0:3 * D], a["L1_mix_w_qkv"], s_w)
            load_weight(sp, w[:, :, 3 * D:], a["L1_gnn_W"], s_w)
            load_weight(sp, wout[:], a["L1_mix_w_out"], s_w)
            for j, name in enumerate(("L1_gnn_att_src", "L1_gnn_att_dst")):
                sp.dma_start(att[:, j, :], a[name].rearrange("h o -> (h o)").partition_broadcast(P)).then_inc(s_w, 16)
            for c in range(DC):
                sp.dma_start(n1[:, c:c + 1], a["L1_mix_w_norm1"][c * P:(c + 1) * P].rearrange("(p a) -> p a", a=1)).then_inc(s_w, 16)
            for t, name in ((n2, "L1_mix_w_norm2"), (bout, "L1_mix_b_out"), (gbias, "L1_gnn_bias")):
                sp.dma_start(t[:], a[name].partition_broadcast(NP)).then_inc(s_w, 16)
            sp.wait_ge(s_z, 3)
            extra = B1 * G1_BINS - NN
            sp.dma_start(k["table1"][NN:, :], zrow[0:extra, :]).then_inc(s_zero, 16)
            sp.dma_start(k["score1"][NN:, :], zrow[0:extra, 0:2 * H]).then_inc(s_zero, 16)
            rows = k["table1"][0:NN, :].rearrange("(p t) d -> p t d", p=NP)

            def step(u, first):
                for j in range(TB):
                    t = u * TB + j
                    wait_alone(sp, s_vxk, t + 1)
                    sp.dma_start(rows[:, bass.ds(t, 1), 0:H * W1].rearrange("p a d -> p (a d)"), lin[:, j, :]).then_inc(s_tab, 16)

            turns(sp, step)
            sp.wait_ge(s_sc, 1)
            sp.dma_start(rows[:, :, H * W1:], score[:, :, 0:H]).then_inc(s_zero, 16)
            sp.dma_start(k["score1"][0:NN, :].rearrange("(p t) d -> p t d", p=NP), score[:]).then_inc(s_zero, 16)
            sp.wait_ge(s_zero, 64)
            sp.wait_ge(s_tab, 16 * TN)

        @block.gpsimd
        def _(pool):
            nc.gpsimd.memset(same[:], 1.0).then_inc(s_same, 1)
            view = same[:].rearrange("p (h d) -> p h d", h=HC)
            pool.wait_ge(s_same, 1)
            nc.gpsimd.affine_select(out=view, in_=view, compare_op=ALU.is_ge, fill=0.0, base=0,
                                    pattern=[[-MD, HC], [0, MD]], channel_multiplier=1).then_inc(s_same, 1)
            pool.wait_ge(s_same, 2)
            nc.gpsimd.affine_select(out=view, in_=view, compare_op=ALU.is_ge, fill=0.0, base=MD - 1,
                                    pattern=[[MD, HC], [0, MD]], channel_multiplier=-1).then_inc(s_same, 1)
            scatter_records(nc, pool, k["sorted1"], k["row1"], k["record1"], stage_row, stage_rec, s_stage, s_scat,
                            SCATTERS_EARLY, SCATTERS)

        @block.scalar
        def _(act):
            act.wait_ge(s_ms, 1)
            nc.scalar.activation(rs[:], rs[:], ACT.Sqrt, bias=eps6[0:NP, :]).then_inc(s_rms, 1)

            def step(u, first):
                wait_alone(act, s_xT, u + 1)
                keep_transposed(nc.scalar, s_xTk, xT[:], ps_T)
                wait_alone(act, s_lowq, u + 1)
                for bank, at, n in SPANS:
                    nc.scalar.activation(highq[:, at:at + n], ps_T[:, bank, 0:n], ACT.Relu)
                nc.scalar.activation(lowq[:], lowq[:], ACT.Exp).then_inc(s_highq, 1)
                for j in range(TB):
                    t = u * TB + j
                    if not first:
                        wait_alone(act, s_kv, t - TB + 1)
                        wait_alone(act, s_tab, u * 16 * TB)
                    wait_alone(act, s_vx, t + 1)
                    nc.scalar.activation(lin[:, j, :].rearrange("p (h c) -> p h c", h=H)[:, :, 0:HD],
                                         ps_p[0:NP, 2, 0:D].rearrange("p (h c) -> p h c", h=H), ACT.Copy,
                                         scale=rms[:, bass.ds(t, 1)]).then_inc(s_vxk, 1)
                    wait_alone(act, s_low, t + 1)
                    nc.scalar.activation(val[:, j, :], ps_p[0:NP, j % 2, D:], ACT.Copy)
                    nc.scalar.activation(high[:, j, :], ps_p[0:NP, j % 2, 0:D], ACT.Relu)
                    nc.scalar.activation(low[:, j, :], low[:, j, :], ACT.Exp).then_inc(s_high, 1)

            turns(act, step)
            act.wait_ge(s_ms, 2)
            nc.scalar.activation(rs[:], rs[:], ACT.Sqrt, bias=eps6[0:NP, :]).then_inc(s_rms, 1)

        @block.vector
        def _(dve):
            o = Order(dve, s_v)
            v = nc.vector
            v.memset(zrow[:], 0.0).then_inc(s_z, 1)
            v.memset(eps6[:], 1e-6).then_inc(s_z, 1)
            v.memset(lin[:].rearrange("p t (h c) -> p t h c", h=H)[:, :, :, HD:], 1.0).then_inc(s_z, 1)

            def root_mean_square(n):
                turn_stats(o, st, mean[:], rs[:], tmp[:])
                o.done(v.tensor_tensor(mean[:], mean[:], mean[:], ALU.mult))
                o.settle()
                o.done(v.tensor_tensor(rs[:], rs[:], mean[:], ALU.add))
                o.settle()
                dve.sem_inc(s_ms, 1)
                dve.wait_ge(s_rms, n)
                o.done(v.tensor_copy(rms[:], rs[:]))
                o.settle()
                o.done(v.reciprocal(rs[:], rs[:]))
                o.settle()

            over_tiles(o, lambda t: v.bn_stats(st[:, bass.ds(t, 1), :], row_of(k["normed"], t)))
            root_mean_square(1)
            dve.wait_ge(s_w, 16 * 10)
            for c in range(DC):
                for j in range(2):
                    o.settle()
                    o.done(v.tensor_tensor(wprod[:], w[:, c, 3 * D:], att[:, j, :], ALU.mult))
                    o.settle()
                    o.done(v.tensor_reduce(wa[:, c, j, :], wprod[:].rearrange("p (h o) -> p h o", h=H), AX, ALU.add))
                v.tensor_scalar(w[:, c, 0:3 * D], w[:, c, 0:3 * D], n1[:, c:c + 1], None, ALU.mult).then_inc(s_wk, 1)
            o.settle()
            dve.sem_inc(s_wk, 1)

            def step(u, first):
                if not first:
                    dve.wait_ge(s_xTk, u)
                for j in range(TB):
                    t = u * TB + j
                    last = v.tensor_scalar(xn[:, j, :], row_of(k["normed"], t), rs[:, bass.ds(t, 1)], None, ALU.mult)
                last.then_inc(s_xn, 1)
                wait_alone(dve, s_q, u + 1)
                for bank, at, n in SPANS:
                    last = v.tensor_scalar(lowq[:, at:at + n], ps_T[:, bank, 0:n], 0.0, None, ALU.min)
                last.then_inc(s_lowq, 1)
                for j in range(TB):
                    t = u * TB + j
                    if not first:
                        wait_alone(dve, s_kv, t - TB + 1)
                    wait_alone(dve, s_qk, t + 1)
                    v.tensor_scalar(low[:, j, :], ps_p[0:NP, j % 2, 0:D], 0.0, None, ALU.min).then_inc(s_low, 1)
                    if j == 0:
                        wait_alone(dve, s_highq, u + 1)
                        o.done(v.tensor_tensor(qT[:, bass.ds(u, 1), :].rearrange("p a n -> p (a n)"), lowq[:], highq[:], ALU.add))
                    wait_alone(dve, s_high, t + 1)
                    v.tensor_tensor(key[:, j, :], low[:, j, :], high[:, j, :], ALU.add).then_inc(s_k, 1)
                xs = k["x"][:, bass.ds(u * TB, TB), :]
                o.done(v.tensor_tensor(xs, xs, spread(gbias[:].unsqueeze(1), NP, TB, D), ALU.add))
                dve.wait_ge(s_a, u + 1)
                v.tensor_tensor(score[:, bass.ds(u * TB, TB), :], ps_a[0:NP, :].rearrange("p (t h) -> p t h", t=TB),
                                spread(rms[:, bass.ds(u * TB, TB)].unsqueeze(2), NP, TB, 2 * H), ALU.mult).then_inc(s_ak, 1)

            step(0, True)
            with dve.Fori(1, NB) as u:
                o.enter(u - 1, 2)
                step(u, False)
                o.leave(NB - 1)
            dve.wait_ge(s_ak, NB)
            v.tensor_reduce(least[:], score[:, :, 0:H].rearrange("p t h -> p h t"), AX, ALU.min).then_inc(s_l, 1)
            dve.wait_ge(s_lT, 1)
            o.done(v.tensor_reduce(least1[:], ps_T[0:H, 0, 0:NP], AX, ALU.min))
            o.settle()
            v.tensor_copy(leastb[:], spread(least1[:], H, P)).then_inc(s_l, 1)
            dve.wait_ge(s_lT, 2)
            o.done(v.tensor_copy(shift[:], ps_a[0:NP, 0:H]))
            o.settle()
            sb = spread(shift[:].unsqueeze(1), NP, TN, H)
            o.done(v.scalar_tensor_tensor(score[:, :, 0:H], score[:, :, 0:H], 1.0, sb, ALU.add, ALU.subtract))
            o.done(v.scalar_tensor_tensor(score[:, :, H:], score[:, :, H:], -1.0, sb, ALU.add, ALU.add))
            o.settle()
            dve.sem_inc(s_sc, 1)
            dve.wait_ge(s_kv, TN + 1)
            dve.wait_ge(s_same, 3)
            for c in range(DC):
                v.tensor_tensor(kv[:, c, :], kv_of[c], same[:], ALU.mult).then_inc(s_kvk, 1)
                v.tensor_scalar(kz[:, c, :], same[:], ks_of[c], None, ALU.mult).then_inc(s_kvk, 1)
            o.settle()
            with dve.Fori(0, NB) as u:
                o.enter(u, 5 + 1 + TB)
                wait_alone(dve, s_num, u + 1)
                for bank, at, n in SPANS:
                    o.done(v.tensor_scalar(zT[:, at:at + n], ps_p[:, bank, 0:n], 1e-6, None, ALU.add))
                o.settle()
                o.done(v.reciprocal(zT[:], zT[:]))
                o.settle()
                for bank, at, n in SPANS:
                    last = v.tensor_tensor(attT[:, at:at + n], ps_T[:, bank, 0:n], zT[:, at:at + n], ALU.mult)
                last.then_inc(s_att, 1)
                rows = k["normed"][:, bass.ds(u * TB, TB), :]
                o.done(v.tensor_tensor(rows, rows, spread(bout[:].unsqueeze(1), NP, TB, D), ALU.add))
                o.settle_alone()
                for j in range(TB):
                    t = u * TB + j
                    wait_alone(dve, s_o, t + 1)
                    v.tensor_tensor(row_of(k["normed"], t), row_of(k["normed"], t), ps_o[0:NP, j % 2, 0:D], ALU.add).then_inc(s_ok, 1)
                wait_alone(dve, s_ok, u * TB + TB)
                xs = k["x"][:, bass.ds(u * TB, TB), :]
                o.done(v.tensor_tensor(xs, xs, rows, ALU.add))
                for j in range(TB):
                    t = u * TB + j
                    o.done(v.bn_stats(st[:, bass.ds(t, 1), :], row_of(k["normed"], t)))
                o.leave(NB)
            h = k["normed"]
            root_mean_square(2)
            over_tiles(o, lambda t: v.scalar_tensor_tensor(row_of(h, t), row_of(h, t), rs[:, bass.ds(t, 1)], n2[:], ALU.mult, ALU.mult))
            o.settle()
            o.done(v.tensor_tensor(k["x"][:], k["x"][:], h, ALU.add))

        @block.tensor
        def _(pe):
            mm = nc.tensor.matmul
            pe.wait_ge(s_wk, DC + 1)
            pe.wait_ge(s_z, 3)
            mm(ps_kv[:], zrow[:, 0:P], w[:, 0, 0:DC * (P + 1)], start=True, stop=False, skip_group_check=True)

            def turn(n):
                wait_alone(pe, s_xn, n)
                for j, place in enumerate(tile_places(ps_T)):
                    for c in range(DC):
                        last = nc.tensor.transpose(place[:, c, :], xn[:, j, c * P:(c + 1) * P], k["ident"][0:NP, 0:NP])
                last.then_inc(s_xT, 1)
                wait_alone(pe, s_xTk, n)

            def state(t, j):
                wait_alone(pe, s_k, t + 1)
                for c in range(DC):
                    kc = key[:, j, c * P:(c + 1) * P]
                    mm(kv_of[c], kc, val[:, j, c * P:(c + 1) * P], start=False, stop=False, skip_group_check=True)
                    last = mm(ks_of[c], kc, k["one"][0:NP, 0:1], start=False, stop=False, skip_group_check=True)
                last.then_inc(s_kv, 1)

            def step(u, first):
                if not first:
                    wait_alone(pe, s_highq, u)
                turn(u + 1)
                for columns, t0, n, bank, at in PIECES:
                    for c in range(DC):
                        last = mm(ps_T[:, bank, at:at + n * NP].rearrange("p (t n) -> p t n", t=n), w[:, c, columns * P:(columns + 1) * P],
                                  xT[:, t0:t0 + n, c, :], start=c == 0, stop=c == DC - 1)
                last.then_inc(s_q, 1)
                for j in range(TB):
                    t = u * TB + j
                    if not (first and j < 2):
                        wait_alone(pe, s_high, t - 1 if j else t)
                    for c in range(DC):
                        last = mm(ps_p[0:NP, j % 2, :], xT[:, j, c, :], w[:, c, D:3 * D], start=c == 0, stop=c == DC - 1)
                    last.then_inc(s_qk, 1)
                    if not (first and j < 1):
                        wait_alone(pe, s_vxk, t)
                    for c in range(DC):
                        last = mm(ps_p[0:NP, 2, 0:D], xT[:, j, c, :], w[:, c, 3 * D:], start=c == 0, stop=c == DC - 1)
                    last.then_inc(s_vx, 1)
                    if not first and j == 0:
                        wait_alone(pe, s_ak, u)
                    for c in range(DC):
                        last = mm(ps_a[0:NP, j * 2 * H:(j + 1) * 2 * H], xT[:, j, c, :], wa[:, c].rearrange("p j h -> p (j h)"),
                                  start=c == 0, stop=c == DC - 1)
                    if j == TB - 1:
                        last.then_inc(s_a, 1)
                    if j > 0:
                        state(t - 1, j - 1)
                state(u * TB + TB - 1, TB - 1)

            turns(pe, step)
            mm(ps_kv[:], zrow[:, 0:P], w[:, 0, 0:DC * (P + 1)], start=False, stop=True, skip_group_check=True).then_inc(s_kv, 1)
            pe.wait_ge(s_l, 1)
            nc.tensor.transpose(ps_T[0:H, 0, 0:NP], least[:], k["ident"][0:NP, 0:NP]).then_inc(s_lT, 1)
            pe.wait_ge(s_l, 2)
            mm(ps_a[:, 0:H], leastb[:], k["ident"][0:H, 0:H], start=True, stop=True).then_inc(s_lT, 1)
            pe.wait_ge(s_kvk, 2 * DC)
            pe.wait_ge(s_sc, 1)

            def numerators(u):
                if not (isinstance(u, int) and u == 0):
                    wait_alone(pe, s_att, u)
                for columns, t0, n, bank, at in PIECES:
                    begin = SPANS[bank][1] + at
                    q_piece = qT[:, bass.ds(u, 1), begin:begin + n * NP].rearrange("p a n -> p (a n)")
                    mm(ps_T[:, bank, at:at + n * NP], kv[:, columns, :], q_piece, start=True, stop=True)
                    last = mm(ps_p[:, bank, at:at + n * NP], kz[:, columns, :], q_piece, start=True, stop=True)
                last.then_inc(s_num, 1)

            def outputs(u, first):
                wait_alone(pe, s_att, u + 1)
                for j in range(TB):
                    t = u * TB + j
                    if not (first and j < 2):
                        wait_alone(pe, s_ok, t - 1 if j else t)
                    for c in range(DC):
                        at = (j if c == 0 else TB + (j + 2) % TB) * NP
                        last = mm(ps_o[0:NP, j % 2, 0:D], attT[:, at:at + NP], wout[:, c, :], start=c == 0, stop=c == DC - 1)
                    last.then_inc(s_o, 1)

            numerators(0)
            outputs(0, True)
            numerators(1)
            with pe.Fori(1, NB - 1) as u:
                outputs(u, False)
                numerators(u + 1)
            outputs(NB - 1, False)


def stage_edges1(nc, a, k):
    with ExitStack() as ctx:
        m = Memory(nc, ctx, "e1")
        TG = 8
        RING = 4
        TURNS = G1_N // TG
        assert (TURNS - 1) % RING == 0
        STEPS = (TURNS - 1) // RING
        SPLIT = 3
        HALF = TG // 2
        PARTS = [slice(0, G1_BINS // 2), slice(G1_BINS // 2, G1_BINS)]
        rec = m.sb("rec", [P, G1_N + TG, 2])
        index = m.sb("index", [P, RING, TG], I32)
        rows = m.sb("rows", [P, RING, TG, ROW1])
        nodes = m.sb("nodes", [P, G1_BINS, 2 * H])
        to = m.sb("to", [P, G1_BINS])
        own = m.sb("own", [P, G1_BINS])
        ownrow = m.sb("ownrow", [P, G1_BINS, W1])
        acc = m.sb("acc", [P, G1_BINS, W1 + 1])
        bins = m.sb("bins", [1, G1_N])
        turned = m.sb("turned", [G1_BINS, 2, P])
        pick = m.sb("pick", [G1_BINS, G1_N])
        same = m.sb("same", [P, G1_N])
        gap = m.sb("gap", [P, G1_N])
        tos = m.sb("tos", [P, G1_N])
        owns = m.sb("owns", [P, G1_N])
        tops = m.sb("tops", [P, G1_N + 1])
        headsel = m.sb("headsel", [P, H])
        identb = m.sb("identb", [P, P], BF16)
        hot = m.sb("hot", [P, RING, TG, B1], BF16)
        hotT = m.sb("hotT", [P, RING, TG, P], BF16)
        marked = m.sb("marked", [P, TG, P])
        weight = m.sb("weight", [P, TG, P])
        most = m.sb("most", [P, TG])
        z = m.sb("z", [P, 2, TG])
        drop = m.sb("drop", [P, TG])
        scale = m.sb("scale", [P, RING, TG])
        state = m.sb("state", [P, RING, TG, W1 + 1])
        tos3 = m.sb("tos3", [P, SPLIT, G1_N], BF16)
        z3 = m.sb("z3", [P, SPLIT, TG], BF16)
        left = m.sb("left", [P, G1_N])
        spreads = m.sb("spreads", [P, TG, 2, SPLIT, H], BF16)
        found = m.sb("found", [P, 2 * TG, H])
        score = m.sb("score", [P, TG, H])
        ex = m.sb("ex", [P, TG, H])
        zend = m.sb("zend", [P, 2, G1_BINS])

        ps_hT = ctx.enter_context(nc.psum_tensor("e1_ps_hT", [P, TG, P], BF16))
        ps_mT = m.banks("ps_mT", 2)
        ps_S = m.ps("ps_S", [P, 2 * TG, SPLIT * H])
        ps_A2 = m.banks("ps_A", 4)

        s_rec = m.sem("records")
        s_in = m.sem("nodes_in")
        s_own = m.sem("own_rows")
        s_const = m.sem("const_ready")
        s_binT = m.sem("block_scores_turned")
        s_binTk = m.sem("block_scores_turned_kept")
        s_bin = m.sem("blocks_spread")
        s_pick = m.sem("picks_ready")
        s_tos = m.sem("tile_scores")
        s_idx = m.sem("index_staged")
        s_rows = [m.sem(f"rows{j}") for j in range(RING)]
        s_hot = m.sem("one_hot")
        s_hT = m.sem("one_hot_T")
        s_hTk = m.sem("one_hot_T_kept")
        s_mk = m.sem("marked_scores")
        s_mT = m.sem("marked_T")
        s_spr = m.sem("spreads_ready")
        s_S = m.sem("edge_spreads")
        s_sc = m.sem("scores")
        s_ex = m.sem("exponentials")
        s_wt = m.sem("weights")
        s_scale = m.sem("scales")
        s_agg = m.sem("added_up")
        s_acc = m.sem("accumulated")
        s_keep = m.sem("sums_kept")
        s_end = m.sem("own_differences")
        s_oe = m.sem("own_exponentials")
        s_done = m.sem("averaged")
        s_out = m.sem("written")
        s_v = m.sem("vector_steps")
        block = ctx.enter_context(nc.Block())

        def turns(eng, step, tail=(), enter=None, leave=None):
            step(0, RING - 1, -1)
            for j in range(RING):
                step(1 + j, j, 0)
            with eng.Fori(1, STEPS) as u:
                if enter:
                    enter(u)
                for j in range(RING):
                    step(u * RING + 1 + j, j, u)
                if leave:
                    leave()
            for n in tail:
                step(TURNS + n, n, None)

        def known(i):
            return isinstance(i, int)

        def sums_of(j):
            return ps_A2[:, j % 2 * 2:j % 2 * 2 + 2]

        def tiles_of(t2, i, shift=0):
            return t2[:, bass.ds(i * TG + shift, TG)]

        @block.sync
        def _(sp):
            sp.dma_start(rec[:, 0:G1_N, :].rearrange("p t f -> p (t f)"),
                         k["sorted1"].rearrange("(p t) f -> p (t f)", p=P)).then_inc(s_rec, 16)
            by_lane = k["score1"].rearrange("(n k) c -> n (k c)", n=B1)
            rows_of = k["table1"].rearrange("(n k) d -> n k d", n=B1)
            out_of = k["attended1"].rearrange("(n k) d -> n k d", n=B1)
            for h in range(H):
                sp.dma_start(nodes[h * B1:(h + 1) * B1].rearrange("p k c -> p (k c)"), by_lane).then_inc(s_in, 16)
            for h in range(H):
                sp.dma_start(ownrow[h * B1:(h + 1) * B1], rows_of[:, :, h * W1:(h + 1) * W1]).then_inc(s_own, 16)
            for n, part in enumerate(PARTS):
                sp.wait_ge(s_done, n + 1)
                for h in range(H):
                    sp.dma_start(out_of[:, part, h * HD:(h + 1) * HD], acc[h * B1:(h + 1) * B1, part, 0:HD]).then_inc(s_out, 16)
            sp.wait_ge(s_out, 16 * H * len(PARTS))

        @block.gpsimd
        def _(pool):
            def step(i, j, u):
                if not known(i) or i >= RING:
                    wait_alone(pool, s_agg, i - RING + 1)
                nc.gpsimd.tensor_copy(index[:, j, :], rec[:, bass.ds(i * TG, TG), 0:1].rearrange("p a b -> p (a b)")
                                      ).then_inc(s_idx, 1)
                wait_alone(pool, s_idx, i + 1)
                for q in range(TG):
                    pool.indirect_dma_start(
                        out=rows[:, j, q, :], out_offset=None, in_=k["table1"],
                        in_offset=bass.IndirectOffsetOnAxis(ap=index[:, j, q:q + 1].bitcast(U32), axis=0)
                    ).then_inc(s_rows[j], 16)

            pool.wait_ge(s_rec, 16)
            turns(pool, step)

        @block.vector
        def _(dve):
            o = Order(dve, s_v)
            v = nc.vector

            def by_head(t3):
                return t3.rearrange("p t (h n) -> p t h n", h=H)

            def over_heads(j):
                return spread(hot[:, j].unsqueeze(2), P, TG, H, B1)

            def one_hot(i, j):
                v.tensor_tensor(hot[:, j], spread(k["iota"][:, 0:B1].unsqueeze(1), P, TG, B1),
                                spread(rec[:, bass.ds(i * TG, TG), 1:2], P, TG, B1), ALU.is_equal).then_inc(s_hot, 1)

            def mark(i, j, u):
                dve.wait_ge(s_rows[j], 128 * (u + 1 + (j == RING - 1)))
                dve.wait_ge(s_hot, i + 1)
                v.tensor_tensor(by_head(marked[:]), over_heads(j), spread(rows[:, j, :, H * W1:].unsqueeze(3), P, TG, H, B1),
                                ALU.mult).then_inc(s_mk, 1)

            def scores(i, j):
                sc = score[:]
                wait_alone(dve, s_S, i + 1)
                o.done(v.tensor_reduce(found[:], ps_S.rearrange("p x (c h) -> p x h c", c=SPLIT), AX, ALU.add))
                to_and_top = found[:].rearrange("p (t a) h -> p t a h", a=2)
                o.settle()
                o.done(v.tensor_tensor(sc, rows[:, j, :, H * W1:], to_and_top[:, :, 0], ALU.add))
                o.settle()
                o.done(v.scalar_tensor_tensor(sc, sc, 0.2, sc, ALU.mult, ALU.max))
                o.settle()
                v.tensor_tensor(sc, sc, to_and_top[:, :, 1], ALU.subtract).then_inc(s_sc, 1)

            def ready_to_add(i, j):
                wait_alone(dve, s_scale, i + 1)
                if not (known(i) and i < RING):
                    wait_alone(dve, s_keep, (i - RING + 1) * TG)
                v.tensor_copy(state[:, j, :, W1], tiles_of(tops, i, 1))
                wait_alone(dve, s_agg, i + 1)

            def add_tile(i, j, q):
                before = state[:, j, q - 1, 0:W1] if q else state[:, (j - 1) % RING, TG - 1, 0:W1]
                if not (known(i) and i == 0 and q == 0):
                    dve.wait_ge(s_acc, i * TG + q)
                v.scalar_tensor_tensor(state[:, j, q, 0:W1], before, scale[:, j, q:q + 1], sums_of(j)[:, q // HALF, q % HALF * W1:(q % HALF + 1) * W1],
                                       ALU.mult, ALU.add).then_inc(s_acc, 1)

            def weigh(i, j):
                dve.wait_ge(s_ex, i + 1)
                v.tensor_tensor(by_head(weight[:]), over_heads(j), spread(ex[:].unsqueeze(3), P, TG, H, B1),
                                ALU.mult).then_inc(s_wt, 1)

            def in_head_column(out, parts):
                shape = [P, TG, SPLIT, H]
                return v.tensor_tensor(out, spread(parts.rearrange("p c t -> p t c").unsqueeze(3), *shape),
                                       spread(headsel[:].unsqueeze(1).unsqueeze(1), *shape), ALU.mult)

            def raise_tops(i, add):
                to_i = tiles_of(tos, i)
                o.done(in_head_column(spreads[:, :, 0], tos3[:, :, bass.ds(i * TG, TG)]))
                wait_alone(dve, s_mT, i + 1)
                o.done(v.tensor_reduce(most[:].rearrange("p (b t) -> p b t", b=2),
                                       ps_mT[:].rearrange("p b (t e) -> p b t e", t=HALF), AX, ALU.max))
                add(0)
                o.settle()
                o.done(v.tensor_tensor(most[:], most[:], tiles_of(owns, i), ALU.max))
                add(1)
                o.settle_alone()
                o.done(v.tensor_tensor_scan(tiles_of(tops, i, 1), tiles_of(same, i), most[:], column(tops, i * TG), ALU.mult, ALU.max))
                add(2)
                o.settle()
                o.done(v.tensor_tensor(z[:, 0, :], tiles_of(tops, i), to_i, ALU.add))
                o.done(v.tensor_tensor(z[:, 1, :], tiles_of(tops, i, 1), to_i, ALU.add))
                add(3)
                o.settle()
                o.done(v.scalar_tensor_tensor(z[:], z[:], 0.2, z[:], ALU.mult, ALU.max))
                add(4)
                o.settle()
                o.done(v.tensor_copy(z3[:, 0], z[:, 1, :]))
                o.done(v.tensor_tensor(drop[:], z[:, 0, :], z[:, 1, :], ALU.subtract))
                add(5)
                o.settle()
                o.done(v.tensor_tensor(left[:, 0:TG], z[:, 1, :], z3[:, 0], ALU.subtract))
                o.done(v.tensor_tensor(drop[:], drop[:], tiles_of(gap, i), ALU.min))
                add(6)
                o.settle_alone()
                o.done(v.tensor_copy(z3[:, 1], left[:, 0:TG]))
                add(7)
                o.settle()
                o.done(v.tensor_tensor(z3[:, 2], left[:, 0:TG], z3[:, 1], ALU.subtract))
                o.settle()
                o.done(in_head_column(spreads[:, :, 1], z3[:]))
                o.settle_alone()
                dve.sem_inc(s_spr, 1)

            def column(t2, at):
                return t2[:, bass.ds(at, 1)]

            dve.wait_ge(s_rec, 16)
            o.done(v.memset(rec[:, G1_N:, :], -1.0))
            o.done(v.memset(headsel[:], 0.0))
            o.done(v.memset(state[:, RING - 2, TG - 1, :], 0.0))
            o.done(v.memset(tops[:, 0:1], 0.0))
            o.done(v.memset(same[:, 0:1], 0.0))
            o.done(v.memset(acc[:], 0.0))
            o.done(v.tensor_copy(bins[:], k["bin1"][:]))
            o.settle()
            for h in range(H):
                o.done(v.memset(headsel[h * B1:(h + 1) * B1, h:h + 1], 1.0))
            v.tensor_copy(identb[:], k["ident"][:]).then_inc(s_const, 1)
            dve.wait_ge(s_in, 16 * H)
            for h in range(H):
                at = slice(h * B1, (h + 1) * B1)
                o.done(v.tensor_copy(own[at, :], nodes[at, :, h]))
                o.done(v.tensor_copy(to[at, :], nodes[at, :, H + h]))
            o.settle()
            v.tensor_copy(acc[:, :, W1], own[:]).then_inc(s_const, 1)
            dve.wait_ge(s_bin, 1)
            spread_bins = ps_mT[:, 0, 0:G1_N]
            v.tensor_scalar(pick[:], spread_bins[0:G1_BINS], k["number"][0:G1_BINS, :], None, ALU.is_equal).then_inc(s_pick, 1)
            o.done(v.tensor_copy(gap[:], spread_bins))
            o.settle()
            o.done(v.tensor_tensor(same[:, 1:], gap[:, 1:], gap[:, 0:G1_N - 1], ALU.is_equal))
            o.settle()
            o.done(v.tensor_scalar(gap[:], same[:], 1.0, 1e30, ALU.subtract, ALU.mult))
            dve.wait_ge(s_tos, 1)
            o.done(v.tensor_copy(tos[:], ps_A2[:, 0, 0:G1_N]))
            o.done(v.tensor_copy(owns[:], ps_A2[:, 1, 0:G1_N]))
            o.settle()
            o.done(v.tensor_copy(tos3[:, 0], tos[:]))
            o.settle()
            o.done(v.tensor_tensor(left[:], tos[:], tos3[:, 0], ALU.subtract))
            o.settle()
            o.done(v.tensor_copy(tos3[:, 1], left[:]))
            o.settle()
            o.done(v.tensor_tensor(tos3[:, 2], left[:], tos3[:, 1], ALU.subtract))
            o.settle()
            one_hot(0, RING - 1)

            def step(i, j, u):
                over = u is None
                before, two_before = (j - 1) % RING, (j - 2) % RING
                adds = not (known(i) and i < 2)

                def add(q):
                    if adds:
                        add_tile(i - 2, two_before, q)

                if not over:
                    mark(i, j, u)
                if not (known(i) and (i < 1 or i > TURNS)):
                    scores(i - 1, before)
                if not over:
                    one_hot(i + 1, (j + 1) % RING)
                if not (known(i) and (i < 1 or i > TURNS)):
                    weigh(i - 1, before)
                if adds:
                    ready_to_add(i - 2, two_before)
                if not over:
                    raise_tops(i, add)
                else:
                    for q in range(TG):
                        add(q)

            per = RING * (3 + 14)

            def enter(u):
                o.enter(u - 1, per)

            turns(dve, step, range(2), enter, lambda: o.leave(STEPS - 1))
            dve.wait_ge(s_keep, G1_N)
            o.done(v.tensor_tensor(zend[:, 0, :], own[:], to[:], ALU.add))
            o.done(v.tensor_tensor(zend[:, 1, :], acc[:, :, W1], to[:], ALU.add))
            o.settle()
            o.done(v.scalar_tensor_tensor(zend[:], zend[:], 0.2, zend[:], ALU.mult, ALU.max))
            o.settle()
            v.tensor_tensor(own[:], zend[:, 0, :], zend[:, 1, :], ALU.subtract).then_inc(s_end, 1)
            dve.wait_ge(s_own, 16 * H)
            dve.wait_ge(s_oe, 1)
            for part in PARTS:
                own_part, sums = ownrow[:, part, :], acc[:, part, 0:W1]
                w = acc[:, part, HD:W1]
                n = part.stop - part.start
                o.done(v.tensor_tensor(own_part, own_part, spread(own[:, part].unsqueeze(2), P, n, W1), ALU.mult))
                o.settle()
                o.done(v.tensor_tensor(sums, sums, own_part, ALU.add))
                o.settle()
                o.done(v.tensor_scalar(w, w, 1e-16, None, ALU.add))
                o.settle()
                o.done(v.reciprocal(w, w))
                o.settle()
                v.tensor_tensor(acc[:, part, 0:HD], acc[:, part, 0:HD], spread(w, P, n, HD), ALU.mult).then_inc(s_done, 1)

        @block.scalar
        def _(act):
            def keep_hot(i, j):
                act.wait_ge(s_hT, i + 1)
                nc.scalar.activation(hotT[:, j], ps_hT[:], ACT.Copy).then_inc(s_hTk, 1)

            def keep_sums(i, j):
                wait_alone(act, s_acc, i * TG + TG)
                for q in range(TG):
                    block_of = act.value_load(k["bin1"][0:1, bass.ds(i * TG + q, 1)], min_val=0, max_val=G1_BINS - 1)
                    if not (known(i) and i == 0 and q == 0):
                        wait_alone(act, s_keep, i * TG + q)
                    nc.scalar.activation(acc[:, bass.ds(block_of, 1), :].rearrange("p a w -> p (a w)"), state[:, j, q, :],
                                         ACT.Copy).then_inc(s_keep, 1)

            def step(i, j, u):
                if not (known(i) and (i < 1 or i > TURNS)):
                    act.wait_ge(s_sc, i)
                    nc.scalar.activation(ex[:], score[:], ACT.Exp).then_inc(s_ex, 1)
                if not (known(i) and i < 3):
                    keep_sums(i - 3, (j - 3) % RING)
                if u is not None:
                    keep_hot(i + 1, (j + 1) % RING)
                    act.wait_ge(s_spr, i + 1)
                    nc.scalar.activation(scale[:, j, :], drop[:], ACT.Exp).then_inc(s_scale, 1)

            act.wait_ge(s_binT, 1)
            nc.scalar.activation(turned[:], ps_mT[0:G1_BINS, 1, 0:2 * P].rearrange("p (a b) -> p a b", a=2), ACT.Copy).then_inc(s_binTk, 1)
            act.wait_ge(s_const, 2)
            keep_hot(0, RING - 1)
            turns(act, step, range(3))
            act.wait_ge(s_end, 1)
            nc.scalar.activation(own[:], own[:], ACT.Exp).then_inc(s_oe, 1)

        @block.tensor
        def _(pe):
            mm = nc.tensor.matmul

            def turn_hot(i, j):
                wait_alone(pe, s_hot, i + 1)
                if not (known(i) and i == 0):
                    wait_alone(pe, s_hTk, i)
                for q in range(TG):
                    for h in range(H):
                        last = nc.tensor.transpose(ps_hT[h * B1:(h + 1) * B1, q, :], hot[:, j, q, :], identb[:])
                last.then_inc(s_hT, 1)

            def turn_marked(i):
                wait_alone(pe, s_mk, i + 1)
                for q in range(TG):
                    last = nc.tensor.transpose(ps_mT[:, q // HALF, q % HALF * P:(q % HALF + 1) * P], marked[:, q, :], k["ident"][:])
                last.then_inc(s_mT, 1)

            def add_up(i, j):
                wait_alone(pe, s_wt, i + 1)
                for q in range(TG):
                    at = q % HALF * W1
                    for h in range(H):
                        last = mm(sums_of(j)[h * B1:(h + 1) * B1, q // HALF, at:at + W1], weight[:, q, h * B1:(h + 1) * B1],
                                  rows[:, j, q, h * W1:(h + 1) * W1], start=True, stop=True)
                last.then_inc(s_agg, 1)

            def spread_to_edges(i, j):
                wait_alone(pe, s_spr, i + 1)
                wait_alone(pe, s_hTk, i + 1)
                for q in range(TG):
                    last = mm(ps_S[:, 2 * q:2 * q + 2, :].rearrange("p a x -> p (a x)"), hotT[:, j, q, :], spreads[:, q].rearrange("p a c h -> p (a c h)"),
                              start=True, stop=True)
                last.then_inc(s_S, 1)

            def step(i, j, u):
                if u is not None:
                    turn_marked(i)
                    turn_hot(i + 1, (j + 1) % RING)
                if not (known(i) and i < 1):
                    add_up(i - 1, (j - 1) % RING)
                if u is not None:
                    spread_to_edges(i, j)

            pe.wait_ge(s_const, 1)
            mm(ps_mT[:, 0, 0:G1_N], k["one"][0:1, :], bins[:], start=True, stop=True).then_inc(s_bin, 1)
            pe.wait_ge(s_const, 2)
            for n, t in enumerate((to, own)):
                last = nc.tensor.transpose(ps_mT[0:G1_BINS, 1, n * P:(n + 1) * P], t[:], k["ident"][:])
            last.then_inc(s_binT, 1)
            pe.wait_ge(s_binTk, 1)
            pe.wait_ge(s_pick, 1)
            for n in range(2):
                last = mm(ps_A2[:, n, 0:G1_N], turned[:, n, :], pick[:], start=True, stop=True)
            last.then_inc(s_tos, 1)
            turn_hot(0, RING - 1)
            turns(pe, step, range(1))


def stage_ffn1(nc, a, k, out):
    with ExitStack() as ctx:
        m = Memory(nc, ctx, "f")
        F = a["L1_ffn_W1"].shape[2]
        FC = F // P
        FF = TOPK * FC
        CAP = float(-(-NN * 5 // (4 * E1)))
        rows = m.sb("rows", [NP, TN, D])
        st = m.sb("st", [NP, TN, 6])
        mean = m.sb("mean", [NP, TN])
        rstd = m.sb("rstd", [NP, TN])
        tmp = m.sb("tmp", [NP, TN])
        xn = m.sb("xn", [NP, TB, D])
        xT = m.sb("xT", [P, TN, DC, NP])
        sums = m.sb("sums", [P, DC, TN])
        total = m.sb("total", [P, DC])
        wr = m.sb("wr", [P, DC, E1])
        br = m.sb("br", [1, E1])
        logit = m.sb("logit", [1, E1])
        route = m.sb("route", [1, E1])
        pick = m.sb("pick", [1, E1])
        norm = m.sb("norm", [1, 1])
        best = m.sb("best", [1, TOPK])
        which = m.sb("which", [1, TOPK])
        expert = m.sb("expert", [1, TOPK], I32)
        share = m.sb("share", [1, TOPK])
        shares = m.sb("shares", [P, TOPK])
        w1 = m.sb("w1", [P, TOPK, DC, F])
        b1 = m.sb("b1", [P, TOPK, FC])
        w2 = m.sb("w2", [P, TOPK, FC, D])
        b2 = m.sb("b2", [NP, TOPK, D])
        gamma = m.sb("gamma", [NP, D])
        beta = m.sb("beta", [NP, D])
        hT = m.sb("hT", [P, FF, TB, NP])
        stu = m.sb("stu", [NP, TB, 6])
        meanu = m.sb("meanu", [NP, TB])
        rstdu = m.sb("rstdu", [NP, TB])
        tmpu = m.sb("tmpu", [NP, TB])
        ps_T = m.banks("ps_T", 3)
        ps_h = [m.ps(f"ps_h{i}", [P, 3, NP]) for i in range(2)]
        ps_y = [m.ps(f"ps_y{i}", [P, D]) for i in range(2)]
        ps_r = m.ps("ps_r", [P, E1 + TOPK])

        s_att = [m.sem(f"attended{u}") for u in range(NB)]
        s_w = m.sem("weights")
        s_var = m.sem("variance")
        s_std = m.sem("std")
        s_xn = m.sem("normed")
        s_xT = m.sem("xT_made")
        s_xTk = m.sem("xT_kept")
        s_tot = m.sem("total")
        s_log = m.sem("logits")
        s_d = m.sem("differences")
        s_e = m.sem("exponentials")
        s_pick = m.sem("picked")
        s_sh = m.sem("shares_spread")
        s_ew = m.sem("expert_weights")
        s_w2 = m.sem("second_weights_scaled")
        s_h = m.sem("hidden_made")
        s_hk = m.sem("hidden_kept")
        s_y = m.sem("y_made")
        s_yk = m.sem("y_kept")
        s_res = m.sem("result_rows")
        s_out = m.sem("written")
        s_v = m.sem("vector_steps")
        block = ctx.enter_context(nc.Block())

        def row_of(t3, t):
            return t3[:, bass.ds(t, 1), :].rearrange("p a d -> p (a d)")

        @block.sync
        def _(sp):
            attended = k["attended1"][0:NN, :].rearrange("(p t) d -> p t d", p=NP)
            for u in range(NB):
                tiles = slice(u * TB, u * TB + TB)
                sp.dma_start(rows[:, tiles, :], attended[:, tiles, :]).then_inc(s_att[u], 16)
            load_weight(sp, wr[:], a["L1_ffn_Wr"], s_w)
            sp.dma_start(br[:], a["L1_ffn_br"].rearrange("(a e) -> a e", a=1)).then_inc(s_w, 16)
            sp.dma_start(gamma[:], a["L1_ffn_gamma"].partition_broadcast(NP)).then_inc(s_w, 16)
            sp.dma_start(beta[:], a["L1_ffn_beta"].partition_broadcast(NP)).then_inc(s_w, 16)
            sp.wait_ge(s_pick, 1)
            for r in range(TOPK):
                e = sp.value_load(expert[0:1, r:r + 1], min_val=0, max_val=E1 - 1)
                load_weight(sp, w1[:, r], a["L1_ffn_W1"][bass.ds(e, 1)].rearrange("a d f -> (a d) f"), s_ew)
                load_weight(sp, w2[:, r], a["L1_ffn_W2"][bass.ds(e, 1)].rearrange("a f d -> (a f) d"), s_ew)
                for c in range(FC):
                    sp.dma_start(b1[:, r, c:c + 1], a["L1_ffn_b1"][bass.ds(e, 1), c * P:(c + 1) * P].rearrange("a p -> p a")
                                 ).then_inc(s_ew, 16)
                sp.dma_start(b2[:, r, :], a["L1_ffn_b2"][bass.ds(e, 1), :].rearrange("a d -> (a d)").partition_broadcast(NP)
                             ).then_inc(s_ew, 16)
            to = out.rearrange("(p t) d -> p t d", p=NP)
            with sp.Fori(0, NB) as u:
                wait_alone(sp, s_res, u + 1)
                sp.dma_start(to[:, bass.ds(u * TB, TB), :], k["x"][:, bass.ds(u * TB, TB), :]).then_inc(s_out, 16)
            sp.wait_ge(s_out, 16 * NB)

        ALL_EW = 16 * TOPK * (3 + FC)

        @block.scalar
        def _(act):
            def root(n):
                act.wait_ge(s_var, n)
                nc.scalar.activation(rstd[:], rstd[:], ACT.Sqrt, bias=k["eps5"][0:NP, :]).then_inc(s_std, 1)

            root(1)
            with act.Fori(0, NB) as u:
                wait_alone(act, s_xT, u + 1)
                keep_transposed(nc.scalar, s_xTk, xT[:, bass.ds(u * TB, TB)], ps_T)
            for n, row in enumerate((route[:], route[:], share[:, 1:2])):
                act.wait_ge(s_d, n + 1)
                nc.scalar.activation(row, row, ACT.Exp).then_inc(s_e, 1)
            act.wait_ge(s_ew, ALL_EW)

            def turn_root(u):
                wait_alone(act, s_var, u + 2)
                nc.scalar.activation(rstdu[:], rstdu[:], ACT.Sqrt, bias=k["eps5"][0:NP, :]).then_inc(s_std, 1)

            def step(u, first):
                for f in range(FF):
                    for b, n in ((0, 3), (1, 2)):
                        wait_alone(act, s_h, u * 2 * FF + f * 2 + b + 1)
                        nc.scalar.activation(hT[:, f, 3 * b:3 * b + n, :], ps_h[b][:, 0:n, :], ACT.Gelu,
                                             bias=b1[:, f // FC, f % FC:f % FC + 1]).then_inc(s_hk, 1)
                    if f == FF // 2 and not first:
                        turn_root(u - 1)

            step(0, True)
            with act.Fori(1, NB) as u:
                step(u, False)
            turn_root(NB - 1)

        @block.vector
        def _(dve):
            o = Order(dve, s_v)
            v = nc.vector

            def inverse_std(n):
                dve.sem_inc(s_var, 1)
                dve.wait_ge(s_std, n)
                o.done(v.reciprocal(rstd[:], rstd[:]))
                o.settle()

            for u in range(NB):
                tiles = slice(u * TB, u * TB + TB)
                dve.wait_ge(s_att[u], 16)
                o.done(v.tensor_tensor(k["x"][:, tiles, :], k["x"][:, tiles, :], rows[:, tiles, :], ALU.add))
                o.settle()
                for t in range(u * TB, u * TB + TB):
                    o.done(v.bn_stats(st[:, t, :], k["x"][:, t, :]))
            turn_stats(o, st, mean[:], rstd[:], tmp[:])
            inverse_std(1)
            def normed_row(to, t):
                return v.tensor_scalar(to, row_of(k["x"], t), mean[:, bass.ds(t, 1)], rstd[:, bass.ds(t, 1)], ALU.subtract, ALU.mult)

            with dve.Fori(0, NB) as u:
                for j in range(TB):
                    last = normed_row(xn[:, j, :], u * TB + j)
                last.then_inc(s_xn, 1)
                for j in range(TB):
                    normed_row(row_of(rows, u * TB + j), u * TB + j)
                wait_alone(dve, s_xT, u + 1)
            dve.wait_ge(s_xTk, NB)
            o.done(v.tensor_reduce(sums[:], xT[:].rearrange("p t c n -> p c t n"), AX, ALU.add))
            o.settle()
            v.tensor_reduce(total[:], sums[:], AX, ALU.add).then_inc(s_tot, 1)
            dve.wait_ge(s_w, 16 * 4)
            dve.wait_ge(s_log, 1)
            o.done(v.scalar_tensor_tensor(logit[:], ps_r[0:1, 0:E1], 1.0 / NN, br[:], ALU.mult, ALU.add))
            o.settle()

            def softmax(n):
                o.done(v.tensor_reduce(norm[:], logit[:], AX, ALU.max))
                o.settle()
                v.tensor_scalar(route[:], logit[:], norm[:], None, ALU.subtract).then_inc(s_d, 1)
                dve.wait_ge(s_e, n)
                o.done(v.tensor_reduce(norm[:], route[:], AX, ALU.add))
                o.settle()
                o.done(v.reciprocal(norm[:], norm[:]))
                o.settle()
                o.done(v.tensor_scalar(route[:], route[:], norm[:], None, ALU.mult))
                o.settle()

            softmax(1)
            o.done(v.tensor_scalar(pick[:], route[:], float(NN), CAP, ALU.mult, ALU.max))
            o.settle()
            o.done(v.reciprocal(pick[:], pick[:]))
            o.settle()
            o.done(v.scalar_tensor_tensor(logit[:], route[:], CAP, pick[:], ALU.mult, ALU.mult))
            o.settle()
            softmax(2)
            iota = k["iota"][0:1, 0:E1]
            for r in range(TOPK):
                o.done(v.tensor_reduce(best[:, r:r + 1], route[:], AX, ALU.max))
                o.settle()
                o.done(v.tensor_scalar(pick[:], route[:], best[:, r:r + 1], None, ALU.is_equal))
                o.settle()
                o.done(v.scalar_tensor_tensor(pick[:], pick[:], -float(E1), iota, ALU.mult, ALU.add))
                o.settle()
                o.done(v.tensor_reduce(which[:, r:r + 1], pick[:], AX, ALU.min))
                o.settle()
                o.done(v.tensor_scalar(which[:, r:r + 1], which[:, r:r + 1], float(E1), None, ALU.add))
                o.settle()
                if r + 1 < TOPK:
                    o.done(v.tensor_scalar(pick[:], iota, which[:, r:r + 1], None, ALU.is_equal))
                    o.settle()
                    o.done(v.scalar_tensor_tensor(route[:], pick[:], -2.0, route[:], ALU.mult, ALU.add))
                    o.settle()
            v.tensor_copy(expert[:], which[:]).then_inc(s_pick, 1)
            v.tensor_tensor(share[:, 1:2], best[:, 1:2], best[:, 0:1], ALU.subtract).then_inc(s_d, 1)
            dve.wait_ge(s_e, 3)
            o.done(v.tensor_scalar(share[:, 0:1], share[:, 1:2], 1.0, None, ALU.add))
            o.settle()
            o.done(v.reciprocal(share[:, 0:1], share[:, 0:1]))
            o.settle()
            o.done(v.tensor_tensor(share[:, 1:2], share[:, 1:2], share[:, 0:1], ALU.mult))
            o.settle()
            dve.sem_inc(s_tot, 1)
            dve.wait_ge(s_sh, 1)
            o.done(v.tensor_copy(shares[:], ps_r[:, E1:]))
            o.settle()
            dve.wait_ge(s_ew, ALL_EW)
            for r in range(TOPK):
                v.tensor_scalar(w2[:, r], w2[:, r], shares[:, r:r + 1], None, ALU.mult).then_inc(s_w2, 1)
            o.done(v.tensor_scalar(b2[:, 0, :], b2[:, 0, :], shares[0:NP, 0:1], None, ALU.mult))
            o.settle()
            o.done(v.scalar_tensor_tensor(b2[:, 0, :], b2[:, 1, :], shares[0:NP, 1:2], b2[:, 0, :], ALU.mult, ALU.add))
            o.settle()
            o.done(v.tensor_tensor(rows[:], rows[:], spread(b2[:, 0:1, :], NP, TN, D), ALU.add))
            o.settle()
            o.done(v.tensor_tensor(k["x"][:], k["x"][:], spread(beta[:].unsqueeze(1), NP, TN, D), ALU.add))
            o.settle()
            with dve.Fori(0, NB) as u:
                o.enter(u, 1 + 7 + 2)
                for j in range(TB):
                    t = u * TB + j
                    wait_alone(dve, s_y, t + 1)
                    v.tensor_tensor(xn[:, j, :], row_of(rows, t), ps_y[j % 2][0:NP, :], ALU.add).then_inc(s_yk, 1)
                    wait_alone(dve, s_yk, t + 1)
                    last = v.bn_stats(stu[:, j, :], xn[:, j, :])
                o.done(last)
                turn_stats(o, stu, meanu[:], rstdu[:], tmpu[:])
                dve.sem_inc(s_var, 1)
                for j in range(TB):
                    last = v.scalar_tensor_tensor(xn[:, j, :], xn[:, j, :], meanu[:, j:j + 1], gamma[:], ALU.subtract, ALU.mult)
                o.done(last)
                wait_alone(dve, s_std, u + 2)
                o.done(v.reciprocal(rstdu[:], rstdu[:]))
                o.settle()
                for j in range(TB):
                    t = u * TB + j
                    last = v.scalar_tensor_tensor(row_of(k["x"], t), xn[:, j, :], rstdu[:, j:j + 1], row_of(k["x"], t), ALU.mult, ALU.add)
                last.then_inc(s_res, 1)
                wait_alone(dve, s_res, u + 1)
                o.leave(NB)

        @block.tensor
        def _(pe):
            mm = nc.tensor.matmul
            def turn(u, first):
                wait_alone(pe, s_xn, u + 1)
                if not first:
                    wait_alone(pe, s_xTk, u)
                for j, place in enumerate(tile_places(ps_T)):
                    for c in range(DC):
                        last = nc.tensor.transpose(place[:, c, :], xn[:, j, c * P:(c + 1) * P], k["ident"][0:NP, 0:NP])
                last.then_inc(s_xT, 1)

            turn(0, True)
            with pe.Fori(1, NB) as u:
                turn(u, False)
            pe.wait_ge(s_w, 16 * 4)
            pe.wait_ge(s_tot, 1)
            for c in range(DC):
                last = mm(ps_r[0:1, 0:E1], total[:, c:c + 1], wr[:, c, :], start=c == 0, stop=c == DC - 1)
            last.then_inc(s_log, 1)
            pe.wait_ge(s_tot, 2)
            mm(ps_r[:, E1:], k["one"][0:1, :], share[:], start=True, stop=True).then_inc(s_sh, 1)
            pe.wait_ge(s_ew, ALL_EW)
            pe.wait_ge(s_w2, TOPK)

            def first_product(u, f, first):
                for b, n in ((0, 3), (1, 2)):
                    if not (first and f == 0):
                        wait_alone(pe, s_hk, u * 2 * FF + f * 2 + b - 1)
                    for c in range(DC):
                        last = mm(ps_h[b][:, 0:n, :], w1[:, f // FC, c, f % FC * P:(f % FC + 1) * P],
                                  xT[:, bass.ds(u * TB + 3 * b, n), c, :], start=c == 0, stop=c == DC - 1)
                    last.then_inc(s_h, 1)

            def second_product(u, j, first):
                t = u * TB + j
                if not (first and j < 2):
                    wait_alone(pe, s_yk, t - 1 if j else t)
                for f in range(FF):
                    last = mm(ps_y[j % 2][0:NP, :], hT[:, f, j, :], w2[:, f // FC, f % FC, :], start=f == 0, stop=f == FF - 1)
                last.then_inc(s_y, 1)

            def step(u, first):
                for f in range(FF):
                    first_product(u, f, first)
                wait_alone(pe, s_hk, u * 2 * FF + 2 * FF)
                for j in range(TB):
                    second_product(u, j, first)

            step(0, True)
            with pe.Fori(1, NB) as u:
                step(u, False)


def build(nc, a, out):
    with ExitStack() as ctx:
        def keep(name, shape, dt=F32):
            return ctx.enter_context(nc.sbuf_tensor(f"keep_{name}", shape, dt))

        def dram(name, shape):
            return nc.dram_tensor(f"mid_{name}", shape, F32, kind="Internal").ap()

        k = {
            "x": keep("x", [NP, TN, D]),
            "iota": keep("iota", [P, P]),
            "number": keep("number", [P, 1]),
            "ident": keep("ident", [P, P]),
            "before": keep("before", [P, P]),
            "one": keep("one", [P, P]),
            "eps5": keep("eps5", [P, 1]),
            "a_src": keep("a_src", [NP, TN, H]),
            "bin0": keep("bin0", [1, G0_N + 8], I32),
            "record1": keep("record1", [NP, EC, 2]),
            "row1": keep("row1", [NP, EC], I32),
            "bin1": keep("bin1", [1, G1_N], I32),
            "pairs": keep("pairs", [NP, TOPK * TN], I32),
            "gate": keep("gate", [NP, TOPK, TN]),
            "expert_of": keep("expert_of", [1, X_N + 2], I32),
            "b1T": keep("b1T", [P, E0 * F0 // P]),
            "sorted0": dram("sorted0", [P * G0_TILES, 4]),
            "sorted1": dram("sorted1", [P * G1_N, 2]),
            "expert_in": dram("expert_in", [X_N * P, D]),
            "expert_out": dram("expert_out", [X_N * P, D]),
            "table1": dram("table1", [B1 * G1_BINS, ROW1]),
            "score1": dram("score1", [B1 * G1_BINS, 2 * H]),
            "attended1": dram("attended1", [B1 * G1_BINS, D]),
            "table": dram("table", [NN, ROW]),
        }
        stage_project0(nc, a, k)
        with nc.sbuf_tensor("acc0", [NP, TN, ROW], F32) as k["acc0"]:
            k["normed"] = k["acc0"][:, :, 0:D]
            with nc.sbuf_tensor("w1", [P, E0, DC, F0], F32) as k["w1"]:
                stage_edges0(nc, a, k)
                stage_gate(nc, a, k)
                stage_experts(nc, a, k)
            stage_combine(nc, a, k)
            stage_project1(nc, a, k)
        stage_edges1(nc, a, k)
        stage_ffn1(nc, a, k, out)




INPUTS = ['x', 'src', 'dst', 'edge_weight', 'L0_gnn_Ws', 'L0_gnn_bs', 'L0_gnn_aw', 'L0_gnn_ab', 'L0_mix_W_qkv',
          'L0_mix_b_qkv', 'L0_mix_W_out', 'L0_mix_b_out', 'L0_ffn_gate_w', 'L0_ffn_gate_b', 'L0_ffn_w1', 'L0_ffn_b1',
          'L0_ffn_w2', 'L0_ffn_b2', 'L0_ffn_gamma', 'L0_ffn_beta', 'L1_gnn_W', 'L1_gnn_att_src', 'L1_gnn_att_dst',
          'L1_gnn_bias', 'L1_mix_w_norm1', 'L1_mix_w_qkv', 'L1_mix_w_out', 'L1_mix_b_out', 'L1_mix_w_norm2', 'L1_ffn_Wr',
          'L1_ffn_br', 'L1_ffn_W1', 'L1_ffn_b1', 'L1_ffn_W2', 'L1_ffn_b2', 'L1_ffn_gamma', 'L1_ffn_beta']


def kernel(**inputs):
    import concourse.bacc as bacc
    import numpy as np
    from concourse import mybir as _mybir
    from concourse.bass_utils import run_bass_kernel_spmd

    nc = bacc.Bacc("TRN2", target_bir_lowering=False, num_devices=1)
    arrays, a = {}, {}
    for name in INPUTS:
        value = np.ascontiguousarray(inputs[name])
        arrays[f"in_{name}"] = value
        a[name] = nc.dram_tensor(f"in_{name}", value.shape, _mybir.dt.from_np(value.dtype), kind="ExternalInput").ap()
    out = nc.dram_tensor("out", (NN, D), _mybir.dt.from_np(np.dtype("float32")), kind="ExternalOutput").ap()
    build(nc, a, out)
    return run_bass_kernel_spmd(nc, [arrays], core_ids=[0]).results[0]["out"]
```
